# Optimizing a Trainium2 kernel written in Bass

```python
import numpy as np
import jax
import jax.numpy as jnp

def _softmax(x, axis=-1):
    return jax.nn.softmax(x, axis=axis)

def _gelu(x):
    return jax.nn.gelu(x, approximate=True)

def _silu(x):
    return jax.nn.silu(x)

def _sigmoid(x):
    return jax.nn.sigmoid(x)

def _layernorm(x, axis=-1, eps=1e-05):
    m = jnp.mean(x, axis=axis, keepdims=True)
    v = jnp.var(x, axis=axis, keepdims=True)
    return (x - m) / jnp.sqrt(v + eps)

def _scatter_add(tgt, idx, src, axis=0):
    return tgt.at[idx].add(src)

def _segment_sum(src, seg, n):
    return jax.ops.segment_sum(src, seg, n)
kernel_name = 'mk_gps_d1_gnn_r8_17e58e'

def setup_inputs(seed: int=0):
    np.random.seed(seed)
    _w = jnp.asarray

    def _rec_inputs():
        import jax
        import jax.numpy as jnp
        _gk = jax.random.key(seed)
        x = -6.415e-05 + 1 * jax.random.normal(jax.random.fold_in(_gk, 1), (1250, 512), jnp.float32)
        _s = jax.random.randint(jax.random.fold_in(_gk, 2), (10000,), 0, 1250, jnp.int32)
        _d = jax.random.randint(jax.random.fold_in(_gk, 3), (10000,), 0, 1250, jnp.int32)
        _loop = jnp.arange(1250, dtype=jnp.int32)
        src = jnp.concatenate([_s, _d, _loop])
        dst = jnp.concatenate([_d, _s, _loop])
        _o = jnp.argsort(dst, stable=True)
        src = src[_o]
        dst = dst[_o]
        edge_weight = -0.00121341 + 0.998923 * jax.random.normal(jax.random.fold_in(_gk, 12), (21250,), jnp.float32)
        return (x, src, dst, edge_weight)
    x, src, dst, edge_weight = _rec_inputs()

    def _L0_gnn_setup():
        import jax, jax.numpy as jnp
        import numpy as np
        N = 2500
        E = 25000
        D = 512
        H = 512

        def _layernorm(x, gamma, beta, eps=1e-05):
            mu = jnp.mean(x, axis=-1, keepdims=True)
            var = jnp.mean((x - mu) ** 2, axis=-1, keepdims=True)
            return (x - mu) * jax.lax.rsqrt(var + eps) * gamma + beta
        key = jax.random.key(seed)
        ks = jax.random.split(key, 12)
        s = 0.02
        return {'source_features': jax.random.normal(ks[0], (N, D), jnp.float32), 'weighting_gate': jax.random.normal(ks[1], (E,), jnp.float32), 'rel_pair_idx': jax.random.randint(ks[2], (E, 2), 0, N, dtype=jnp.int32), 'Wm': jax.random.normal(ks[3], (D, D // 2), jnp.float32) * s, 'bm': jnp.zeros((D // 2,), jnp.float32), 'W1': jax.random.normal(ks[4], (D, D // 4), jnp.float32) * s, 'b1': jnp.zeros((D // 4,), jnp.float32), 'gamma': jnp.ones((D // 4,), jnp.float32), 'beta': jnp.zeros((D // 4,), jnp.float32), 'W2': jax.random.normal(ks[5], (D // 4, H), jnp.float32) * s, 'b2': jnp.zeros((H,), jnp.float32)}
    _L0_gnn_all = _L0_gnn_setup()
    _L0_gnn_in = {k: v for k, v in _L0_gnn_all.items() if k in ('Wm', 'bm', 'W1', 'b1', 'gamma', 'beta', 'W2', 'b2')}
    del _L0_gnn_all

    def _L0_mix_setup():
        import jax, jax.numpy as jnp
        import numpy as np
        DIM, HEADS, DIM_HEAD = (512, 8, 64)
        key = jax.random.key(seed)
        ks = jax.random.split(key, 9)
        B, T = (4, 512)
        s = 1.0 / np.sqrt(DIM)
        x = jax.random.normal(ks[0], (B, T, DIM), dtype=jnp.float32)
        Wq = jax.random.uniform(ks[1], (DIM, DIM), jnp.float32, -s, s)
        Wk = jax.random.uniform(ks[2], (DIM, DIM), jnp.float32, -s, s)
        Wv = jax.random.uniform(ks[3], (DIM, DIM), jnp.float32, -s, s)
        Wp = jax.random.uniform(ks[4], (DIM, DIM), jnp.float32, -s, s)
        bq = jax.random.uniform(ks[5], (DIM,), jnp.float32, -s, s)
        bk = jax.random.uniform(ks[6], (DIM,), jnp.float32, -s, s)
        bv = jax.random.uniform(ks[7], (DIM,), jnp.float32, -s, s)
        bp = jax.random.uniform(ks[8], (DIM,), jnp.float32, -s, s)
        return {'x': x, 'Wq': Wq, 'bq': bq, 'Wk': Wk, 'bk': bk, 'Wv': Wv, 'bv': bv, 'Wp': Wp, 'bp': bp}
    _L0_mix_all = _L0_mix_setup()
    _L0_mix_in = {k: v for k, v in _L0_mix_all.items() if k in ('Wq', 'bq', 'Wk', 'bk', 'Wv', 'bv', 'Wp', 'bp')}
    del _L0_mix_all

    def _L0_ffn_setup():
        import jax, jax.numpy as jnp
        import numpy as np
        B, S, D, F, E = (4, 256, 512, 256, 8)
        key = jax.random.key(seed)
        k = jax.random.split(key, 5)
        x = jax.random.normal(k[0], (B, S, D), dtype=jnp.float32)
        Ws = jax.random.normal(k[1], (D, E), dtype=jnp.float32) * 0.02
        bs = jnp.zeros((E,), dtype=jnp.float32)
        W1 = jax.random.normal(k[2], (E, D, F), dtype=jnp.float32) * 0.02
        b1 = jnp.zeros((E, F), dtype=jnp.float32)
        W2 = jax.random.normal(k[3], (E, F, D), dtype=jnp.float32) * 0.02
        b2 = jnp.zeros((E, D), dtype=jnp.float32)
        return {'x': x, 'Ws': Ws, 'bs': bs, 'W1': W1, 'b1': b1, 'W2': W2, 'b2': b2}
    _L0_ffn_all = _L0_ffn_setup()
    _L0_ffn_in = {k: v for k, v in _L0_ffn_all.items() if k in ('Ws', 'bs', 'W1', 'b1', 'W2', 'b2')}
    del _L0_ffn_all
    return {'x': x, 'src': src, 'dst': dst, 'edge_weight': edge_weight, 'L0_gnn_Wm': _L0_gnn_in['Wm'], 'L0_gnn_bm': _L0_gnn_in['bm'], 'L0_gnn_W1': _L0_gnn_in['W1'], 'L0_gnn_b1': _L0_gnn_in['b1'], 'L0_gnn_gamma': _L0_gnn_in['gamma'], 'L0_gnn_beta': _L0_gnn_in['beta'], 'L0_gnn_W2': _L0_gnn_in['W2'], 'L0_gnn_b2': _L0_gnn_in['b2'], 'L0_mix_Wq': _L0_mix_in['Wq'], 'L0_mix_bq': _L0_mix_in['bq'], 'L0_mix_Wk': _L0_mix_in['Wk'], 'L0_mix_bk': _L0_mix_in['bk'], 'L0_mix_Wv': _L0_mix_in['Wv'], 'L0_mix_bv': _L0_mix_in['bv'], 'L0_mix_Wp': _L0_mix_in['Wp'], 'L0_mix_bp': _L0_mix_in['bp'], 'L0_ffn_Ws': _L0_ffn_in['Ws'], 'L0_ffn_bs': _L0_ffn_in['bs'], 'L0_ffn_W1': _L0_ffn_in['W1'], 'L0_ffn_b1': _L0_ffn_in['b1'], 'L0_ffn_W2': _L0_ffn_in['W2'], 'L0_ffn_b2': _L0_ffn_in['b2']}

def reference(x, src, dst, edge_weight, L0_gnn_Wm, L0_gnn_bm, L0_gnn_W1, L0_gnn_b1, L0_gnn_gamma, L0_gnn_beta, L0_gnn_W2, L0_gnn_b2, L0_mix_Wq, L0_mix_bq, L0_mix_Wk, L0_mix_bk, L0_mix_Wv, L0_mix_bv, L0_mix_Wp, L0_mix_bp, L0_ffn_Ws, L0_ffn_bs, L0_ffn_W1, L0_ffn_b1, L0_ffn_W2, L0_ffn_b2):
    import jax
    import jax.numpy as jnp

    def _L0_gnn_ref(source_features, weighting_gate, rel_pair_idx, Wm, bm, W1, b1, gamma, beta, W2, b2):
        import jax, jax.numpy as jnp
        import numpy as np
        N = 2500
        E = 25000
        D = 512
        H = 512

        def _layernorm(x, gamma, beta, eps=1e-05):
            mu = jnp.mean(x, axis=-1, keepdims=True)
            var = jnp.mean((x - mu) ** 2, axis=-1, keepdims=True)
            return (x - mu) * jax.lax.rsqrt(var + eps) * gamma + beta
        src = rel_pair_idx[:, 0]
        dst = rel_pair_idx[:, 1]
        n_nodes = source_features.shape[0]
        m = jnp.maximum(jnp.max(weighting_gate), jnp.float32(0.0))
        exp_e = jnp.exp(weighting_gate - m)
        row_sum = jax.ops.segment_sum(exp_e, src, num_segments=n_nodes)
        atten_e = exp_e / (row_sum[src] + 1e-06)
        Mfeat = source_features @ Wm + bm
        out0 = jax.ops.segment_sum(atten_e[:, None] * Mfeat[dst], src, num_segments=n_nodes)
        out1 = jax.ops.segment_sum(atten_e[:, None] * Mfeat[src], dst, num_segments=n_nodes)
        message_feats = jnp.concatenate([out0, out1], axis=-1)
        h = message_feats @ W1 + b1
        h = jax.nn.relu(_layernorm(h, gamma, beta))
        h = jax.nn.relu(h @ W2 + b2)
        valid = (row_sum > 0)[:, None]
        return jnp.where(valid, h, jnp.float32(0.0))

    def _L0_mix_ref(x, Wq, bq, Wk, bk, Wv, bv, Wp, bp):
        import jax, jax.numpy as jnp
        import numpy as np
        DIM, HEADS, DIM_HEAD = (512, 8, 64)
        B, T, _ = x.shape
        H, D = (HEADS, DIM_HEAD)

        def proj(W, b):
            return (x @ W.T + b).reshape(B, T, H, D).transpose(0, 2, 1, 3)
        q = jax.nn.softmax(proj(Wq, bq), axis=-1)
        k = jax.nn.softmax(proj(Wk, bk), axis=-1)
        v = proj(Wv, bv)
        k_sum = k.sum(axis=2, keepdims=True)
        D_inv = 1.0 / (q * k_sum).sum(axis=-1, keepdims=True)
        context = jnp.einsum('bhtd,bhte->bhde', k, v)
        out = jnp.einsum('bhtd,bhde->bhte', q, context) * D_inv + q
        out = out.transpose(0, 2, 1, 3).reshape(B, T, H * D)
        return out @ Wp.T + bp

    def _L0_ffn_ref(x, Ws, bs, W1, b1, W2, b2):
        import jax, jax.numpy as jnp
        import numpy as np
        B, S, D, F, E = (4, 256, 512, 256, 8)
        Bb, Ss, Dd = x.shape
        xt = x.reshape(-1, Dd)
        logits = xt @ Ws + bs
        probs = jax.nn.softmax(logits, axis=-1)
        prob_max = jnp.max(probs, axis=-1)
        routes = jnp.argmax(probs, axis=-1)
        onehot = jax.nn.one_hot(routes, W1.shape[0], dtype=xt.dtype)

        def expert_ffn(w1, bb1, w2, bb2):
            h = jax.nn.gelu(xt @ w1 + bb1, approximate=False)
            return h @ w2 + bb2
        y = jax.vmap(expert_ffn)(W1, b1, W2, b2)
        out = jnp.einsum('te,etd->td', onehot, y)
        out = out * prob_max[:, None]
        return out.reshape(Bb, Ss, Dd)
    edge_index_t = jnp.stack([src, dst], axis=1)
    xn = _layernorm(x, axis=-1)
    x = x + _L0_gnn_ref(xn, edge_weight, edge_index_t, L0_gnn_Wm, L0_gnn_bm, L0_gnn_W1, L0_gnn_b1, L0_gnn_gamma, L0_gnn_beta, L0_gnn_W2, L0_gnn_b2) + _L0_mix_ref(xn[None], L0_mix_Wq, L0_mix_bq, L0_mix_Wk, L0_mix_bk, L0_mix_Wv, L0_mix_bv, L0_mix_Wp, L0_mix_bp)[0]
    x = x + _L0_ffn_ref(_layernorm(x, axis=-1)[None], L0_ffn_Ws, L0_ffn_bs, L0_ffn_W1, L0_ffn_b1, L0_ffn_W2, L0_ffn_b2)[0]
    return x

_drawn_inputs = setup_inputs


def setup_inputs(seed=0):
    import zlib

    import numpy as np

    out = dict(_drawn_inputs(seed))
    spreads = {'L0_gnn_bm': (0.0, 0.1),
     'L0_gnn_b1': (0.0, 0.1),
     'L0_gnn_gamma': (1.0, 0.6),
     'L0_gnn_beta': (0.0, 0.689),
     'L0_gnn_b2': (0.0, 0.1),
     'L0_ffn_bs': (0.0, 0.596),
     'L0_ffn_b1': (0.0, 0.8),
     'L0_ffn_b2': (0.0, 0.349)}
    factors = {'L0_mix_Wq': 4.397,
     'L0_mix_bq': 8.0,
     'L0_mix_Wk': 8.0,
     'L0_mix_bk': 8.0,
     'L0_mix_Wv': 6.047,
     'L0_mix_bv': 3.788,
     'L0_ffn_W1': 3.132,
     'L0_ffn_W2': 2.941}
    for name, (base, spread) in spreads.items():
        noise = np.random.default_rng([zlib.crc32(name.encode()), seed]).standard_normal(out[name].shape)
        drawn = base * np.exp(spread * noise) if base else spread * noise
        out[name] = jnp.asarray(drawn.astype(out[name].dtype))
    for name, factor in factors.items():
        out[name] = (out[name] * factor).astype(out[name].dtype)
    return out
```

```python
from contextlib import ExitStack

import numpy as np
import concourse.bass as bass
import concourse.mybir as mybir

F32 = mybir.dt.float32
I32 = mybir.dt.int32
ALU = mybir.AluOpType
ACT = mybir.ActivationFunctionType
X = mybir.AxisListType.X

N, D, NE = 1250, 512, 21250
TP, NT = 125, 10
KD = D // 128
H, DH = 8, 64
MD, GH = D // 2, D // 4
E, F = 8, 256
KF = F // 128
EC = NE // TP
GC = 4
NG = (EC + GC - 1) // GC
NTAB = 3
TABW = 12288
SPARE = N * N
CH = 128
NC = (N + E * (CH - 1)) // CH
REC = D + 4
R_P, R_ID, R_RS, R_NM = D, D + 1, D + 2, D + 3
PADID = 2000
LN_EPS = 1e-5
SPANS = [(0, 500), (500, 1000), (1000, 1250)]

CONSTS, CW = {}, 0
for _n, _w in (("ident", 128), ("ones", 128), ("before", TP), ("rank", 1), ("rank2", 1), ("spare", 1),
               ("tag", NT), ("prefer", NT * E), ("chunk", NC * E), ("eps", 1)):
    CONSTS[_n] = (CW, _w)
    CW += _w
BIAS, BW = {}, 0
for _n, _w in (("q", D), ("k", D), ("v", D), ("m", MD), ("p", D), ("g1", GH), ("g2", D), ("s", E)):
    BIAS[_n] = (BW, _w)
    BW += _w
SMALL, SW = {}, 0
for _n, _w in (("gamma", 1), ("beta", 1), ("b1", KF * E), ("ws", KD * E), ("w1g", KD * GH), ("w2g", D)):
    SMALL[_n] = (SW, _w)
    SW += _w

LOTS = [(0, 2), (2, 10), (10, 26), (26, NG)]


def table_turns():
    out = [0] * 6 + [0, 1] * 6
    while len(out) < EC:
        out.append(len(out) % NTAB)
    return out


def build(nc, x, edge_src, edge_dst, edge_w, consts, biases, small, wqkvm, wp, w1f, w2f, b2f, out):
    turns = table_turns()
    with ExitStack() as ctx:
        def sb(name, shape, dt=F32):
            return ctx.enter_context(nc.sbuf_tensor(name, shape, dt))

        def sem(name):
            return ctx.enter_context(nc.semaphore(name))

        tables = [nc.dram_tensor(f"edge_table{k}", [128 * TABW, 1], F32).ap() for k in range(NTAB)]
        sorted_rec = nc.dram_tensor("sorted_rec", [NC * CH, REC], F32).ap()

        cst = sb("cst", [128, CW])
        bia = sb("bia", [128, BW])
        sml = sb("sml", [128, SW])
        rec = sb("rec", [TP, NT, REC])
        msg = sb("msg", [TP, NT, MD])
        w1_sb = sb("w1_sb", [128, KD, E * F])
        area1 = sb("area1", [128, 8192])
        area2 = sb("area2", [128, 5000])
        area3 = sb("area3", [128, 5000])
        area4 = sb("area4", [128, 4096])
        area5 = sb("area5", [128, 5000])
        xn = sb("xn", [TP, 2, D])

        def const(name):
            a, w = CONSTS[name]
            return cst[:, a:a + w]

        def bias(name):
            a, w = BIAS[name]
            return bia[0:TP, a:a + w]

        def little(name):
            a, w = SMALL[name]
            return sml[:, a:a + w]

        ident, ones = const("ident"), const("ones")
        w_sb = area1[:, 0:7168].rearrange("p (k n) -> p k n", k=KD)
        v_sb = area1[0:TP, 7168:8192].rearrange("p (r n) -> p r n", r=2)
        w2_sb = area1[:, :].rearrange("p (f n) -> p f n", f=KF)
        xT = area2[:, :].rearrange("p (k n) -> p k n", k=KD)
        aoT = xT
        qT = area3[:, :].rearrange("p (k n) -> p k n", k=KD)
        wp_sb = area4[:, 0:2048].rearrange("p (k n) -> p k n", k=KD)
        qk = area4[0:TP, 2048:4096].rearrange("p (r a n) -> p r a n", r=2, a=2)
        rows = [a[0:TP, 0:NTAB * N].rearrange("p (k n) -> p k n", k=NTAB) for a in (area3, area2, area4)]
        adjT = [a[0:TP, 3750:5000].rearrange("p (j n) -> p j n", j=NT) for a in (area2, area3)]
        b2_sb = area4
        msgT = area5[:, :].rearrange("p (k n) -> p k n", k=KD)
        x2T = msgT
        src_i = area5[0:TP, 0:EC].bitcast(I32)
        dst_i = area5[0:TP, EC:2 * EC].bitcast(I32)
        wraw = area5[0:TP, 2 * EC:3 * EC]
        cell = area5[0:TP, 3 * EC:4 * EC]
        away = area5[0:TP, 4 * EC:5 * EC]
        again = area5[0:TP, 5 * EC:6 * EC]
        cell_i = area5[0:TP, 6 * EC:7 * EC].bitcast(I32)
        wsum = area5[0:TP, 7 * EC:8 * EC]
        wu = area5[0:TP, 8 * EC:10 * EC].rearrange("p (c a) -> p c a", a=2)
        zeros = area5[:, 1700:2724]
        same = area5[0:TP, 2724:3724].rearrange("p (r c q) -> p r c q", r=2, c=GC)
        hid = area2[0:TP, 0:NT * GH].rearrange("p (t n) -> p t n", t=NT)
        hidT = area2[:, 1280:1280 + 2 * TP].rearrange("p (r n) -> p r n", r=2)
        upd = area2[0:TP, 1536:2560].rearrange("p (r n) -> p r n", r=2)
        rec_c = area3[:, 0:3 * REC].rearrange("p (r n) -> p r n", r=3)
        xs = area3[:, 1548:2572].rearrange("p (r n) -> p r n", r=2)
        xsT = area3[:, 2572:3596].rearrange("p (r k n) -> p r k n", r=2, k=KD)
        h_sb = area3[:, 3596:4108].rearrange("p (r n) -> p r n", r=2)
        hT = area3[:, 4108:4620].rearrange("p (r f n) -> p r f n", r=2, f=KF)
        y_sb = area2[:, 2560:3584].rearrange("p (r n) -> p r n", r=2)
        o_sb = area2[:, 3584:4608].rearrange("p (r n) -> p r n", r=2)

        top = sb("top", [TP, 4])
        stat = sb("stat", [TP, NT, 6])
        mv = sb("mv", [TP, NT, 2])
        std = sb("std", [TP, NT])
        rstd = sb("rstd", [TP, NT])
        nmr = sb("nmr", [TP, NT])
        hmax = sb("hmax", [TP, 2 * H])
        hsum = sb("hsum", [TP, 2 * H])
        hrec = sb("hrec", [TP, 2 * H])
        ctxd = sb("ctxd", [128, 4, 128])
        ksumd = sb("ksumd", [128, 4, 128])
        rden = sb("rden", [128, 2, 500])
        rs = sb("rs", [TP, NT])
        rse = sb("rse", [TP, NT])
        rinv = sb("rinv", [TP, NT])
        valid = sb("valid", [TP, NT])
        logit = sb("logit", [TP, NT, E])
        eq = sb("eq", [TP, NT, E])
        oh = sb("oh", [TP, NT, E])
        best = sb("best", [TP, NT])
        lmax = sb("lmax", [TP, NT])
        psm = sb("psm", [TP, NT])
        cnt_i = sb("cnt_i", [TP, 2, E], I32)
        cnt = sb("cnt", [TP, 4, E])
        pos_i = sb("pos_i", [TP, NT], I32)
        own = sb("own", [1, NC, E])
        ownf = sb("ownf", [1, NC])
        own_i = sb("own_i", [1, NC], I32)
        out_i = sb("out_i", [128, NC], I32)

        bank = [ctx.enter_context(nc.psum_tensor(f"bank{i}", [128, 512], F32)) for i in range(8)]

        ld_const, ld_edge, ld_bias, ld_small = sem("ld_const"), sem("ld_edge"), sem("ld_bias"), sem("ld_small")
        ld_x = [sem("ld_x0"), sem("ld_x1")]
        ld_w, ld_wp, ld_w1, ld_w2, ld_b2 = sem("ld_w"), sem("ld_wp"), sem("ld_w1"), sem("ld_w2"), sem("ld_b2")
        tab_zero = [sem(f"tab_zero{k}") for k in range(NTAB)]
        rec_zero = sem("rec_zero")
        ld_rows = [sem(f"ld_rows{r}") for r in range(3)]
        ld_rec = [sem(f"ld_rec{r}") for r in range(3)]
        tab_add = [sem(f"tab_add{k}") for k in range(NTAB)]
        rec_out = sem("rec_out")
        out_st = [sem("out_st0"), sem("out_st1")]
        zeros_set, top_col, top_row, top_val, top_bc, top_sb, w_exp = (
            sem("zeros_set"), sem("top_col"), sem("top_row"), sem("top_val"), sem("top_bc"), sem("top_sb"), sem("w_exp"))
        cell_ok, cell_ps, same_ok, tot_ps, lot_ok = (
            sem("cell_ok"), sem("cell_ps"), sem("same_ok"), sem("tot_ps"), sem("lot_ok"))
        var_ok, std_ok, xn_ok, xT_ps, xT_ok = sem("var_ok"), sem("std_ok"), sem("xn_ok"), sem("xT_ps"), sem("xT_ok")
        q_ps, k_ps, v_ps, m_ps = sem("q_ps"), sem("k_ps"), sem("v_ps"), sem("m_ps")
        q_sb, k_sb, v_ok, m_ok = sem("q_sb"), sem("k_sb"), sem("v_ok"), sem("m_ok")
        shifted, exp_ok, soft_ok, qT_ps, qT_ok, ctx_ps, ctx_ok = (
            sem("shifted"), sem("exp_ok"), sem("soft_ok"), sem("qT_ps"), sem("qT_ok"), sem("ctx_ps"), sem("ctx_ok"))
        num_ps, den_ps, ao_ok, mix_ps, mix_ok = sem("num_ps"), sem("den_ps"), sem("ao_ok"), sem("mix_ps"), sem("mix_ok")
        add1_ok, adj_sum, rinv_ok, adj_ok, adjT_ps, adjT_ok = (
            sem("add1_ok"), sem("adj_sum"), sem("rinv_ok"), sem("adj_ok"), sem("adjT_ps"), sem("adjT_ok"))
        out0_ps, out0_ok, out1_ps, out1_ok = (
            sem("out0_ps"), sem("out0_ok"), sem("out1_ps"), sem("out1_ok"))
        hid_ps, hid_ok, hvar_ok, hstd_ok, hn_ok, hT_ps, hidT_ok, upd_ps, upd_ok, relu_ok, x1_ok = (
            sem("hid_ps"), sem("hid_ok"), sem("hvar_ok"), sem("hstd_ok"), sem("hn_ok"), sem("hT_ps"), sem("hidT_ok"),
            sem("upd_ps"), sem("upd_ok"), sem("relu_ok"), sem("x1_ok"))
        var2_ok, std2_ok, nmr2_ok, x2_ok, x2T_ps, x2T_ok, log_ps, log_ok, lexp_ok, oh_ok, rank_ps = (
            sem("var2_ok"), sem("std2_ok"), sem("nmr2_ok"), sem("x2_ok"), sem("x2T_ps"),
            [sem("x2T_even"), sem("x2T_odd")], sem("log_ps"),
            sem("log_ok"), sem("lexp_ok"), sem("oh_ok"), sem("rank_ps"))
        pos_ok, own_ok = sem("pos_ok"), sem("own_ok")
        xs_ok, xsT_ps, xsT_ok, h_ps, h_ok, hc_ps, gelu_ok, y_ps, y_ok, o_ok, oi_ok = (
            sem("xs_ok"), sem("xsT_ps"), sem("xsT_ok"), sem("h_ps"), sem("h_ok"), sem("hc_ps"), sem("gelu_ok"),
            sem("y_ps"), sem("y_ok"), sem("o_ok"), sem("oi_ok"))
        v_step = sem("v_step")

        lot_of = [next(i for i, (a, b) in enumerate(LOTS) if a <= c // GC < b) for c in range(EC)]

        def split(eng, dst, srcs, s):
            for a, b in ((0, 112), (112, TP)):
                eng.dma_start(dst(a, b), srcs(a, b)).then_inc(s, 16)

        block = ctx.enter_context(nc.Block())

        @block.sync
        def _(sp):
            def edges(v):
                return v.rearrange("(p c) -> p c", p=TP)

            split(sp, lambda a, b: src_i[a:b], lambda a, b: edges(edge_src)[a:b], ld_edge)
            split(sp, lambda a, b: dst_i[a:b], lambda a, b: edges(edge_dst)[a:b], ld_edge)
            split(sp, lambda a, b: wraw[a:b], lambda a, b: edges(edge_w)[a:b], ld_edge)
            sp.dma_start(cst[:, :], consts).then_inc(ld_const, 16)
            xv = x.rearrange("(t p) d -> p t d", p=TP)
            for h in range(2):
                t0 = 5 * h
                split(sp, lambda a, b: rec[a:b, t0:t0 + 5, 0:D], lambda a, b: xv[a:b, t0:t0 + 5, :], ld_x[h])
            sp.wait_ge(zeros_set, 1)

            def zero(dram, width, s):
                sp.dma_start(dram, zeros[:, 0:width].unsqueeze(1).to_broadcast([128, 12, width])).then_inc(s, 16)

            tab_v = [tb.rearrange("(p a n) b -> p a (n b)", p=128, a=12) for tb in tables]
            zero(tab_v[0], 1024, tab_zero[0])
            sp.dma_start(w_sb, wqkvm).then_inc(ld_w, 16)
            sp.dma_start(bia[:, :], biases.partition_broadcast(128)).then_inc(ld_bias, 16)
            zero(tab_v[1], 1024, tab_zero[1])
            zero(tab_v[2], 1024, tab_zero[2])
            sp.dma_start(wp_sb, wp).then_inc(ld_wp, 16)
            sp.dma_start(sml[:, :], small).then_inc(ld_small, 16)
            flat = sorted_rec.rearrange("(p b) n -> p (b n)", p=128)
            zero(flat.rearrange("p (a n) -> p a n", a=12), NC * REC // 12, rec_zero)
            sp.dma_start(w1_sb[:, :, :], w1f).then_inc(ld_w1, 16)
            sp.wait_ge(ctx_ps, NT)
            sp.dma_start(w2_sb, w2f).then_inc(ld_w2, 16)
            for k in range(NTAB):
                sp.wait_ge(tab_add[k], 16 * turns.count(k))
            views = [tb[0:N * N, :].rearrange("(t p n) b -> p t (n b)", p=TP, t=NT) for tb in tables]
            for t in range(NT):
                r = t % 3
                if t == 0:
                    sp.wait_ge(ao_ok, 12)
                if t == 1:
                    sp.wait_ge(mix_ps, NT)
                if t >= 3:
                    sp.wait_ge(out1_ps, t - 2)
                for k in range(NTAB):
                    split(sp, lambda a, b: rows[r][a:b, k, :], lambda a, b: views[k][a:b, t, :], ld_rows[r])
            sp.wait_ge(out1_ps, NT - 1)
            sp.dma_start(b2_sb[:, :], b2f.partition_broadcast(128)).then_inc(ld_b2, 16)
            sp.wait_ge(rec_out, 16 * NT)
            for c in range(NC):
                if c >= 3:
                    sp.wait_ge(o_ok, c - 2)
                sp.dma_start(rec_c[:, c % 3, :], sorted_rec[c * CH:(c + 1) * CH, :]).then_inc(ld_rec[c % 3], 16)

        @block.gpsimd
        def _(pool):
            pool.memset(zeros, 0.0).then_inc(zeros_set, 1)
            used = [0] * NTAB
            for c, k in enumerate(turns):
                if c == 0 or lot_of[c] != lot_of[c - 1]:
                    pool.wait_ge(lot_ok, lot_of[c] + 1)
                if used[k] == 0:
                    pool.wait_ge(tab_zero[k], 16)
                else:
                    pool.wait_ge(tab_add[k], 16 * used[k])
                pool.indirect_dma_start(tables[k], bass.IndirectOffsetOnAxis(ap=cell_i[:, c:c + 1], axis=0),
                                        wsum[:, c:c + 1], None, compute_op=ALU.add).then_inc(tab_add[k], 16)
                used[k] += 1
            for t in range(NT):
                pool.wait_ge(ld_rows[t % 3], 96 * (t // 3 + 1))
                pool.tensor_tensor(rows[t % 3][:, 0, :], rows[t % 3][:, 0, :], rows[t % 3][:, 1, :],
                                   ALU.add).then_inc(add1_ok, 1)
            pool.wait_ge(rec_zero, 16)
            pool.wait_ge(pos_ok, 1)
            for t in range(NT):
                pool.indirect_dma_start(sorted_rec, bass.IndirectOffsetOnAxis(ap=pos_i[:, t:t + 1], axis=0),
                                        rec[:, t, :], None).then_inc(rec_out, 16)
            for c in range(NC):
                pool.wait_ge(o_ok, c + 1)
                pool.indirect_dma_start(out, bass.IndirectOffsetOnAxis(ap=out_i[:, c:c + 1], axis=0),
                                        o_sb[:, c % 2, :], None, bounds_check=N - 1,
                                        oob_is_err=False).then_inc(out_st[c % 2], 16)
            pool.wait_ge(out_st[0], 16 * ((NC + 1) // 2))
            pool.wait_ge(out_st[1], 16 * (NC // 2))

        @block.tensor
        def _(pe):
            pe.wait_ge(ld_const, 16)
            pe.wait_ge(top_col, 1)
            pe.transpose(bank[3][0:1, 0:TP], top[:, 0:1], ident[0:TP, 0:TP]).then_inc(top_row, 1)
            pe.wait_ge(top_val, 1)
            pe.matmul(bank[4][0:TP, 0:1], ones[0:1, 0:TP], top[0:1, 2:3], start=True, stop=True).then_inc(top_bc, 1)
            pe.wait_ge(cell_ok, 1)

            def spread(g):
                if g >= 2:
                    pe.wait_ge(same_ok, g - 1)
                n = min(GC, EC - g * GC)
                for i in range(n):
                    c = g * GC + i
                    mm = pe.transpose(bank[g % 2][0:TP, i * TP:(i + 1) * TP],
                                      cell[:, c:c + 1].to_broadcast([TP, TP]), ident[0:TP, 0:TP])
                mm.then_inc(cell_ps, 1)

            def totals(g):
                if g == 0:
                    pe.wait_ge(w_exp, 1)
                pe.wait_ge(same_ok, g + 1)
                n = min(GC, EC - g * GC)
                for i in range(n):
                    c = g * GC + i
                    mm = pe.matmul(bank[2][0:TP, 2 * c:2 * c + 2], same[:, g % 2, i, :], wu[:, c, :],
                                   start=True, stop=True)
                mm.then_inc(tot_ps, 1)

            spread(0)
            for g in range(NG):
                if g + 1 < NG:
                    spread(g + 1)
                totals(g)

            def x_turn(t):
                pe.wait_ge(xn_ok, t + 1)
                if t == 0:
                    pe.wait_ge(same_ok, NG)
                else:
                    pe.wait_ge(xT_ok, t)
                for k in range(KD):
                    mm = pe.transpose(bank[0][:, k * TP:(k + 1) * TP], xn[:, t % 2, k * 128:(k + 1) * 128],
                                      ident[0:TP, 0:TP])
                mm.then_inc(xT_ps, 1)

            def project(t):
                pe.wait_ge(xT_ok, t + 1)
                if t == 0:
                    pe.wait_ge(ld_w, 16)
                    pe.wait_ge(top_sb, 1)
                for b, a, n, free, done in ((3, 0, D, q_sb, q_ps), (4, D, D, k_sb, k_ps),
                                            (5, 2 * D, D, v_ok, v_ps), (6, 3 * D, MD, m_ok, m_ps)):
                    if t >= 1:
                        pe.wait_ge(free, t)
                    for k in range(KD):
                        mm = pe.matmul(bank[b][0:TP, 0:n], xT[:, k, t * TP:(t + 1) * TP], w_sb[:, k, a:a + n],
                                       start=(k == 0), stop=(k == KD - 1))
                    mm.then_inc(done, 1)

            def context(t):
                r = t % 2
                pe.wait_ge(soft_ok, t + 1)
                if t >= 1:
                    pe.wait_ge(qT_ok, t)
                for k in range(KD):
                    mm = pe.transpose(bank[1][:, k * TP:(k + 1) * TP], qk[:, r, 0, k * 128:(k + 1) * 128],
                                      ident[0:TP, 0:TP])
                mm.then_inc(qT_ps, 1)
                if t == 0:
                    pe.wait_ge(lot_ok, len(LOTS))
                for k in range(KD):
                    kk = qk[:, r, 1, k * 128:(k + 1) * 128]
                    first, last = t == 0 and k == 0, t == NT - 1
                    pe.matmul(bank[7][:, k * 128:(k + 1) * 128], kk, v_sb[:, r, k * 128:(k + 1) * 128],
                              start=first, stop=last, skip_group_check=True)
                    mm = pe.matmul(bank[2][:, k:k + 1], kk, ones[0:TP, 0:1], start=first, stop=last,
                                   skip_group_check=True)
                mm.then_inc(ctx_ps, 1)

            x_turn(0)
            for t in range(NT):
                if t + 1 < NT:
                    x_turn(t + 1)
                project(t)
                if t >= 1:
                    context(t - 1)
            context(NT - 1)

            pe.wait_ge(ctx_ok, 1)
            pe.wait_ge(qT_ok, NT)
            pe.wait_ge(ld_wp, 16)

            def attend(step):
                s, k = divmod(step, 4)
                a, b = SPANS[s]
                if step < 2:
                    pe.wait_ge(m_ok, NT)
                else:
                    pe.wait_ge(ao_ok, step - 1)
                pe.matmul(bank[5 + step % 2][:, 0:b - a], ksumd[:, k, :], qT[:, k, a:b],
                          start=True, stop=True).then_inc(den_ps, 1)
                pe.matmul(bank[3 + step % 2][:, 0:b - a], ctxd[:, k, :], qT[:, k, a:b],
                          start=True, stop=True).then_inc(num_ps, 1)

            def mix_out(t):
                pe.wait_ge(ao_ok, 4 * (t // 4 + 1))
                if t >= 2:
                    pe.wait_ge(mix_ok, t - 1)
                for k in range(KD):
                    mm = pe.matmul(bank[t % 2][0:TP, :], aoT[:, k, t * TP:(t + 1) * TP], wp_sb[:, k, :],
                                   start=(k == 0), stop=(k == KD - 1))
                mm.then_inc(mix_ps, 1)

            for step in range(12):
                attend(step)
                if step >= 5:
                    tt = step - 5
                    if step < 9:
                        mix_out(tt)
            for t in range(4, NT):
                mix_out(t)

            def adj_turn(t, part):
                n = 3 * t + part
                if n >= 2:
                    pe.wait_ge(adjT_ok, n - 1)
                else:
                    pe.wait_ge(mix_ok, NT)
                lo, hi = (0, 4, 8)[part], (4, 8, 10)[part]
                for j in range(lo, hi):
                    mm = pe.transpose(bank[n % 2][0:TP, (j - lo) * TP:(j - lo + 1) * TP],
                                      rows[t % 3][:, 0, j * TP:(j + 1) * TP], ident[0:TP, 0:TP])
                mm.then_inc(adjT_ps, 1)

            def into(t, m):
                for i, (a, b) in enumerate(SPANS):
                    if i < 2:
                        dst = bank[3 + 2 * m + i][:, 0:500]
                    else:
                        dst = bank[7][:, 250 * m:250 * m + 250]
                    mm = pe.matmul(dst, msg[:, t, m * 128:(m + 1) * 128], rows[t % 3][:, 0, a:b],
                                   start=(t == 0 and not (i == 2 and m == 1)), stop=(t == NT - 1),
                                   skip_group_check=True)
                if m == 1:
                    mm.then_inc(out1_ps, 1)

            for t in range(NT):
                pe.wait_ge(adj_ok, t + 1)
                adj_turn(t, 0)
                adj_turn(t, 1)
                into(t, 0)
                adj_turn(t, 2)
                into(t, 1)
                pe.wait_ge(adjT_ok, 3 * t + 3)
                if t >= 1:
                    pe.wait_ge(out0_ok, t)
                for m in range(2):
                    for j in range(NT):
                        mm = pe.matmul(bank[2][:, m * TP:(m + 1) * TP], msg[:, j, m * 128:(m + 1) * 128],
                                       adjT[t % 2][:, j, :], start=(j == 0), stop=(j == NT - 1))
                mm.then_inc(out0_ps, 1)

            pe.wait_ge(out0_ok, NT)
            pe.wait_ge(out1_ok, 6)
            pe.wait_ge(ld_small, 16)
            w1g = little("w1g").rearrange("p (k n) -> p k n", k=KD)
            for t in range(NT):
                if t >= 2:
                    pe.wait_ge(hid_ok, t - 1)
                for k in range(KD):
                    mm = pe.matmul(bank[t % 2][0:TP, 0:GH], msgT[:, k, t * TP:(t + 1) * TP], w1g[:, k, :],
                                   start=(k == 0), stop=(k == KD - 1))
                mm.then_inc(hid_ps, 1)

            def hid_turn(t):
                pe.wait_ge(hn_ok, t + 1)
                if t >= 2:
                    pe.wait_ge(hidT_ok, t - 1)
                pe.transpose(bank[2 + t % 2][:, 0:TP], hid[:, t, :], ident[0:TP, 0:TP]).then_inc(hT_ps, 1)

            def hid_out(t):
                pe.wait_ge(hidT_ok, t + 1)
                if t >= 2:
                    pe.wait_ge(upd_ok, t - 1)
                pe.matmul(bank[4 + t % 2][0:TP, :], hidT[:, t % 2, :], little("w2g"),
                          start=True, stop=True).then_inc(upd_ps, 1)

            hid_turn(0)
            for t in range(NT):
                if t + 1 < NT:
                    hid_turn(t + 1)
                hid_out(t)

            ws = little("ws").rearrange("p (k e) -> p k e", k=KD)

            def x2_turn(t):
                pe.wait_ge(x2_ok, t + 1)
                if t >= 2:
                    pe.wait_ge(x2T_ok[t % 2], t // 2)
                for k in range(KD):
                    mm = pe.transpose(bank[t % 2][:, k * TP:(k + 1) * TP], xn[:, t % 2, k * 128:(k + 1) * 128],
                                      ident[0:TP, 0:TP])
                mm.then_inc(x2T_ps, 1)

            def route(t):
                pe.wait_ge(x2T_ok[t % 2], t // 2 + 1)
                for k in range(KD):
                    mm = pe.matmul(bank[6][0:TP, t * E:(t + 1) * E], x2T[:, k, t * TP:(t + 1) * TP], ws[:, k, :],
                                   start=(k == 0), stop=(k == KD - 1))
                mm.then_inc(log_ps, 1)

            x2_turn(0)
            for t in range(NT):
                if t + 1 < NT:
                    x2_turn(t + 1)
                route(t)
            pe.wait_ge(oh_ok, 1)
            for t in range(NT - 1):
                n = NT - 1 - t
                pe.matmul(bank[7][0:TP, (t + 1) * E:NT * E].rearrange("p (a e) -> p a e", a=n), ones[0:TP, 0:TP],
                          oh[:, t:t + 1, :].to_broadcast([TP, n, E]), start=(t == 0), stop=False,
                          skip_group_check=True)
            pe.matmul(bank[7][0:TP, 0:NT * E], const("before")[0:TP, :], oh[:, :, :].rearrange("p t e -> p (t e)"),
                      start=False, stop=True, skip_group_check=True)
            for t in range(NT):
                mm = pe.matmul(bank[5][0:TP, 0:E], ones[0:TP, 0:TP], oh[:, t, :], start=(t == 0), stop=(t == NT - 1))
            mm.then_inc(rank_ps, 1)

            def xs_turn(c):
                pe.wait_ge(xs_ok, c + 1)
                if c >= 1:
                    pe.wait_ge(xsT_ok, c)
                for k in range(KD):
                    mm = pe.transpose(bank[0][:, k * CH:(k + 1) * CH], xs[:, c % 2, k * 128:(k + 1) * 128], ident)
                mm.then_inc(xsT_ps, 1)

            def up(c):
                pe.wait_ge(xsT_ok, c + 1)
                if c >= 1:
                    pe.wait_ge(h_ok, c)
                e = pe.value_load(own_i[0:1, c:c + 1], min_val=0, max_val=E - 1)
                for k in range(KD):
                    mm = pe.matmul(bank[1][:, 0:F], xsT[:, c % 2, k, :], w1_sb[:, k, bass.ds(e * F, F)],
                                   start=(k == 0), stop=(k == KD - 1))
                mm.then_inc(h_ps, 1)
                return e

            def h_turn(c):
                pe.wait_ge(h_ok, c + 1)
                if c >= 1:
                    pe.wait_ge(gelu_ok, 2 * c)
                for f in range(KF):
                    mm = pe.transpose(bank[2][:, f * CH:(f + 1) * CH], h_sb[:, c % 2, f * 128:(f + 1) * 128], ident)
                mm.then_inc(hc_ps, 1)

            def down(c, e):
                pe.wait_ge(gelu_ok, 2 * c + 2)
                if c >= 2:
                    pe.wait_ge(y_ok, c - 1)
                for f in range(KF):
                    mm = pe.matmul(bank[3 + c % 2][:, :], hT[:, c % 2, f, :], w2_sb[:, f, bass.ds(e * D, D)],
                                   start=(f == 0), stop=(f == KF - 1))
                mm.then_inc(y_ps, 1)

            pe.wait_ge(own_ok, 1)
            pe.wait_ge(ld_w1, 16)
            pe.wait_ge(ld_w2, 16)
            xs_turn(0)
            e = up(0)
            for c in range(NC):
                if c + 1 < NC:
                    xs_turn(c + 1)
                h_turn(c)
                e_next = up(c + 1) if c + 1 < NC else None
                down(c, e)
                e = e_next

        @block.vector
        def _(dve):
            steps = [0]

            def own_step(ins):
                ins.then_inc(v_step, 1)
                steps[0] += 1
                dve.wait_ge(v_step, steps[0])

            dve.wait_ge(ld_edge, 96)
            dve.tensor_reduce(top[:, 0:1], wraw, X, ALU.max).then_inc(top_col, 1)
            dve.tensor_copy(cell, src_i)
            own_step(dve.tensor_copy(away, dst_i))
            own_step(dve.scalar_tensor_tensor(cell, cell, float(N), away, ALU.mult, ALU.add))
            dve.wait_ge(ld_const, 16)
            dve.tensor_copy(wu[:, :, 1], const("rank")[0:TP, :].to_broadcast([TP, EC])).then_inc(cell_ok, 1)
            dve.wait_ge(top_row, 1)
            own_step(dve.tensor_reduce(top[0:1, 1:2], bank[3][0:1, 0:TP], X, ALU.max))
            dve.tensor_scalar(top[0:1, 2:3], top[0:1, 1:2], 0.0, -1.0, ALU.max, ALU.mult).then_inc(top_val, 1)
            own_step(dve.tensor_scalar(away, cell, -1.0, const("spare")[0:TP, :], ALU.mult, ALU.add))
            dve.wait_ge(top_bc, 1)
            dve.tensor_copy(top[:, 3:4], bank[4][0:TP, 0:1]).then_inc(top_sb, 1)

            def compare(g):
                n = min(GC, EC - g * GC)
                dve.wait_ge(cell_ps, g + 1)
                if g >= 2:
                    dve.wait_ge(tot_ps, g - 1)
                dve.tensor_tensor(same[:, g % 2, 0:n, :],
                                  bank[g % 2][0:TP, 0:n * TP].rearrange("p (c q) -> p c q", c=n),
                                  cell[:, g * GC:g * GC + n].unsqueeze(2).to_broadcast([TP, n, TP]),
                                  ALU.is_equal).then_inc(same_ok, 1)

            def finish_lot(i):
                g0, g1 = LOTS[i]
                a, b = g0 * GC, min(g1 * GC, EC)
                dve.wait_ge(tot_ps, g1)
                tv = bank[2][0:TP, 2 * a:2 * b].rearrange("p (c a) -> p c a", a=2)
                dve.tensor_copy(wsum[:, a:b], tv[:, :, 0])
                own_step(dve.tensor_scalar(again[:, a:b], tv[:, :, 1], const("rank2")[0:TP, :], None, ALU.is_ge))
                own_step(dve.tensor_tensor(again[:, a:b], again[:, a:b], away[:, a:b], ALU.mult))
                dve.tensor_tensor(cell_i[:, a:b], again[:, a:b], cell[:, a:b], ALU.add).then_inc(lot_ok, 1)

            def norm_stats(t):
                if t % 5 == 0:
                    dve.wait_ge(ld_x[t // 5], 32)
                own_step(dve.bn_stats(stat[:, t, :], rec[:, t, 0:D]))
                dve.bn_aggr(mv[:, t, :], stat[:, t, :]).then_inc(var_ok, 1)

            for i, (g0, g1) in enumerate(LOTS):
                for g in range(g0, g1):
                    compare(g)
                finish_lot(i)
                if i == 1:
                    for t in range(NT):
                        norm_stats(t)

            dve.wait_ge(std_ok, 1)
            own_step(dve.reciprocal(rstd[:, :], std[:, :]))

            def norm(t):
                if t >= 2:
                    dve.wait_ge(xT_ps, t - 1)
                dve.tensor_scalar(xn[:, t % 2, :], rec[:, t, 0:D], mv[:, t, 0:1], rstd[:, t:t + 1],
                                  ALU.subtract, ALU.mult).then_inc(xn_ok, 1)

            norm(0)
            norm(1)
            dve.memset(ctxd[:, :, :], 0.0)
            own_step(dve.memset(ksumd[:, :, :], 0.0))
            dve.wait_ge(ld_bias, 16)
            for t in range(NT):
                r = t % 2
                if t >= 2:
                    dve.wait_ge(ctx_ps, t - 1)
                dve.wait_ge(q_ps, t + 1)
                dve.tensor_tensor(qk[:, r, 0, :], bank[3][0:TP, :], bias("q"), ALU.add).then_inc(q_sb, 1)
                dve.wait_ge(k_ps, t + 1)
                dve.tensor_tensor(qk[:, r, 1, :], bank[4][0:TP, :], bias("k"), ALU.add).then_inc(k_sb, 1)
                heads = qk[:, r, :, :].rearrange("p a (h d) -> p (a h) d", d=DH)
                dve.wait_ge(q_sb, t + 1)
                dve.wait_ge(k_sb, t + 1)
                own_step(dve.tensor_reduce(hmax[:, :], heads, X, ALU.max))
                dve.tensor_tensor(heads, heads, hmax[:, :].unsqueeze(2).to_broadcast([TP, 2 * H, DH]),
                                  ALU.subtract).then_inc(shifted, 1)
                if t + 2 < NT:
                    norm(t + 2)
                dve.wait_ge(v_ps, t + 1)
                dve.tensor_tensor(v_sb[:, r, :], bank[5][0:TP, :], bias("v"), ALU.add).then_inc(v_ok, 1)
                dve.wait_ge(m_ps, t + 1)
                dve.tensor_tensor(msg[:, t, :], bank[6][0:TP, 0:MD], bias("m"), ALU.add).then_inc(m_ok, 1)
                dve.wait_ge(exp_ok, t + 1)
                own_step(dve.tensor_reduce(hsum[:, :], heads, X, ALU.add))
                own_step(dve.reciprocal(hrec[:, :], hsum[:, :]))
                dve.wait_ge(v_ok, t + 1)
                dve.tensor_tensor(heads, heads, hrec[:, :].unsqueeze(2).to_broadcast([TP, 2 * H, DH]),
                                  ALU.mult).then_inc(soft_ok, 1)

            dve.wait_ge(ctx_ps, NT)
            for h in range(2):
                s = slice(64 * h, 64 * h + 64)
                dve.tensor_copy(ctxd[s, :, s], bank[7][s, :].rearrange("p (k n) -> p k n", k=4)[:, :, s])
                last = dve.tensor_copy(ksumd[s, :, s], bank[2][s, 0:4].unsqueeze(2).to_broadcast([64, 4, 64]))
            last.then_inc(ctx_ok, 1)
            for t in range(NT):
                last = dve.tensor_tensor(rec[:, t, 0:D], rec[:, t, 0:D], bias("p"), ALU.add)
            own_step(last)

            def attend(step):
                s, k = divmod(step, 4)
                a, b = SPANS[s]
                rd = rden[:, step % 2, 0:b - a]
                dve.wait_ge(den_ps, step + 1)
                own_step(dve.reciprocal(rd, bank[5 + step % 2][:, 0:b - a]))
                dve.wait_ge(num_ps, step + 1)
                own_step(dve.tensor_tensor(rd, bank[3 + step % 2][:, 0:b - a], rd, ALU.mult))
                dve.tensor_tensor(aoT[:, k, a:b], rd, qT[:, k, a:b], ALU.add).then_inc(ao_ok, 1)

            def mix_add(t):
                dve.wait_ge(mix_ps, t + 1)
                dve.tensor_tensor(rec[:, t, 0:D], rec[:, t, 0:D], bank[t % 2][0:TP, :], ALU.add).then_inc(mix_ok, 1)

            dve.wait_ge(qT_ok, NT)
            for step in range(12):
                attend(step)
                if 6 <= step < 10:
                    mix_add(step - 6)
            for t in range(4, NT):
                mix_add(t)

            def adj_add(t):
                rw = rows[t % 3]
                dve.wait_ge(add1_ok, t + 1)
                dve.scalar_tensor_tensor(rw[:, 0, :], rw[:, 0, :], 1.0, rw[:, 2, :], ALU.mult, ALU.add,
                                         accum_out=rs[:, t:t + 1]).then_inc(adj_sum, 1)
                dve.wait_ge(adj_sum, t + 1)
                dve.tensor_scalar(valid[:, t:t + 1], rs[:, t:t + 1], 0.0, None, ALU.is_gt)
                own_step(dve.tensor_scalar(rse[:, t:t + 1], rs[:, t:t + 1], 1e-6, None, ALU.add))
                dve.reciprocal(rinv[:, t:t + 1], rse[:, t:t + 1]).then_inc(rinv_ok, 1)

            def out0_copy(t):
                dve.wait_ge(out0_ps, t + 1)
                dve.tensor_copy(msgT[:, 0:2, t * TP:(t + 1) * TP],
                                bank[2][:, 0:2 * TP].rearrange("p (m n) -> p m n", m=2)).then_inc(out0_ok, 1)

            for t in range(NT):
                adj_add(t)
                if t >= 1:
                    out0_copy(t - 1)
            dve.wait_ge(out1_ps, NT)
            for m, a, b, bk, lo in ((0, 0, 500, 3, 0), (0, 1000, 1250, 7, 0), (1, 1000, 1250, 7, 250)):
                dve.tensor_copy(msgT[:, 2 + m, a:b], bank[bk][:, lo:lo + b - a]).then_inc(out1_ok, 1)
            out0_copy(NT - 1)

            for t in range(NT):
                dve.wait_ge(hid_ps, t + 1)
                dve.tensor_tensor(hid[:, t, :], bank[t % 2][0:TP, 0:GH], bias("g1"), ALU.add).then_inc(hid_ok, 1)
                dve.wait_ge(hid_ok, t + 1)
                own_step(dve.bn_stats(stat[:, t, :], hid[:, t, :]))
                dve.bn_aggr(mv[:, t, :], stat[:, t, :]).then_inc(hvar_ok, 1)
            dve.wait_ge(hstd_ok, 1)
            own_step(dve.reciprocal(rstd[:, :], std[:, :]))

            def hid_norm(t):
                dve.tensor_scalar(hid[:, t, :], hid[:, t, :], mv[:, t, 0:1], rstd[:, t:t + 1],
                                  ALU.subtract, ALU.mult).then_inc(hn_ok, 1)

            def upd_bias(t):
                dve.wait_ge(upd_ps, t + 1)
                if t >= 2:
                    dve.wait_ge(x1_ok, t - 1)
                dve.tensor_tensor(upd[:, t % 2, :], bank[4 + t % 2][0:TP, :], bias("g2"), ALU.add).then_inc(upd_ok, 1)

            def x1_add(t):
                dve.wait_ge(relu_ok, t + 1)
                dve.tensor_tensor(rec[:, t, 0:D], rec[:, t, 0:D], upd[:, t % 2, :], ALU.add).then_inc(x1_ok, 1)
                dve.wait_ge(x1_ok, t + 1)
                own_step(dve.bn_stats(stat[:, t, :], rec[:, t, 0:D]))
                dve.wait_ge(hn_ok, NT)
                dve.bn_aggr(mv[:, t, :], stat[:, t, :]).then_inc(var2_ok, 1)

            for t in range(NT):
                hid_norm(t)
            for t in range(NT):
                upd_bias(t)
                if t >= 1:
                    x1_add(t - 1)
            x1_add(NT - 1)

            dve.wait_ge(std2_ok, 1)
            own_step(dve.reciprocal(rstd[:, :], std[:, :]))
            own_step(dve.scalar_tensor_tensor(nmr[:, :], mv[:, :, 0], -1.0, rstd[:, :], ALU.mult, ALU.mult))
            dve.tensor_copy(rec[:, :, R_RS], rstd[:, :]).then_inc(nmr2_ok, 1)
            dve.tensor_copy(rec[:, :, R_NM], nmr[:, :])
            dve.tensor_copy(rec[:, :, R_ID], const("tag")[0:TP, :])
            for t in range(0, NT, 2):
                dve.wait_ge(x2T_ps, t + 1)
                dve.tensor_copy(x2T[:, :, t * TP:(t + 1) * TP],
                                bank[t % 2][:, 0:KD * TP].rearrange("p (k n) -> p k n", k=KD)).then_inc(x2T_ok[0], 1)

            def over_e(a):
                return a.unsqueeze(2).to_broadcast([TP, NT, E])

            dve.wait_ge(log_ps, NT)
            own_step(dve.tensor_tensor(logit[:, :, :], bank[6][0:TP, 0:NT * E].rearrange("p (t e) -> p t e", t=NT),
                                       bias("s").unsqueeze(1).to_broadcast([TP, NT, E]), ALU.add))
            own_step(dve.tensor_reduce(lmax[:, :], logit[:, :, :], X, ALU.max))
            dve.tensor_tensor(eq[:, :, :], logit[:, :, :], over_e(lmax[:, :]), ALU.is_equal)
            own_step(dve.tensor_tensor(logit[:, :, :], logit[:, :, :], over_e(lmax[:, :]), ALU.subtract))
            prefer = const("prefer")[0:TP, :].rearrange("p (t e) -> p t e", t=NT)
            dve.tensor_copy(cnt[:, 2, :], cst[0:TP, CONSTS["ident"][0]:CONSTS["ident"][0] + E]).then_inc(log_ok, 1)
            own_step(dve.tensor_tensor(eq[:, :, :], eq[:, :, :], prefer, ALU.mult))
            own_step(dve.tensor_reduce(best[:, :], eq[:, :, :], X, ALU.max))
            dve.tensor_tensor(oh[:, :, :], prefer, over_e(best[:, :]), ALU.is_equal).then_inc(oh_ok, 1)
            dve.wait_ge(lexp_ok, 1)
            own_step(dve.tensor_reduce(psm[:, :], logit[:, :, :], X, ALU.add))
            dve.reciprocal(rec[:, :, R_P], psm[:, :])
            own_step(dve.memset(cnt[:, 2, :], 0.0))
            dve.wait_ge(rank_ps, 1)
            own_step(dve.tensor_scalar(cnt_i[:, 0, :], bank[5][0:TP, 0:E], float(CH - 1), None, ALU.add))
            own_step(dve.tensor_scalar(cnt_i[:, 1, :], cnt_i[:, 0, :], CH.bit_length() - 1, None,
                                       ALU.logical_shift_right))
            own_step(dve.tensor_copy(cnt[:, 0, :], cnt_i[:, 1, :]))
            own_step(dve.tensor_tensor_scan(cnt[:, 1, :], cnt[:, 0, :], cnt[:, 2, :], 0.0, ALU.add, ALU.add))
            own_step(dve.tensor_tensor(cnt[:, 3, :], cnt[:, 1, :], cnt[:, 0, :], ALU.subtract))
            own_step(dve.tensor_scalar(cnt[:, 3, :], cnt[:, 3, :], float(CH), None, ALU.mult))
            own_step(dve.tensor_tensor(eq[:, :, :], bank[7][0:TP, 0:NT * E].rearrange("p (t e) -> p t e", t=NT),
                                       cnt[:, 3:4, :].to_broadcast([TP, NT, E]), ALU.add))
            own_step(dve.tensor_tensor(eq[:, :, :], eq[:, :, :], oh[:, :, :], ALU.mult))
            own_step(dve.tensor_reduce(best[:, :], eq[:, :, :], X, ALU.add))
            dve.tensor_copy(pos_i[:, :], best[:, :]).then_inc(pos_ok, 1)
            own_step(dve.tensor_tensor(own[:, :, :], cnt[0:1, 1:2, :].to_broadcast([1, NC, E]),
                                       const("chunk")[0:1, :].rearrange("p (c e) -> p c e", c=NC), ALU.is_le))
            own_step(dve.tensor_reduce(ownf[:, :], own[:, :, :], X, ALU.add))
            dve.tensor_scalar(own_i[:, :], ownf[:, :], float(E - 1), None, ALU.min).then_inc(own_ok, 1)

            def h_copy(c):
                dve.wait_ge(h_ps, c + 1)
                if c >= 2:
                    dve.wait_ge(hc_ps, c - 1)
                dve.tensor_copy(h_sb[:, c % 2, :], bank[1][:, 0:F]).then_inc(h_ok, 1)

            def finish(c):
                e = dve.value_load(own_i[0:1, c:c + 1], min_val=0, max_val=E - 1)
                dve.tensor_scalar(out_i[:, c:c + 1], rec_c[:, c % 3, R_ID:R_ID + 1], -1.0, float(PADID),
                                  ALU.mult, ALU.add)
                dve.wait_ge(y_ps, c + 1)
                dve.tensor_tensor(y_sb[:, c % 2, :], bank[3 + c % 2][:, :], b2_sb[:, bass.ds(e * D, D)],
                                  ALU.add).then_inc(y_ok, 1)
                dve.wait_ge(y_ok, c + 1)
                if c >= 2:
                    dve.wait_ge(out_st[c % 2], 16 * (c // 2))
                dve.scalar_tensor_tensor(o_sb[:, c % 2, :], y_sb[:, c % 2, :], rec_c[:, c % 3, R_P:R_P + 1],
                                         rec_c[:, c % 3, 0:D], ALU.mult, ALU.add).then_inc(o_ok, 1)

            dve.wait_ge(own_ok, 1)
            dve.wait_ge(ld_b2, 16)
            h_copy(0)
            for c in range(NC):
                if c + 1 < NC:
                    h_copy(c + 1)
                dve.wait_ge(ld_rec[c % 3], 16 * (c // 3 + 1))
                finish(c)

        @block.scalar
        def _(act):
            act.wait_ge(ld_edge, 96)
            act.wait_ge(top_sb, 1)
            act.activation(wu[:, :, 0], wraw, ACT.Exp, bias=top[:, 3:4]).then_inc(w_exp, 1)
            act.wait_ge(var_ok, NT)
            act.activation(std[:, :], mv[:, :, 1], ACT.Sqrt, bias=const("eps")[0:TP, :]).then_inc(std_ok, 1)

            def x_copy(t):
                act.wait_ge(xT_ps, t + 1)
                act.activation(xT[:, :, t * TP:(t + 1) * TP],
                               bank[0][:, 0:KD * TP].rearrange("p (k n) -> p k n", k=KD), ACT.Copy).then_inc(xT_ok, 1)

            def q_copy(t):
                act.wait_ge(qT_ps, t + 1)
                act.activation(qT[:, :, t * TP:(t + 1) * TP],
                               bank[1][:, 0:KD * TP].rearrange("p (k n) -> p k n", k=KD), ACT.Copy).then_inc(qT_ok, 1)

            x_copy(0)
            for t in range(NT):
                if t + 1 < NT:
                    x_copy(t + 1)
                act.wait_ge(shifted, t + 1)
                act.activation(qk[:, t % 2, :, :], qk[:, t % 2, :, :], ACT.Exp).then_inc(exp_ok, 1)
                if t >= 1:
                    q_copy(t - 1)
            q_copy(NT - 1)

            def adj_norm(t):
                act.wait_ge(rinv_ok, t + 1)
                act.activation(rows[t % 3][:, 0, :], rows[t % 3][:, 0, :], ACT.Copy,
                               scale=rinv[:, t:t + 1]).then_inc(adj_ok, 1)

            def adj_copy(t, part):
                lo, hi = (0, 4, 8)[part], (4, 8, 10)[part]
                n = 3 * t + part
                act.wait_ge(adjT_ps, n + 1)
                if t >= 2 and part == 0:
                    act.wait_ge(out0_ps, t - 1)
                act.activation(adjT[t % 2][:, lo:hi, :],
                               bank[n % 2][0:TP, 0:(hi - lo) * TP].rearrange("p (j n) -> p j n", j=hi - lo),
                               ACT.Copy).then_inc(adjT_ok, 1)

            adj_norm(0)
            for t in range(NT):
                adj_copy(t, 0)
                adj_copy(t, 1)
                adj_copy(t, 2)
                if t + 1 < NT:
                    adj_norm(t + 1)
            act.wait_ge(out1_ps, NT)
            for m, a, b, bk in ((1, 0, 500, 5), (1, 500, 1000, 6), (0, 500, 1000, 4)):
                act.activation(msgT[:, 2 + m, a:b], bank[bk][:, 0:500], ACT.Copy).then_inc(out1_ok, 1)

            act.wait_ge(hvar_ok, NT)
            act.activation(std[:, :], mv[:, :, 1], ACT.Sqrt, bias=const("eps")[0:TP, :]).then_inc(hstd_ok, 1)

            def hid_copy(t):
                act.wait_ge(hT_ps, t + 1)
                if t >= 2:
                    act.wait_ge(upd_ps, t - 1)
                act.activation(hidT[:, t % 2, :], bank[2 + t % 2][:, 0:TP], ACT.Relu, bias=little("beta"),
                               scale=little("gamma")).then_inc(hidT_ok, 1)

            def relu(t):
                act.wait_ge(upd_ok, t + 1)
                act.activation(upd[:, t % 2, :], upd[:, t % 2, :], ACT.Relu, scale=valid[:, t:t + 1]).then_inc(relu_ok, 1)

            hid_copy(0)
            for t in range(NT):
                if t + 1 < NT:
                    hid_copy(t + 1)
                relu(t)

            act.wait_ge(var2_ok, NT)
            act.activation(std[:, :], mv[:, :, 1], ACT.Sqrt, bias=const("eps")[0:TP, :]).then_inc(std2_ok, 1)
            act.wait_ge(nmr2_ok, 1)

            def x2_norm(t):
                if t >= 2:
                    act.wait_ge(x2T_ps, t - 1)
                act.activation(xn[:, t % 2, :], rec[:, t, 0:D], ACT.Identity, bias=nmr[:, t:t + 1],
                               scale=rstd[:, t:t + 1]).then_inc(x2_ok, 1)

            x2_norm(0)
            for t in range(NT):
                if t + 1 < NT:
                    x2_norm(t + 1)
                if t % 2 == 1:
                    act.wait_ge(x2T_ps, t + 1)
                    act.activation(x2T[:, :, t * TP:(t + 1) * TP],
                                   bank[t % 2][:, 0:KD * TP].rearrange("p (k n) -> p k n", k=KD),
                                   ACT.Copy).then_inc(x2T_ok[1], 1)
            act.wait_ge(log_ok, 1)
            act.activation(logit[:, :, :], logit[:, :, :], ACT.Exp).then_inc(lexp_ok, 1)

            def xs_norm(c):
                act.wait_ge(ld_rec[c % 3], 16 * (c // 3 + 1))
                if c >= 2:
                    act.wait_ge(xsT_ps, c - 1)
                rc = rec_c[:, c % 3, :]
                act.activation(xs[:, c % 2, :], rc[:, 0:D], ACT.Identity, bias=rc[:, R_NM:R_NM + 1],
                               scale=rc[:, R_RS:R_RS + 1]).then_inc(xs_ok, 1)

            def xs_copy(c):
                act.wait_ge(xsT_ps, c + 1)
                if c >= 2:
                    act.wait_ge(h_ps, c - 1)
                act.activation(xsT[:, c % 2, :, :], bank[0][:, :].rearrange("p (k n) -> p k n", k=KD),
                               ACT.Copy).then_inc(xsT_ok, 1)

            def gelu(c):
                e = act.value_load(own_i[0:1, c:c + 1], min_val=0, max_val=E - 1)
                act.wait_ge(hc_ps, c + 1)
                if c >= 2:
                    act.wait_ge(y_ps, c - 1)
                for f in range(KF):
                    b1 = little("b1").rearrange("p (f e) -> p f e", f=KF)
                    act.activation(hT[:, c % 2, f, :], bank[2][:, f * CH:(f + 1) * CH], ACT.Gelu,
                                   bias=b1[:, f, bass.ds(e, 1)]).then_inc(gelu_ok, 1)

            act.wait_ge(own_ok, 1)
            xs_norm(0)
            xs_norm(1)
            xs_copy(0)
            for c in range(NC):
                if c + 1 < NC:
                    xs_copy(c + 1)
                gelu(c)
                if c + 2 < NC:
                    xs_norm(c + 2)


def constants():
    c = np.zeros((128, CW), np.float32)
    p = np.arange(128)

    def put(name, v):
        a, w = CONSTS[name]
        c[:, a:a + w] = v

    put("ident", np.eye(128))
    put("ones", 1.0)
    put("before", p[:, None] < np.arange(TP)[None, :])
    rank = np.where(p < TP, 2.0 ** (126.0 - 2 * np.minimum(p, TP - 1)), 0.0)
    put("rank", rank[:, None])
    put("rank2", 2 * rank[:, None])
    put("spare", (SPARE + p)[:, None])
    put("tag", PADID - (np.arange(NT)[None, :] * TP + p[:, None]))
    put("prefer", np.tile(E - np.arange(E), NT)[None, :])
    put("chunk", np.repeat(np.arange(NC), E)[None, :])
    put("eps", LN_EPS)
    return c


def kernel(x, src, dst, edge_weight, L0_gnn_Wm, L0_gnn_bm, L0_gnn_W1, L0_gnn_b1, L0_gnn_gamma, L0_gnn_beta,
           L0_gnn_W2, L0_gnn_b2, L0_mix_Wq, L0_mix_bq, L0_mix_Wk, L0_mix_bk, L0_mix_Wv, L0_mix_bv, L0_mix_Wp,
           L0_mix_bp, L0_ffn_Ws, L0_ffn_bs, L0_ffn_W1, L0_ffn_b1, L0_ffn_W2, L0_ffn_b2):
    import concourse.bacc as bacc
    from concourse.bass_utils import run_bass_kernel_spmd

    def arr(a):
        return np.asarray(a)

    def rows_first(w):
        return arr(w).reshape(-1, 128, w.shape[-1]).transpose(1, 0, 2)

    wqkvm = np.concatenate([rows_first(arr(w).T) for w in (L0_mix_Wq, L0_mix_Wk, L0_mix_Wv)]
                           + [rows_first(L0_gnn_Wm)], axis=2)
    biases = np.concatenate([arr(b) for b in (L0_mix_bq, L0_mix_bk, L0_mix_bv, L0_gnn_bm, L0_mix_bp, L0_gnn_b1,
                                              L0_gnn_b2, L0_ffn_bs)])
    small = np.concatenate([
        arr(L0_gnn_gamma)[:, None], arr(L0_gnn_beta)[:, None],
        arr(L0_ffn_b1).reshape(E, KF, 128).transpose(2, 1, 0).reshape(128, -1),
        rows_first(L0_ffn_Ws).reshape(128, -1), rows_first(L0_gnn_W1).reshape(128, -1), arr(L0_gnn_W2)], axis=1)
    arrays = {
        "x": arr(x), "edge_src": arr(src), "edge_dst": arr(dst), "edge_w": arr(edge_weight),
        "consts": constants(), "biases": biases, "small": small, "wqkvm": wqkvm,
        "wp": rows_first(arr(L0_mix_Wp).T),
        "w1f": arr(L0_ffn_W1).reshape(E, KD, 128, F).transpose(2, 1, 0, 3).reshape(128, KD, E * F),
        "w2f": arr(L0_ffn_W2).reshape(E, KF, 128, D).transpose(2, 1, 0, 3).reshape(128, KF, E * D),
        "b2f": arr(L0_ffn_b2).reshape(-1),
    }
    arrays = {k: np.ascontiguousarray(v) for k, v in arrays.items()}
    nc = bacc.Bacc("TRN2", target_bir_lowering=False, num_devices=1)
    args = {k: nc.dram_tensor(f"in_{k}", v.shape, mybir.dt.from_np(v.dtype), kind="ExternalInput").ap()
            for k, v in arrays.items()}
    out = nc.dram_tensor("out", (N, D), F32, kind="ExternalOutput").ap()
    build(nc, out=out, **args)
    r = run_bass_kernel_spmd(nc, [{f"in_{k}": v for k, v in arrays.items()}], core_ids=[0])
    return r.results[0]["out"]
```

```python
from contextlib import ExitStack

import numpy as np
import concourse.bass as bass
import concourse.mybir as mybir

F32 = mybir.dt.float32
I32 = mybir.dt.int32
BF16 = mybir.dt.bfloat16
F16 = mybir.dt.float16
F32R = mybir.dt.float32r
ALU = mybir.AluOpType
ACT = mybir.ActivationFunctionType
X = mybir.AxisListType.X

N, D, NE = 1250, 512, 21250
TP, NT = 125, 10
KD = D // 128
H, DH = 8, 64
MD, GH = D // 2, D // 4
E, F = 8, 256
KF = F // 128
EC = NE // TP
GC = 2
NG = EC // GC
TG = 4
G0 = NG - TG * NT
STATS_FROM = 24
NTAB = 2
PIECES = 6
TABW = 12288
SPARE = N * N
CH = 128
NC = (N + E * (CH - 1)) // CH
RING = 8
PADID = 2000
W_ROW = D + 4
R_P, R_RS, R_NM = D, D + 1, D + 2
SRCMUL = 2048
LN_EPS = 1e-5
SPANS = [(0, 500), (500, 1000), (1000, 1250)]

CONSTS, CW = {}, 0
for _n, _w in (("ident", 128), ("ones", 128), ("before", TP), ("rank", 2), ("limit", 2), ("spare", 2),
               ("tag", NT), ("prefer", NT * E), ("chunk", NC * E), ("cols", CH), ("eps", 1)):
    CONSTS[_n] = (CW, _w)
    CW += _w
BIAS, BW = {}, 0
for _n, _w in (("q", D), ("k", D), ("v", D), ("m", MD), ("p", D), ("g1", GH), ("g2", D), ("s", E)):
    BIAS[_n] = (BW, _w)
    BW += _w
SMALL, SW = {}, 0
for _n, _w in (("gamma", 1), ("beta", 1), ("b1", KF * E), ("ws", KD * E), ("w1g", KD * GH), ("w2g", D)):
    SMALL[_n] = (SW, _w)
    SW += _w

REGION = 39304
ZW = 1024
WN = 3 * D + MD

LOTS = [(0, 2), (2, 12), (12, 28), (28, G0)]
LOTS0 = len(LOTS)
LOTS += [(G0 + TG * t, G0 + TG * (t + 1)) for t in range(NT)]
HIDBANK = (0, 1, 2, 5, 6)
HALF = 4
KEYBANK = (0, 1, 6, 7)
ALONE = 3


def table_turns():
    return [0 if g < ALONE else (g - ALONE + 1) % NTAB for g in range(NG)]


def build(nc, x, edge_src, edge_dst, edge_w, consts, biases, small, wqkvm, wp, w1f, w2f, b2f, out):
    turns = table_turns()
    with ExitStack() as ctx:
        def sb(name, shape, dt=F32):
            return ctx.enter_context(nc.sbuf_tensor(name, shape, dt))

        def sem(name):
            return ctx.enter_context(nc.semaphore(name))

        tables = [nc.dram_tensor(f"edge_table{k}", [128 * TABW, 1], F32).ap() for k in range(NTAB)]
        x1_rows = nc.dram_tensor("x1_rows", [N, W_ROW], F32).ap()

        cst = sb("cst", [128, CW])
        bia = sb("bia", [128, BW])
        sml = sb("sml", [128, SW])
        rec = sb("rec", [TP, NT, D])
        xn = sb("xn", [TP, 2, D])

        def const(name):
            a, w = CONSTS[name]
            return cst[:, a:a + w]

        def bias(name):
            a, w = BIAS[name]
            return bia[0:TP, a:a + w]

        def little(name):
            a, w = SMALL[name]
            return sml[:, a:a + w]

        ident, ones = const("ident"), const("ones")
        base = (nc.sbuf_usable_end - 4 * REGION) // 32 * 32

        def place(name, col, shape, dt=F32):
            return nc.alloc_sbuf_tensor_at(name, shape, dt, offset=base + 4 * col)

        E0 = 35288
        src_i = place("src_i", E0, [TP, EC], I32)
        dst_i = place("dst_i", E0 + 176, [TP, EC], I32)
        wraw = place("wraw", E0 + 352, [TP, EC])
        cell = place("cell", E0 + 528, [TP, EC])
        away = place("away", E0 + 704, [TP, EC])
        again = place("again", E0 + 880, [TP, EC])
        cell_i = place("cell_i", E0 + 1056, [TP, EC], I32)
        wsum = place("wsum", E0 + 1232, [TP, EC])
        wexp = place("wexp", E0 + 1408, [TP, EC])
        key = place("key", E0 + 1584, [TP, EC])
        same = place("same", E0 + 1760, [TP, 2, GC, GC * TP], BF16)
        wu = place("wu", E0 + 2264, [TP, EC, 4], BF16)
        endsT = place("endsT", E0 + 2608, [NG, 2, GC * TP], F16)
        eye16 = place("eye16", E0 + 2864, [TP, 2, TP], F16)
        zeros = place("zeros", E0 + 2992, [128, ZW])
        w_raw = place("w_raw", 0, [128, KD, WN])
        w_hi = place("w_hi", 7168, [128, KD, WN], F32R)
        w_lo = place("w_lo", 14336, [128, KD, WN], F32R)
        q_sb = place("q_sb", 21504, [TP, NT, D])
        wp_raw = place("wp_raw", 26624, [128, KD, D])
        k_sb = place("k_sb", 28672, [TP, 2, D])
        v_sb = place("v_sb", 29696, [TP, 2, KD, 129])
        xT_hi = place("xT_hi", 30728, [128, 2, KD, TP], F32R)
        xT_lo = place("xT_lo", 31728, [128, 2, KD, TP], F32R)
        msg = place("msg", 32728, [TP, NT, MD])
        qT = place("qT", 0, [128, KD, N])
        wp_hi = place("wp_hi", 7168, [128, KD, D], F32R)
        wp_lo = place("wp_lo", 9216, [128, KD, D], F32R)
        ao = k_sb
        msg_hi = place("msg_hi", 14336, [TP, NT, MD], F32R)
        msg_lo = place("msg_lo", 16896, [TP, NT, MD], F32R)
        scaled_hi = place("scaled_hi", 19456, [TP, 2, MD], F32R)
        scaled_lo = place("scaled_lo", 19968, [TP, 2, MD], F32R)
        rows = [place(f"rows{r}", col, [TP, NTAB, N]) for r, col in enumerate((35288, 11264, 21504))]
        adj_hi = place("adj_hi", 0, [TP, 2, N], F32R)
        adj_lo = place("adj_lo", 2504, [TP, 2, N], F32R)
        adjT_hi = place("adjT_hi", 5008, [TP, 2, NT, TP], F32R)
        adjT_lo = place("adjT_lo", 7512, [TP, 2, NT, TP], F32R)
        msgT = place("msgT", 24008, [128, KD, N])
        out0 = place("out0", 32296, [TP, MD])
        hid = place("hid", 29008, [TP, NT, GH])
        hidT = place("hidT", 30288, [128, 2, TP])
        upd = place("upd", 30544, [TP, 2, D])
        w1_sb = place("w1_sb", 0, [128, KD, E * F])
        b2_sb = place("b2_sb", 8192, [128, E * D])
        w2_sb = place("w2_sb", 14336, [128, KF, E * D])
        x2T = msgT
        row_hot = place("row_hot", 31568, [TP, NT, CH], F16)
        chunk_tag = place("chunk_tag", 32208, [TP, NT, NC], F16)
        rec_c = place("rec_c", 24008, [128, RING, W_ROW])
        xs = place("xs", 32728, [128, 2, D])
        xsT = place("xsT", 33752, [128, 2, KD, CH])
        h_sb = place("h_sb", 34776, [128, 2, F])
        hT = place("hT", 35288, [128, 2, KF, CH])
        y_sb = place("y_sb", 35800, [128, 2, D])
        o_sb = place("o_sb", 36824, [128, 2, D])

        top = sb("top", [TP, 4])
        stat = sb("stat", [TP, NT, 6])
        mv = sb("mv", [TP, NT, 2])
        std = sb("std", [TP, NT])
        rstd = sb("rstd", [TP, NT])
        factors = sb("factors", [TP, NT, 4])
        hmax = sb("hmax", [TP, 2, H])
        hsum = sb("hsum", [TP, 2, H])
        hrec = sb("hrec", [TP, 2, H])
        ctxd = sb("ctxd", [128, 4, 130])
        rden = sb("rden", [TP, 2, 2, 2])
        rs = sb("rs", [TP, NT])
        rse = sb("rse", [TP, NT])
        rinv = sb("rinv", [TP, NT])
        valid = sb("valid", [TP, NT])
        logit = sb("logit", [TP, NT, E])
        eq = sb("eq", [TP, NT, E])
        oh = sb("oh", [TP, NT, E])
        oh16 = sb("oh16", [TP, NT, E], BF16)
        count16 = sb("count16", [TP, 2, TP], BF16)
        best = sb("best", [TP, NT])
        lmax = sb("lmax", [TP, NT])
        psm = sb("psm", [TP, NT])
        cnt_i = sb("cnt_i", [TP, 2, E], I32)
        cnt = sb("cnt", [TP, 4, E])
        pos_i = sb("pos_i", [TP, NT], I32)
        own = sb("own", [1, NC, E])
        ownf = sb("ownf", [1, NC])
        own_i = sb("own_i", [1, NC], I32)
        posf = sb("posf", [TP, 2, NT])
        rc_i = sb("rc_i", [TP, 2, NT], I32)
        chunk_hot = sb("chunk_hot", [TP, NT, NC])
        idf = sb("idf", [128, NC])
        out_i = sb("out_i", [128, NC], I32)
        get_i = sb("get_i", [128, NC], I32)

        bank = [ctx.enter_context(nc.psum_tensor(f"bank{i}", [128, 512], F32)) for i in range(8)]

        def hid_at(t):
            return bank[HIDBANK[t // 2]][0:TP, (t % 2) * GH:(t % 2 + 1) * GH]

        def key_at(g):
            if g < G0:
                return bank[KEYBANK[g % 4]][0:TP, 0:GC * TP]
            a = 256 * ((g - G0) % 2)
            return bank[1][0:TP, a:a + GC * TP]

        def tot_at(g0, g1):
            if g0 < G0:
                return bank[2][0:TP, 4 * GC * g0:4 * GC * g1]
            a = (g0 - G0) % TG
            return bank[6][0:TP, 256 + 4 * GC * a:256 + 4 * GC * (a + g1 - g0)]

        def ctx_at(k):
            return bank[7][:, k * 129:(k + 1) * 129] if k < 3 else bank[2][:, 0:129]

        def num_at(t, half):
            return bank[((3, 2), (4, 7))[t % 2][half]][0:TP, 0:260].rearrange("p (k n) -> p k n", k=2)

        ld_const, ld_edge, ld_bias, ld_small = sem("ld_const"), sem("ld_edge"), sem("ld_bias"), sem("ld_small")
        ld_x = [sem("ld_x0"), sem("ld_x1")]
        ld_wp, ld_w1, ld_w2, ld_b2 = sem("ld_wp"), sem("ld_w1"), sem("ld_w2"), sem("ld_b2")
        tab_zero = sem("tab_zero")
        ld_rows = [sem(f"ld_rows{r}") for r in range(3)]
        ld_wk = [sem(f"ld_wk{k}") for k in range(KD)]
        zero1 = [sem(f"zero1_{i}") for i in range(PIECES)]
        w_hi_ok, w_lo_ok, xT_lo_ok, wp_hi_ok, wp_lo_ok, aoT_lo_ok, msg_hi_ok, msg_lo_ok = (
            sem("w_hi_ok"), sem("w_lo_ok"), sem("xT_lo_ok"), sem("wp_hi_ok"), sem("wp_lo_ok"), sem("aoT_lo_ok"),
            sem("msg_hi_ok"), sem("msg_lo_ok"))
        adj_lo_ok, adjT_lo_ok, scaled_hi_ok, scaled_lo_ok, out0_sb, out0T_ps = (
            sem("adj_lo_ok"), sem("adjT_lo_ok"), sem("scaled_hi_ok"), sem("scaled_lo_ok"), sem("out0_sb"),
            sem("out0T_ps"))
        ld_rec = [sem(f"ld_rec{r}") for r in range(RING)]
        tab_add = [sem(f"tab_add{k}") for k in range(NTAB)]
        x1_st = sem("x1_st")
        out_st = [sem("out_st0"), sem("out_st1")]
        zeros_set, top_col, top_row, top_val, top_bc, top_sb, w_exp = (
            sem("zeros_set"), sem("top_col"), sem("top_row"), sem("top_val"), sem("top_bc"), sem("top_sb"), sem("w_exp"))
        w_split = sem("w_split")
        bp_ok, hid_got = sem("bp_ok"), sem("hid_got")
        ends_ok, ends_ps = sem("ends_ok"), sem("ends_ps")
        cell_ok, cell_ps, same_ok, tot_ps, lot_ok = (
            sem("cell_ok"), sem("cell_ps"), sem("same_ok"), sem("tot_ps"), sem("lot_ok"))
        stat_ok, var_ok, std_ok, xn_ok, xT_ps, xT_ok = sem("stat_ok"), sem("var_ok"), sem("std_ok"), sem("xn_ok"), sem("xT_ps"), sem("xT_ok")
        q_ps, k_ps, v_ps, m_ps = sem("q_ps"), sem("k_ps"), sem("v_ps"), sem("m_ps")
        q_got, k_got, v_ok, m_ok = sem("q_got"), sem("k_got"), sem("v_ok"), sem("m_ok")
        shifted, exp_ok, soft_ok, qT_ps, qT_ok, ctx_ps, ctx_ok = (
            sem("shifted"), sem("exp_ok"), sem("soft_ok"), sem("qT_ps"), sem("qT_ok"), sem("ctx_ps"), sem("ctx_ok"))
        num_ps, num_used, ao_ok, aoT_ps, aoT_ok, mix_ps, mix_ok = (
            sem("num_ps"), sem("num_used"), sem("ao_ok"), sem("aoT_ps"), sem("aoT_ok"),
            sem("mix_ps"), sem("mix_ok"))
        adj_sum, rinv_ok, adj_ok, adjT_ps, adjT_ok = (
            sem("adj_sum"), sem("rinv_ok"), sem("adj_ok"), sem("adjT_ps"), sem("adjT_ok"))
        out0_ps, out0_ok, out1_ps, out1_ok = (
            sem("out0_ps"), sem("out0_ok"), sem("out1_ps"), sem("out1_ok"))
        hid_ps, hvar_ok, hstd_ok, hn_ok, hT_ps, hidT_ok, upd_ps, upd_ok, relu_ok, x1_ok = (
            sem("hid_ps"), sem("hvar_ok"), sem("hstd_ok"), sem("hn_ok"), sem("hT_ps"), sem("hidT_ok"),
            sem("upd_ps"), sem("upd_ok"), sem("relu_ok"), sem("x1_ok"))
        var2_ok, std2_ok, x2_ok, x2T_ps, x2T_ok, log_ps, log_ok, lexp_ok, oh_ok, rank_ps = (
            sem("var2_ok"), sem("std2_ok"), sem("x2_ok"), sem("x2T_ps"), sem("x2T_ok"), sem("log_ps"),
            sem("log_ok"), sem("lexp_ok"), sem("oh_ok"), sem("rank_ps"))
        fac_ok, fac_st = sem("fac_ok"), sem("fac_st")
        hot_ok, ctab_ps, id_ok, own_ok = sem("hot_ok"), sem("ctab_ps"), sem("id_ok"), sem("own_ok")
        xs_ok, xsT_ps, xsT_ok, h_ps, h_ok, hc_ps, gelu_ok, y_ps, y_ok, o_ok = (
            sem("xs_ok"), sem("xsT_ps"), sem("xsT_ok"), sem("h_ps"), sem("h_ok"), sem("hc_ps"), sem("gelu_ok"),
            sem("y_ps"), sem("y_ok"), sem("o_ok"))
        v_step = sem("v_step")

        lot_of = [next(i for i, (a, b) in enumerate(LOTS) if a <= g < b) for g in range(NG)]

        def split(eng, dst, srcs, s):
            for a, b in ((0, 112), (112, TP)):
                eng.dma_start(dst(a, b), srcs(a, b)).then_inc(s, 16)

        block = ctx.enter_context(nc.Block())

        @block.sync
        def _(sp):
            def edges(v):
                return v.rearrange("(p c) -> p c", p=TP)

            split(sp, lambda a, b: src_i[a:b], lambda a, b: edges(edge_src)[a:b], ld_edge)
            split(sp, lambda a, b: dst_i[a:b], lambda a, b: edges(edge_dst)[a:b], ld_edge)
            split(sp, lambda a, b: wraw[a:b], lambda a, b: edges(edge_w)[a:b], ld_edge)
            sp.dma_start(cst[:, :], consts).then_inc(ld_const, 16)
            sp.wait_ge(zeros_set, 1)
            tab_v = [tb.rearrange("(p a n) b -> p a (n b)", p=128, n=ZW) for tb in tables]

            def zero(k, a, b, s):
                sp.dma_start(tab_v[k][:, a:b, :], zeros[:, :].unsqueeze(1).to_broadcast([128, b - a, ZW])).then_inc(s, 16)

            zero(0, 0, TABW // ZW, tab_zero)
            sp.wait_ge(tab_zero, 16)
            xv = x.rearrange("(t p) d -> p t d", p=TP)
            for h in range(2):
                t0 = 5 * h
                split(sp, lambda a, b: rec[a:b, t0:t0 + 5, :], lambda a, b: xv[a:b, t0:t0 + 5, :], ld_x[h])
            for k in range(KD):
                if k < 2:
                    sp.wait_ge(ld_x[k], 32)
                else:
                    sp.wait_ge(ld_wk[k - 2], 16)
                sp.dma_start(w_raw[:, k, :], wqkvm[:, k, :]).then_inc(ld_wk[k], 16)
            step = TABW // ZW // PIECES
            for i in range(PIECES):
                sp.wait_ge(ld_wk[2 + i] if i < 2 else zero1[i - 2], 16)
                zero(1, i * step, (i + 1) * step, zero1[i])
            sp.wait_ge(zero1[PIECES - 2], 16)
            sp.dma_start(bia[:, :], biases.partition_broadcast(128)).then_inc(ld_bias, 16)
            sp.wait_ge(zero1[PIECES - 1], 16)
            sp.dma_start(wp_raw[:, :, :], wp).then_inc(ld_wp, 16)
            for k in range(NTAB):
                sp.wait_ge(tab_add[k], 16 * GC * turns.count(k))
            views = [tb[0:N * N, :].rearrange("(t p n) b -> p t (n b)", p=TP, t=NT) for tb in tables]
            for t in range(NT):
                r = t % 3
                if t == 1:
                    sp.wait_ge(m_ps, NT)
                if t == 2:
                    sp.wait_ge(ao_ok, NT)
                if t >= 3:
                    sp.wait_ge(adj_lo_ok, t - 2)
                    sp.wait_ge(adjT_ps, 3 * (t - 2))
                for k in range(NTAB):
                    split(sp, lambda a, b: rows[r][a:b, k, :], lambda a, b: views[k][a:b, t, :], ld_rows[r])
                if t == 2:
                    sp.dma_start(sml[:, :], small).then_inc(ld_small, 16)
            sp.wait_ge(out1_ps, NT)
            sp.wait_ge(out0_ps, NT)
            sp.dma_start(w1_sb[:, :, :], w1f).then_inc(ld_w1, 16)
            sp.dma_start(w2_sb[:, :, :], w2f).then_inc(ld_w2, 16)
            sp.dma_start(b2_sb[:, :], b2f.partition_broadcast(128)).then_inc(ld_b2, 16)
            for t in range(NT):
                sp.wait_ge(x1_ok, t + 1)
                split(sp, lambda a, b: x1_rows[t * TP + a:t * TP + b, 0:D], lambda a, b: rec[a:b, t, :], x1_st)
            sp.wait_ge(fac_ok, 1)
            sp.dma_start(x1_rows.rearrange("(t p) n -> p t n", p=TP)[:, :, D:W_ROW], factors[:, :, :]).then_inc(fac_st, 16)

        @block.gpsimd
        def _(pool):
            pool.memset(zeros[:, :], 0.0).then_inc(zeros_set, 1)
            used = [0] * NTAB
            for g, k in enumerate(turns):
                if g == 0 or lot_of[g] != lot_of[g - 1]:
                    pool.wait_ge(lot_ok, lot_of[g] + 1)
                if used[k]:
                    pool.wait_ge(tab_add[k], 16 * GC * used[k])
                elif k == 0:
                    pool.wait_ge(tab_zero, 16)
                else:
                    for i in range(KD):
                        pool.wait_ge(w_hi_ok, i + 1)
                        pool.tensor_tensor(w_lo[:, i, :], w_raw[:, i, :], w_hi[:, i, :],
                                           ALU.subtract).then_inc(w_lo_ok, 1)
                    for z in zero1:
                        pool.wait_ge(z, 16)
                for c in range(g * GC, (g + 1) * GC):
                    pool.indirect_dma_start(tables[k], bass.IndirectOffsetOnAxis(ap=cell_i[:, c:c + 1], axis=0),
                                            wsum[:, c:c + 1], None, compute_op=ALU.add).then_inc(tab_add[k], 16)
                used[k] += 1
            for t in range(NT):
                if t == 0:
                    pool.wait_ge(num_ps, NT)
                if t >= 2:
                    pool.wait_ge(out1_ps, t - 1)
                pool.wait_ge(adj_ok, t + 1)
                pool.tensor_tensor(adj_lo[:, t % 2, :], rows[t % 3][:, 0, :], adj_hi[:, t % 2, :],
                                   ALU.subtract).then_inc(adj_lo_ok, 1)
                pool.wait_ge(mix_ok, NT)
                pool.tensor_tensor(rec[:, t, :], rec[:, t, :], bias("p"), ALU.add).then_inc(bp_ok, 1)
            pool.wait_ge(bp_ok, NT)
            for t in range(NT):
                pool.wait_ge(relu_ok, t + 1)
                pool.tensor_tensor(rec[:, t, :], rec[:, t, :], upd[:, t % 2, :], ALU.add).then_inc(x1_ok, 1)
            pool.wait_ge(x1_st, 32 * NT)
            pool.wait_ge(fac_st, 16)
            pool.wait_ge(id_ok, 1)

            def gather(c):
                if c >= RING:
                    pool.wait_ge(o_ok, c - RING + 1)
                pool.indirect_dma_start(rec_c[:, c % RING, :], None, x1_rows,
                                        bass.IndirectOffsetOnAxis(ap=get_i[:, c:c + 1], axis=0)
                                        ).then_inc(ld_rec[c % RING], 16)

            for c in range(RING):
                gather(c)
            for c in range(NC):
                pool.wait_ge(o_ok, c + 1)
                pool.indirect_dma_start(out, bass.IndirectOffsetOnAxis(ap=out_i[:, c:c + 1], axis=0),
                                        o_sb[:, c % 2, :], None, bounds_check=N - 1,
                                        oob_is_err=False).then_inc(out_st[c % 2], 16)
                if c + RING < NC:
                    gather(c + RING)
            pool.wait_ge(out_st[0], 16 * ((NC + 1) // 2))
            pool.wait_ge(out_st[1], 16 * (NC // 2))

        @block.tensor
        def _(pe):
            pe.wait_ge(ld_const, 16)
            pe.wait_ge(ends_ok, 1)
            for a, ends in enumerate((cell, away)):
                for i in range(GC):
                    o = (a * GC + i) * TP
                    mm = pe.transpose(bank[5][0:NG, o:o + TP], ends[:, :].rearrange("p (g i) -> p g i", i=GC)[:, :, i],
                                      ident[0:TP, 0:TP])
            mm.then_inc(ends_ps, 1)
            pe.wait_ge(ld_const, 16)
            pe.wait_ge(top_col, 1)
            pe.transpose(bank[3][0:1, 0:TP], top[:, 0:1], ident[0:TP, 0:TP]).then_inc(top_row, 1)
            pe.wait_ge(top_val, 1)
            pe.matmul(bank[4][0:TP, 0:1], ones[0:1, 0:TP], top[0:1, 2:3], start=True, stop=True).then_inc(top_bc, 1)
            pe.wait_ge(cell_ok, 1)

            def spread(g):
                if g >= G0:
                    pe.wait_ge(same_ok, G0 + (g - G0) // 2 * 2)
                elif g >= 4:
                    pe.wait_ge(same_ok, g - 3)
                for a in range(2):
                    mm = pe.matmul(key_at(g), eye16[0:NG, a, g:g + 1].to_broadcast([NG, TP]), endsT[:, a, :],
                                   start=(a == 0), stop=(a == 1))
                mm.then_inc(cell_ps, 1)

            def totals(g):
                if g == 0:
                    pe.wait_ge(w_split, 1)
                    pe.wait_ge(top_sb, 1)
                pe.wait_ge(same_ok, g + 1)
                for j in range(GC):
                    for i in range(GC):
                        mm = pe.matmul(tot_at(g, g + 1)[:, 4 * j:4 * j + 4],
                                       same[:, g % 2, i, j * TP:(j + 1) * TP], wu[:, g * GC + i, :],
                                       start=(i == 0), stop=(i == GC - 1))
                mm.then_inc(tot_ps, 1)

            spread(0)
            spread(1)
            for g in range(G0):
                if g + 2 < G0:
                    spread(g + 2)
                totals(g)

            def x_turn(t):
                pe.wait_ge(xn_ok, t + 1)
                if t == 0:
                    pe.wait_ge(same_ok, G0)
                else:
                    pe.wait_ge(xT_lo_ok, t)
                    if t >= 3:
                        pe.wait_ge(qT_ok, t - 2)
                for k in range(KD):
                    mm = pe.transpose(bank[0][:, k * TP:(k + 1) * TP], xn[:, t % 2, k * 128:(k + 1) * 128],
                                      ident[0:TP, 0:TP])
                mm.then_inc(xT_ps, 1)

            def split_product(dst, parts):
                n = 3 * len(parts)
                for i, (ab, cd) in enumerate([(u, v) for (ah, al), (bh, bl) in parts
                                              for u, v in ((ah, bh), (ah, bl), (al, bh))]):
                    mm = pe.matmul(dst, ab, cd, start=(i == 0), stop=(i == n - 1))
                return mm

            def project(t):
                pe.wait_ge(xT_ok, t + 1)
                pe.wait_ge(xT_lo_ok, t + 1)
                if t == 0:
                    pe.wait_ge(w_hi_ok, KD)
                    pe.wait_ge(w_lo_ok, KD)
                    pe.wait_ge(lot_ok, LOTS0)
                g = G0 + TG * t
                spread(g)
                spread(g + 1)
                for b, a, n, free, done in ((3, 0, D, q_got, q_ps), (4, D, D, k_got, k_ps),
                                            (5, 2 * D, D, v_ok, v_ps), (6, 3 * D, MD, m_ok, m_ps)):
                    if t >= 1:
                        pe.wait_ge(free, t)
                    split_product(bank[b][0:TP, 0:n],
                                  [((xT_hi[:, t % 2, k, :], xT_lo[:, t % 2, k, :]),
                                    (w_hi[:, k, a:a + n], w_lo[:, k, a:a + n])) for k in range(KD)]).then_inc(done, 1)
                    if b == 3:
                        if t >= 1:
                            pe.wait_ge(m_ok, t)
                            pe.wait_ge(lot_ok, LOTS0 + t)
                        totals(g)
                        totals(g + 1)
                        spread(g + 2)
                        spread(g + 3)
                    if b == 4:
                        totals(g + 2)
                        totals(g + 3)

            def context(t):
                r = t % 2
                pe.wait_ge(soft_ok, t + 1)
                pe.wait_ge(xT_lo_ok, min(t + 3, NT))
                if t >= 1:
                    pe.wait_ge(qT_ok, t)
                for k in range(KD):
                    mm = pe.transpose(bank[0][:, k * TP:(k + 1) * TP], q_sb[:, t, k * 128:(k + 1) * 128],
                                      ident[0:TP, 0:TP])
                mm.then_inc(qT_ps, 1)
                for k in range(KD):
                    kk = k_sb[:, r, k * 128:(k + 1) * 128]
                    first, last = t == 0 and k == 0, t == NT - 1
                    mm = pe.matmul(ctx_at(k), kk, v_sb[:, r, k, :], start=first or (t == 0 and k == 3), stop=last,
                                   skip_group_check=True)
                mm.then_inc(ctx_ps, 1)

            x_turn(0)
            for t in range(NT):
                if t + 1 < NT:
                    x_turn(t + 1)
                project(t)
                if t >= 1:
                    context(t - 1)
            context(NT - 1)

            pe.wait_ge(ctx_ok, 1)
            pe.wait_ge(qT_ok, NT)

            def attend(t):
                if t >= 2:
                    pe.wait_ge(num_used, t - 1)
                for k in range(KD):
                    mm = pe.matmul(num_at(t, k // 2)[:, k % 2, :], qT[:, k, t * TP:(t + 1) * TP],
                                   ctxd[:, k, :], start=True, stop=True)
                mm.then_inc(num_ps, 1)

            def ao_turn(t):
                pe.wait_ge(ao_ok, t + 1)
                if t >= 2:
                    pe.wait_ge(aoT_lo_ok, t - 1)
                for k in range(KD):
                    mm = pe.transpose(bank[5 + t % 2][:, k * TP:(k + 1) * TP], ao[:, t % 2, k * 128:(k + 1) * 128],
                                      ident[0:TP, 0:TP])
                mm.then_inc(aoT_ps, 1)

            def mix_out(t):
                pe.wait_ge(aoT_ok, t + 1)
                if t >= 2:
                    pe.wait_ge(mix_ok, t - 1)
                pe.wait_ge(aoT_lo_ok, t + 1)
                if t == 0:
                    pe.wait_ge(wp_hi_ok, 1)
                    pe.wait_ge(wp_lo_ok, 1)
                split_product(bank[t % 2][0:TP, :],
                              [((xT_hi[:, t % 2, k, :], xT_lo[:, t % 2, k, :]),
                                (wp_hi[:, k, :], wp_lo[:, k, :])) for k in range(KD)]).then_inc(mix_ps, 1)

            pe.wait_ge(m_ok, NT)
            attend(0)
            attend(1)
            ao_turn(0)
            for t in range(NT):
                if t + 2 < NT:
                    attend(t + 2)
                if t + 1 < NT:
                    ao_turn(t + 1)
                mix_out(t)

            def adj_turn(t, part):
                n = 3 * t + part
                if n >= 2:
                    pe.wait_ge(adjT_lo_ok, n - 1)
                else:
                    pe.wait_ge(mix_ok, NT)
                lo, hi = (0, 4, 8)[part], (4, 8, 10)[part]
                for j in range(lo, hi):
                    mm = pe.transpose(bank[n % 2][0:TP, (j - lo) * TP:(j - lo + 1) * TP],
                                      rows[t % 3][:, 0, j * TP:(j + 1) * TP], ident[0:TP, 0:TP])
                mm.then_inc(adjT_ps, 1)

            def into(t, m):
                r = t % 2
                ms = slice(m * 128, (m + 1) * 128)
                for i, (a, b) in enumerate(SPANS):
                    if i < 2:
                        dst = bank[3 + 2 * m + i][:, 0:500]
                    else:
                        dst = bank[7][:, 250 * m:250 * m + 250]
                    for j, (w, v) in enumerate(((scaled_hi, adj_hi), (scaled_hi, adj_lo), (scaled_lo, adj_hi))):
                        mm = pe.matmul(dst, w[:, r, ms], v[:, r, a:b],
                                       start=(t == 0 and j == 0 and not (i == 2 and m == 1)),
                                       stop=(t == NT - 1 and j == 2), skip_group_check=True)
                if m == 1:
                    mm.then_inc(out1_ps, 1)

            def out0_turn(t):
                pe.wait_ge(out0_sb, t + 1)
                for m in range(2):
                    mm = pe.transpose(bank[2][:, MD + m * TP:MD + (m + 1) * TP], out0[:, m * 128:(m + 1) * 128],
                                      ident[0:TP, 0:TP])
                mm.then_inc(out0T_ps, 1)

            pe.wait_ge(msg_lo_ok, NT)
            for t in range(NT):
                pe.wait_ge(adj_sum, t + 1)
                adj_turn(t, 0)
                adj_turn(t, 1)
                pe.wait_ge(scaled_hi_ok, t + 1)
                pe.wait_ge(scaled_lo_ok, t + 1)
                pe.wait_ge(adj_ok, t + 1)
                pe.wait_ge(adj_lo_ok, t + 1)
                into(t, 0)
                adj_turn(t, 2)
                if t >= 1:
                    out0_turn(t - 1)
                into(t, 1)
                pe.wait_ge(adjT_ok, 3 * t + 3)
                pe.wait_ge(adjT_lo_ok, 3 * t + 3)
                if t >= 1:
                    pe.wait_ge(out0_ok, t)
                split_product(bank[2][0:TP, 0:MD],
                              [((adjT_hi[:, t % 2, j, :], adjT_lo[:, t % 2, j, :]), (msg_hi[:, j, :], msg_lo[:, j, :]))
                               for j in range(NT)]).then_inc(out0_ps, 1)
            out0_turn(NT - 1)

            pe.wait_ge(ld_small, 16)
            pe.wait_ge(adjT_lo_ok, 3 * NT)
            pe.wait_ge(out0_ok, NT)
            w1g = little("w1g").rearrange("p (k n) -> p k n", k=KD)
            for t in range(NT):
                for k in range(KD):
                    if t == 0 and k == 2:
                        pe.wait_ge(out1_ok, 6)
                    mm = pe.matmul(hid_at(t), msgT[:, k, t * TP:(t + 1) * TP], w1g[:, k, :],
                                   start=(k == 0), stop=(k == KD - 1))
                mm.then_inc(hid_ps, 1)

            ws = little("ws").rearrange("p (k e) -> p k e", k=KD)

            def hid_turn(t):
                pe.wait_ge(hn_ok, t + 1)
                if t >= 2:
                    pe.wait_ge(hidT_ok, t - 1)
                pe.transpose(bank[3 + t % 2][:, 0:TP], hid[:, t, :], ident[0:TP, 0:TP]).then_inc(hT_ps, 1)

            def hid_out(t):
                pe.wait_ge(hidT_ok, t + 1)
                if t == 0:
                    pe.wait_ge(hid_got, NT // 2)
                if t >= 2:
                    pe.wait_ge(upd_ok, t - 1)
                pe.matmul(bank[5 + t % 2][0:TP, :], hidT[:, t % 2, :], little("w2g"),
                          start=True, stop=True).then_inc(upd_ps, 1)

            def x2_turn(t):
                pe.wait_ge(x2_ok, t + 1)
                if t == 0:
                    pe.wait_ge(hid_got, NT // 2)
                if t >= 2:
                    pe.wait_ge(x2T_ok, t - 1)
                for k in range(KD):
                    mm = pe.transpose(bank[t % 2][:, k * TP:(k + 1) * TP], xn[:, t % 2, k * 128:(k + 1) * 128],
                                      ident[0:TP, 0:TP])
                mm.then_inc(x2T_ps, 1)

            def route(t):
                pe.wait_ge(x2T_ok, t + 1)
                for k in range(KD):
                    mm = pe.matmul(bank[2][0:TP, t * E:(t + 1) * E], x2T[:, k, t * TP:(t + 1) * TP], ws[:, k, :],
                                   start=(k == 0), stop=(k == KD - 1))
                mm.then_inc(log_ps, 1)

            hid_turn(0)
            for i in range(NT + 4):
                if i + 1 < NT:
                    hid_turn(i + 1)
                if i < NT:
                    hid_out(i)
                if 3 <= i < NT + 3:
                    x2_turn(i - 3)
                if i >= 4:
                    route(i - 4)
            pe.wait_ge(oh_ok, 1)
            for t in range(NT - 1):
                n = NT - 1 - t
                pe.matmul(bank[7][0:TP, (t + 1) * E:NT * E].rearrange("p (a e) -> p a e", a=n), count16[:, 0, :],
                          oh16[:, t:t + 1, :].to_broadcast([TP, n, E]), start=(t == 0), stop=False,
                          skip_group_check=True)
            pe.matmul(bank[7][0:TP, 0:NT * E], count16[:, 1, :], oh16[:, :, :].rearrange("p t e -> p (t e)"),
                      start=False, stop=True, skip_group_check=True)
            for t in range(NT):
                mm = pe.matmul(bank[5][0:TP, 0:E], count16[:, 0, :], oh16[:, t, :], start=(t == 0), stop=(t == NT - 1))
            mm.then_inc(rank_ps, 1)
            pe.wait_ge(hot_ok, 1)
            for t in range(NT):
                mm = pe.matmul(bank[6][:, 0:NC], row_hot[:, t, :], chunk_tag[:, t, :], start=(t == 0), stop=(t == NT - 1))
            mm.then_inc(ctab_ps, 1)

            def xs_turn(c):
                pe.wait_ge(xs_ok, c + 1)
                if c >= 2:
                    pe.wait_ge(xsT_ok, c - 1)
                for k in range(KD):
                    mm = pe.transpose(bank[7 * (c % 2)][:, k * CH:(k + 1) * CH], xs[:, c % 2, k * 128:(k + 1) * 128], ident)
                mm.then_inc(xsT_ps, 1)

            def up(c):
                pe.wait_ge(xsT_ok, c + 1)
                if c >= 1:
                    pe.wait_ge(h_ok, c)
                e = pe.value_load(own_i[0:1, c:c + 1], min_val=0, max_val=E - 1)
                for k in range(KD):
                    mm = pe.matmul(bank[1][:, 0:F], xsT[:, c % 2, k, :], w1_sb[:, k, bass.ds(e * F, F)],
                                   start=(k == 0), stop=(k == KD - 1))
                mm.then_inc(h_ps, 1)
                return e

            def h_turn(c):
                pe.wait_ge(h_ok, c + 1)
                if c >= 1:
                    pe.wait_ge(gelu_ok, 2 * c)
                for f in range(KF):
                    mm = pe.transpose(bank[2][:, f * CH:(f + 1) * CH], h_sb[:, c % 2, f * 128:(f + 1) * 128], ident)
                mm.then_inc(hc_ps, 1)

            def down(c, e):
                pe.wait_ge(gelu_ok, 2 * c + 2)
                if c >= 2:
                    pe.wait_ge(y_ok, c - 1)
                for f in range(KF):
                    mm = pe.matmul(bank[3 + c % 2][:, :], hT[:, c % 2, f, :], w2_sb[:, f, bass.ds(e * D, D)],
                                   start=(f == 0), stop=(f == KF - 1))
                mm.then_inc(y_ps, 1)

            pe.wait_ge(own_ok, 1)
            pe.wait_ge(ld_w1, 16)
            pe.wait_ge(ld_w2, 16)
            xs_turn(0)
            xs_turn(1)
            e = up(0)
            for c in range(NC):
                h_turn(c)
                e_next = up(c + 1) if c + 1 < NC else None
                if c + 2 < NC:
                    xs_turn(c + 2)
                down(c, e)
                e = e_next

        @block.vector
        def _(dve):
            steps = [0]

            def own_step(ins):
                ins.then_inc(v_step, 1)
                steps[0] += 1
                dve.wait_ge(v_step, steps[0])

            def pairs(a):
                return a[:, :].rearrange("p (g i) -> p g i", i=GC)

            dve.wait_ge(ld_edge, 96)
            dve.tensor_reduce(top[:, 0:1], wraw[:, :], X, ALU.max).then_inc(top_col, 1)
            dve.tensor_copy(cell[:, :], src_i[:, :])
            own_step(dve.tensor_copy(away[:, :], dst_i[:, :]))
            dve.engine_nop().then_inc(ends_ok, 1)
            dve.scalar_tensor_tensor(key[:, :], cell[:, :], float(SRCMUL), away[:, :], ALU.mult, ALU.add)
            dve.wait_ge(ld_const, 16)
            dve.tensor_scalar(eye16[:, 0, :], ident[0:TP, 0:TP], float(SRCMUL), None, ALU.mult)
            dve.tensor_copy(eye16[:, 1, :], ident[0:TP, 0:TP])
            dve.wait_ge(ends_ps, 1)
            dve.tensor_copy(endsT[:, :, :], bank[5][0:NG, 0:2 * GC * TP].rearrange("p (a q) -> p a q", a=2)
                            ).then_inc(cell_ok, 1)
            own_step(dve.scalar_tensor_tensor(cell[:, :], cell[:, :], float(N), away[:, :], ALU.mult, ALU.add))
            dve.wait_ge(top_row, 1)
            own_step(dve.tensor_reduce(top[0:1, 1:2], bank[3][0:1, 0:TP], X, ALU.max))
            dve.tensor_scalar(top[0:1, 2:3], top[0:1, 1:2], 0.0, -1.0, ALU.max, ALU.mult).then_inc(top_val, 1)
            for i in range(GC):
                last = dve.tensor_scalar(pairs(away)[:, :, i], pairs(cell)[:, :, i], -1.0,
                                         const("spare")[0:TP, i:i + 1], ALU.mult, ALU.add)
            own_step(last)
            dve.wait_ge(top_bc, 1)
            dve.tensor_copy(top[:, 3:4], bank[4][0:TP, 0:1]).then_inc(top_sb, 1)

            def compare(g):
                dve.wait_ge(cell_ps, g + 1 if g < G0 else G0 + (g - G0) // 2 * 2 + 2)
                if g >= 2:
                    dve.wait_ge(tot_ps, g - 1)
                dve.tensor_tensor(same[:, g % 2, :, :],
                                  key_at(g).unsqueeze(1).to_broadcast([TP, GC, GC * TP]),
                                  key[:, g * GC:(g + 1) * GC].unsqueeze(2).to_broadcast([TP, GC, GC * TP]),
                                  ALU.is_equal).then_inc(same_ok, 1)

            def finish_lot(i):
                g0, g1 = LOTS[i]
                a, b = g0 * GC, g1 * GC
                dve.wait_ge(tot_ps, g1)
                tv = tot_at(g0, g1).rearrange("p (c a) -> p c a", a=4)
                own_step(dve.tensor_tensor(pairs(again)[:, g0:g1, :], tv[:, :, 3].rearrange("p (g i) -> p g i", i=GC),
                                           const("limit")[0:TP, :].unsqueeze(1).to_broadcast([TP, g1 - g0, GC]),
                                           ALU.is_ge))
                dve.tensor_reduce(wsum[:, a:b], tv[:, :, 0:3], X, ALU.add)
                own_step(dve.tensor_tensor(again[:, a:b], again[:, a:b], away[:, a:b], ALU.mult))
                dve.tensor_tensor(cell_i[:, a:b], again[:, a:b], cell[:, a:b], ALU.add).then_inc(lot_ok, 1)

            def norm_stats(t):
                if t % 5 == 0:
                    dve.wait_ge(ld_x[t // 5], 32)
                dve.bn_stats(stat[:, t, :], rec[:, t, 0:D]).then_inc(stat_ok, 1)

            def norm_var(t):
                dve.wait_ge(stat_ok, t + 1)
                dve.bn_aggr(mv[:, t, :], stat[:, t, :]).then_inc(var_ok, 1)

            def split_exp():
                dve.wait_ge(w_exp, 1)
                dve.tensor_copy(wu[:, :, 3].rearrange("p (g i) -> p g i", i=GC),
                                const("rank")[0:TP, :].unsqueeze(1).to_broadcast([TP, NG, GC]))
                for i in range(3):
                    own_step(dve.tensor_copy(wu[:, :, i], wexp[:, :]))
                    if i < 2:
                        own_step(dve.tensor_tensor(wexp[:, :], wexp[:, :], wu[:, :, i], ALU.subtract))
                dve.engine_nop().then_inc(w_split, 1)

            for i, (g0, g1) in enumerate(LOTS[:LOTS0]):
                for g in range(g0, g1):
                    compare(g)
                    if g == 1:
                        split_exp()
                    n = g - STATS_FROM
                    if n >= 0 and n % 2 == 0 and n // 2 < NT:
                        norm_stats(n // 2)
                    if n >= 0 and n % 2 == 1 and n // 2 < NT:
                        norm_var(n // 2)
                finish_lot(i)

            dve.wait_ge(std_ok, 1)
            own_step(dve.reciprocal(rstd[:, :], std[:, :]))

            def norm(t):
                if t >= 2:
                    dve.wait_ge(xT_ps, t - 1)
                dve.tensor_scalar(xn[:, t % 2, :], rec[:, t, 0:D], mv[:, t, 0:1], rstd[:, t:t + 1],
                                  ALU.subtract, ALU.mult).then_inc(xn_ok, 1)

            def xT_split(t):
                dve.wait_ge(xT_ok, t + 1)
                dve.tensor_tensor(xT_lo[:, t % 2, :, :], bank[0][:, 0:KD * TP].rearrange("p (k n) -> p k n", k=KD),
                                  xT_hi[:, t % 2, :, :], ALU.subtract).then_inc(xT_lo_ok, 1)

            norm(0)
            norm(1)
            xT_split(0)
            dve.memset(v_sb[:, :, :, 128:129], 1.0)
            own_step(dve.memset(ctxd[:, :, :], 0.0))
            dve.wait_ge(ld_bias, 16)
            for t in range(NT):
                r = t % 2
                if t >= 2:
                    dve.wait_ge(ctx_ps, t - 1)
                heads = [a.rearrange("p (h d) -> p h d", d=DH) for a in (q_sb[:, t, :], k_sb[:, r, :])]

                def shift(i, b, a, ps, got):
                    dve.wait_ge(ps, t + 1)
                    dve.tensor_tensor(a, bank[3 + i][0:TP, :], bias(b), ALU.add).then_inc(got, 1)
                    dve.wait_ge(got, t + 1)
                    own_step(dve.tensor_reduce(hmax[:, i, :], heads[i], X, ALU.max))
                    dve.tensor_tensor(heads[i], heads[i], hmax[:, i, :].unsqueeze(2).to_broadcast([TP, H, DH]),
                                      ALU.subtract).then_inc(shifted, 1)

                g = G0 + TG * t
                compare(g)
                compare(g + 1)
                shift(0, "q", q_sb[:, t, :], q_ps, q_got)
                compare(g + 2)
                compare(g + 3)
                shift(1, "k", k_sb[:, r, :], k_ps, k_got)
                if t + 1 < NT:
                    xT_split(t + 1)
                if t + 2 < NT:
                    norm(t + 2)
                dve.wait_ge(v_ps, t + 1)
                dve.tensor_tensor(v_sb[:, r, :, 0:128], bank[5][0:TP, :].rearrange("p (k n) -> p k n", k=KD),
                                  bias("v").rearrange("p (k n) -> p k n", k=KD), ALU.add).then_inc(v_ok, 1)
                dve.wait_ge(m_ps, t + 1)
                dve.tensor_tensor(msg[:, t, :], bank[6][0:TP, 0:MD], bias("m"), ALU.add).then_inc(m_ok, 1)
                finish_lot(LOTS0 + t)
                for i in range(2):
                    dve.wait_ge(exp_ok, 2 * t + i + 1)
                    last = dve.tensor_reduce(hsum[:, i, :], heads[i], X, ALU.add)
                own_step(last)
                own_step(dve.reciprocal(hrec[:, :, :], hsum[:, :, :]))
                dve.wait_ge(v_ok, t + 1)
                for i in range(2):
                    last = dve.tensor_tensor(heads[i], heads[i], hrec[:, i, :].unsqueeze(2).to_broadcast([TP, H, DH]),
                                             ALU.mult)
                last.then_inc(soft_ok, 1)

            dve.wait_ge(ctx_ps, NT)
            for h in range(2):
                s = slice(64 * h, 64 * h + 64)
                got = bank[7][s, 0:387].rearrange("p (k n) -> p k n", k=3)
                dve.tensor_copy(ctxd[s, 0:3, s], got[:, :, s])
                dve.tensor_copy(ctxd[s, 0:3, 128 + h], got[:, :, 128])
                dve.tensor_copy(ctxd[s, 3, s], bank[2][s, s])
                last = dve.tensor_copy(ctxd[s, 3, 128 + h:129 + h], bank[2][s, 128:129])
            last.then_inc(ctx_ok, 1)

            dve.wait_ge(wp_hi_ok, 1)
            dve.tensor_tensor(wp_lo[:, :, :], wp_raw[:, :, :], wp_hi[:, :, :], ALU.subtract).then_inc(wp_lo_ok, 1)

            def aoT_split(t):
                dve.wait_ge(aoT_ok, t + 1)
                dve.tensor_tensor(xT_lo[:, t % 2, :, :], bank[5 + t % 2][:, 0:KD * TP].rearrange("p (k n) -> p k n", k=KD),
                                  xT_hi[:, t % 2, :, :], ALU.subtract).then_inc(aoT_lo_ok, 1)

            def msg_split(t):
                dve.wait_ge(msg_hi_ok, t + 1)
                dve.tensor_tensor(msg_lo[:, t, :], msg[:, t, :], msg_hi[:, t, :], ALU.subtract).then_inc(msg_lo_ok, 1)

            def attend(t):
                dve.wait_ge(num_ps, t + 1)
                if t >= 2:
                    dve.wait_ge(aoT_ps, t - 1)
                for half in range(2):
                    last = dve.reciprocal(rden[:, half, :, :], num_at(t, half)[:, :, 128:130])
                own_step(last)
                for half in range(2):
                    last = dve.tensor_tensor(
                        ao[:, t % 2, half * 256:(half + 1) * 256].rearrange("p (k h d) -> p k h d", k=2, h=2),
                        num_at(t, half)[:, :, 0:128].rearrange("p k (h d) -> p k h d", h=2),
                        rden[:, half, :, :].unsqueeze(3).to_broadcast([TP, 2, 2, DH]), ALU.mult)
                last.then_inc(num_used, 1)
                dve.wait_ge(num_used, t + 1)
                dve.tensor_tensor(ao[:, t % 2, :], ao[:, t % 2, :], q_sb[:, t, :], ALU.add).then_inc(ao_ok, 1)

            def mix_add(t):
                dve.wait_ge(mix_ps, t + 1)
                dve.tensor_tensor(rec[:, t, :], rec[:, t, :], bank[t % 2][0:TP, :], ALU.add).then_inc(mix_ok, 1)

            for t in range(NT):
                attend(t)
                if t >= 1:
                    aoT_split(t - 1)
                if t >= 2:
                    mix_add(t - 2)
                msg_split(t)
            aoT_split(NT - 1)

            def adj_add(t):
                rw = rows[t % 3]
                dve.wait_ge(ld_rows[t % 3], 64 * (t // 3 + 1))
                dve.scalar_tensor_tensor(rw[:, 0, :], rw[:, 0, :], 1.0, rw[:, 1, :], ALU.mult, ALU.add,
                                         accum_out=rs[:, t:t + 1]).then_inc(adj_sum, 1)
                dve.wait_ge(adj_sum, t + 1)
                dve.tensor_scalar(valid[:, t:t + 1], rs[:, t:t + 1], 0.0, None, ALU.is_gt)
                own_step(dve.tensor_scalar(rse[:, t:t + 1], rs[:, t:t + 1], 1e-6, None, ALU.add))
                dve.reciprocal(rinv[:, t:t + 1], rse[:, t:t + 1]).then_inc(rinv_ok, 1)

            adj_add(0)
            mix_add(NT - 2)
            mix_add(NT - 1)

            def scaled_split(t):
                dve.wait_ge(scaled_hi_ok, t + 1)
                dve.scalar_tensor_tensor(scaled_lo[:, t % 2, :], msg[:, t, :], rinv[:, t:t + 1], scaled_hi[:, t % 2, :],
                                         ALU.mult, ALU.subtract).then_inc(scaled_lo_ok, 1)

            def adjT_split(t, part):
                lo, hi = (0, 4, 8)[part], (4, 8, 10)[part]
                n = 3 * t + part
                dve.wait_ge(adjT_ok, n + 1)
                dve.tensor_tensor(adjT_lo[:, t % 2, lo:hi, :],
                                  bank[n % 2][0:TP, 0:(hi - lo) * TP].rearrange("p (j n) -> p j n", j=hi - lo),
                                  adjT_hi[:, t % 2, lo:hi, :], ALU.subtract).then_inc(adjT_lo_ok, 1)

            for t in range(NT):
                scaled_split(t)
                adjT_split(t, 0)
                adjT_split(t, 1)
                if t + 1 < NT:
                    adj_add(t + 1)
                adjT_split(t, 2)
            dve.wait_ge(out1_ps, NT)
            for m, a, b, bk, lo in ((0, 0, 500, 3, 0), (0, 1000, 1250, 7, 0), (1, 1000, 1250, 7, 250)):
                dve.tensor_copy(msgT[:, 2 + m, a:b], bank[bk][:, lo:lo + b - a]).then_inc(out1_ok, 1)

            def hid_norm(t0, t1, part):
                dve.wait_ge(hstd_ok, part)
                own_step(dve.reciprocal(rstd[:, t0:t1], std[:, t0:t1]))
                for t in range(t0, t1):
                    dve.tensor_scalar(hid[:, t, :], hid[:, t, :], mv[:, t, 0:1],
                                      rstd[:, t:t + 1], ALU.subtract, ALU.mult).then_inc(hn_ok, 1)

            for j in range(NT // 2):
                dve.wait_ge(hid_ps, 2 * j + 2)
                both = bank[HIDBANK[j]][0:TP, 0:2 * GH].rearrange("p (a n) -> p a n", a=2)
                dve.tensor_tensor(hid[:, 2 * j:2 * j + 2, :], both, bias("g1").unsqueeze(1).to_broadcast([TP, 2, GH]),
                                  ALU.add).then_inc(hid_got, 1)
                dve.wait_ge(hid_got, j + 1)
                for t in (2 * j, 2 * j + 1):
                    last = dve.bn_stats(stat[:, t, :], hid[:, t, :])
                own_step(last)
                for t in (2 * j, 2 * j + 1):
                    dve.bn_aggr(mv[:, t, :], stat[:, t, :]).then_inc(hvar_ok, 1)
                if j == 2:
                    hid_norm(0, HALF, 1)
            hid_norm(HALF, NT, 2)

            def upd_bias(t):
                dve.wait_ge(upd_ps, t + 1)
                if t >= 2:
                    dve.wait_ge(x1_ok, t - 1)
                dve.tensor_tensor(upd[:, t % 2, :], bank[5 + t % 2][0:TP, :], bias("g2"), ALU.add).then_inc(upd_ok, 1)

            def x1_norm(t):
                dve.wait_ge(x1_ok, t + 1)
                own_step(dve.bn_stats(stat[:, t, :], rec[:, t, :]))
                dve.wait_ge(hn_ok, NT)
                dve.bn_aggr(mv[:, t, :], stat[:, t, :]).then_inc(var2_ok, 1)
                dve.wait_ge(var2_ok, t + 1)
                if t >= 2:
                    dve.wait_ge(x2T_ps, t - 1)
                dve.tensor_scalar(xn[:, t % 2, :], rec[:, t, :], mv[:, t, 0:1], None, ALU.subtract).then_inc(x2_ok, 1)

            for t in range(NT):
                upd_bias(t)
                if t >= 2:
                    x1_norm(t - 2)
            x1_norm(NT - 2)
            x1_norm(NT - 1)

            dve.tensor_copy(count16[:, 0, :], ones[0:TP, 0:TP])
            dve.tensor_copy(count16[:, 1, :], const("before")[0:TP, :])
            dve.wait_ge(std2_ok, 1)
            own_step(dve.reciprocal(rstd[:, :], std[:, :]))
            dve.memset(factors[:, :, 3], 0.0)
            dve.tensor_copy(factors[:, :, 1], rstd[:, :])
            own_step(dve.scalar_tensor_tensor(factors[:, :, 2], mv[:, :, 0], -1.0, rstd[:, :], ALU.mult, ALU.mult))

            def over_e(a):
                return a.unsqueeze(2).to_broadcast([TP, NT, E])

            dve.wait_ge(log_ps, NT)
            own_step(dve.tensor_tensor(logit[:, :, :], bank[2][0:TP, 0:NT * E].rearrange("p (t e) -> p t e", t=NT),
                                       over_e(rstd[:, :]), ALU.mult))
            own_step(dve.tensor_tensor(logit[:, :, :], logit[:, :, :],
                                       bias("s").unsqueeze(1).to_broadcast([TP, NT, E]), ALU.add))
            own_step(dve.tensor_reduce(lmax[:, :], logit[:, :, :], X, ALU.max))
            dve.tensor_tensor(eq[:, :, :], logit[:, :, :], over_e(lmax[:, :]), ALU.is_equal)
            own_step(dve.tensor_tensor(logit[:, :, :], logit[:, :, :], over_e(lmax[:, :]), ALU.subtract))
            prefer = const("prefer")[0:TP, :].rearrange("p (t e) -> p t e", t=NT)
            dve.memset(cnt[:, 2, :], 0.0).then_inc(log_ok, 1)
            own_step(dve.tensor_tensor(eq[:, :, :], eq[:, :, :], prefer, ALU.mult))
            own_step(dve.tensor_reduce(best[:, :], eq[:, :, :], X, ALU.max))
            dve.tensor_tensor(oh16[:, :, :], prefer, over_e(best[:, :]), ALU.is_equal).then_inc(oh_ok, 1)
            dve.tensor_tensor(oh[:, :, :], prefer, over_e(best[:, :]), ALU.is_equal)
            dve.wait_ge(lexp_ok, 1)
            own_step(dve.tensor_reduce(psm[:, :], logit[:, :, :], X, ALU.add))
            dve.reciprocal(factors[:, :, 0], psm[:, :]).then_inc(fac_ok, 1)
            dve.wait_ge(rank_ps, 1)
            own_step(dve.tensor_scalar(cnt_i[:, 0, :], bank[5][0:TP, 0:E], float(CH - 1), None, ALU.add))
            own_step(dve.tensor_scalar(cnt_i[:, 1, :], cnt_i[:, 0, :], CH.bit_length() - 1, None,
                                       ALU.logical_shift_right))
            own_step(dve.tensor_copy(cnt[:, 0, :], cnt_i[:, 1, :]))
            own_step(dve.tensor_tensor_scan(cnt[:, 1, :], cnt[:, 0, :], cnt[:, 2, :], 0.0, ALU.add, ALU.add))
            own_step(dve.tensor_tensor(cnt[:, 3, :], cnt[:, 1, :], cnt[:, 0, :], ALU.subtract))
            own_step(dve.tensor_scalar(cnt[:, 3, :], cnt[:, 3, :], float(CH), None, ALU.mult))
            own_step(dve.tensor_tensor(eq[:, :, :], bank[7][0:TP, 0:NT * E].rearrange("p (t e) -> p t e", t=NT),
                                       cnt[:, 3:4, :].to_broadcast([TP, NT, E]), ALU.add))
            own_step(dve.tensor_tensor(eq[:, :, :], eq[:, :, :], oh[:, :, :], ALU.mult))
            own_step(dve.tensor_reduce(best[:, :], eq[:, :, :], X, ALU.add))
            own_step(dve.tensor_copy(pos_i[:, :], best[:, :]))
            dve.tensor_scalar(rc_i[:, 0, :], pos_i[:, :], CH - 1, None, ALU.bitwise_and)
            own_step(dve.tensor_scalar(rc_i[:, 1, :], pos_i[:, :], CH.bit_length() - 1, None, ALU.logical_shift_right))
            own_step(dve.tensor_copy(posf[:, :, :], rc_i[:, :, :]))
            dve.tensor_tensor(row_hot[:, :, :], const("cols")[0:TP, :].unsqueeze(1).to_broadcast([TP, NT, CH]),
                              posf[:, 0, :].unsqueeze(2).to_broadcast([TP, NT, CH]), ALU.is_equal)
            own_step(dve.tensor_tensor(chunk_hot[:, :, :], const("cols")[0:TP, 0:NC].unsqueeze(1).to_broadcast([TP, NT, NC]),
                                       posf[:, 1, :].unsqueeze(2).to_broadcast([TP, NT, NC]), ALU.is_equal))
            dve.tensor_tensor(chunk_tag[:, :, :], chunk_hot[:, :, :],
                              const("tag")[0:TP, :].unsqueeze(2).to_broadcast([TP, NT, NC]), ALU.mult).then_inc(hot_ok, 1)
            own_step(dve.tensor_tensor(own[:, :, :], cnt[0:1, 1:2, :].to_broadcast([1, NC, E]),
                                       const("chunk")[0:1, :].rearrange("p (c e) -> p c e", c=NC), ALU.is_le))
            own_step(dve.tensor_reduce(ownf[:, :], own[:, :, :], X, ALU.add))
            dve.tensor_scalar(own_i[:, :], ownf[:, :], float(E - 1), None, ALU.min).then_inc(own_ok, 1)
            dve.wait_ge(ctab_ps, 1)
            own_step(dve.tensor_scalar(idf[:, :], bank[6][:, 0:NC], -1.0, float(PADID), ALU.mult, ALU.add))
            dve.tensor_copy(out_i[:, :], idf[:, :])
            dve.tensor_scalar(get_i[:, :], idf[:, :], float(N - 1), None, ALU.min).then_inc(id_ok, 1)

            def h_copy(c):
                dve.wait_ge(h_ps, c + 1)
                if c >= 2:
                    dve.wait_ge(hc_ps, c - 1)
                dve.tensor_copy(h_sb[:, c % 2, :], bank[1][:, 0:F]).then_inc(h_ok, 1)

            def finish(c):
                e = dve.value_load(own_i[0:1, c:c + 1], min_val=0, max_val=E - 1)
                dve.wait_ge(y_ps, c + 1)
                dve.tensor_tensor(y_sb[:, c % 2, :], bank[3 + c % 2][:, :], b2_sb[:, bass.ds(e * D, D)],
                                  ALU.add).then_inc(y_ok, 1)
                dve.wait_ge(y_ok, c + 1)
                if c >= 2:
                    dve.wait_ge(out_st[c % 2], 16 * (c // 2))
                dve.scalar_tensor_tensor(o_sb[:, c % 2, :], y_sb[:, c % 2, :],
                                         rec_c[:, c % RING, R_P:R_P + 1], rec_c[:, c % RING, 0:D], ALU.mult, ALU.add).then_inc(o_ok, 1)

            dve.wait_ge(own_ok, 1)
            dve.wait_ge(ld_b2, 16)
            h_copy(0)
            for c in range(NC):
                if c + 1 < NC:
                    h_copy(c + 1)
                dve.wait_ge(ld_rec[c % RING], 16 * (c // RING + 1))
                finish(c)

        @block.scalar
        def _(act):
            act.wait_ge(ld_edge, 96)
            act.wait_ge(top_sb, 1)
            act.activation(wexp[:, :], wraw[:, :], ACT.Exp, bias=top[:, 3:4]).then_inc(w_exp, 1)
            for k in range(KD):
                act.wait_ge(ld_wk[k], 16)
                act.activation(w_hi[:, k, :], w_raw[:, k, :], ACT.Copy).then_inc(w_hi_ok, 1)
            act.wait_ge(var_ok, NT)
            act.activation(std[:, :], mv[:, :, 1], ACT.Sqrt, bias=const("eps")[0:TP, :]).then_inc(std_ok, 1)

            def x_copy(t):
                act.wait_ge(xT_ps, t + 1)
                if t >= 2:
                    act.wait_ge(m_ps, t - 1)
                act.activation(xT_hi[:, t % 2, :, :],
                               bank[0][:, 0:KD * TP].rearrange("p (k n) -> p k n", k=KD), ACT.Copy).then_inc(xT_ok, 1)

            def q_copy(t):
                act.wait_ge(qT_ps, t + 1)
                if t == 0:
                    act.wait_ge(w_lo_ok, KD)
                act.activation(qT[:, :, t * TP:(t + 1) * TP],
                               bank[0][:, 0:KD * TP].rearrange("p (k n) -> p k n", k=KD), ACT.Copy).then_inc(qT_ok, 1)

            x_copy(0)
            for t in range(NT):
                if t + 1 < NT:
                    x_copy(t + 1)
                for i, a in enumerate((q_sb[:, t, :], k_sb[:, t % 2, :])):
                    act.wait_ge(shifted, 2 * t + i + 1)
                    act.activation(a, a, ACT.Exp).then_inc(exp_ok, 1)
                if t >= 1:
                    q_copy(t - 1)
            q_copy(NT - 1)
            act.wait_ge(m_ps, NT)
            act.wait_ge(ld_wp, 16)
            act.activation(wp_hi[:, :, :], wp_raw[:, :, :], ACT.Copy).then_inc(wp_hi_ok, 1)
            act.wait_ge(m_ok, NT)
            for t in range(NT):
                act.activation(msg_hi[:, t, :], msg[:, t, :], ACT.Copy).then_inc(msg_hi_ok, 1)
                act.wait_ge(aoT_ps, t + 1)
                if t >= 2:
                    act.wait_ge(mix_ps, t - 1)
                act.activation(xT_hi[:, t % 2, :, :],
                               bank[5 + t % 2][:, 0:KD * TP].rearrange("p (k n) -> p k n", k=KD),
                               ACT.Copy).then_inc(aoT_ok, 1)

            def adj_high(t):
                act.wait_ge(adj_sum, t + 1)
                if t == 0:
                    act.wait_ge(num_ps, NT)
                if t >= 2:
                    act.wait_ge(out1_ps, t - 1)
                act.activation(adj_hi[:, t % 2, :], rows[t % 3][:, 0, :], ACT.Copy).then_inc(adj_ok, 1)
                act.wait_ge(rinv_ok, t + 1)
                act.activation(scaled_hi[:, t % 2, :], msg[:, t, :], ACT.Copy,
                               scale=rinv[:, t:t + 1]).then_inc(scaled_hi_ok, 1)

            def adjT_high(t, part):
                lo, hi = (0, 4, 8)[part], (4, 8, 10)[part]
                n = 3 * t + part
                act.wait_ge(adjT_ps, n + 1)
                if t == 0 and part == 0:
                    act.wait_ge(mix_ps, NT)
                if t >= 2 and part == 0:
                    act.wait_ge(out0_ps, t - 1)
                act.activation(adjT_hi[:, t % 2, lo:hi, :],
                               bank[n % 2][0:TP, 0:(hi - lo) * TP].rearrange("p (j n) -> p j n", j=hi - lo),
                               ACT.Copy).then_inc(adjT_ok, 1)

            def out0_scale(t):
                act.wait_ge(out0_ps, t + 1)
                if t >= 1:
                    act.wait_ge(out0T_ps, t)
                act.activation(out0[:, :], bank[2][0:TP, 0:MD], ACT.Copy, scale=rinv[:, t:t + 1]).then_inc(out0_sb, 1)

            def out0_copy(t):
                act.wait_ge(out0T_ps, t + 1)
                act.activation(msgT[:, 0:2, t * TP:(t + 1) * TP],
                               bank[2][:, MD:MD + 2 * TP].rearrange("p (m n) -> p m n", m=2),
                               ACT.Copy).then_inc(out0_ok, 1)

            adj_high(0)
            for t in range(NT):
                adjT_high(t, 0)
                if t >= 1:
                    out0_scale(t - 1)
                adjT_high(t, 1)
                adjT_high(t, 2)
                if t >= 1:
                    out0_copy(t - 1)
                if t + 1 < NT:
                    adj_high(t + 1)
            act.wait_ge(out1_ps, NT)
            for m, a, b, bk in ((1, 0, 500, 5), (1, 500, 1000, 6), (0, 500, 1000, 4)):
                act.activation(msgT[:, 2 + m, a:b], bank[bk][:, 0:500], ACT.Copy).then_inc(out1_ok, 1)
            out0_scale(NT - 1)
            out0_copy(NT - 1)

            def hid_std(t0, t1):
                act.wait_ge(hvar_ok, t1)
                act.activation(std[:, t0:t1], mv[:, t0:t1, 1], ACT.Sqrt, bias=const("eps")[0:TP, :]).then_inc(hstd_ok, 1)

            def hid_copy(t):
                act.wait_ge(hT_ps, t + 1)
                if t >= 2:
                    act.wait_ge(upd_ps, t - 1)
                act.activation(hidT[:, t % 2, :], bank[3 + t % 2][:, 0:TP], ACT.Relu, bias=little("beta"),
                               scale=little("gamma")).then_inc(hidT_ok, 1)

            def relu(t):
                act.wait_ge(upd_ok, t + 1)
                act.activation(upd[:, t % 2, :], upd[:, t % 2, :], ACT.Relu, scale=valid[:, t:t + 1]).then_inc(relu_ok, 1)

            def x2_copy(t):
                act.wait_ge(x2T_ps, t + 1)
                act.activation(x2T[:, :, t * TP:(t + 1) * TP],
                               bank[t % 2][:, 0:KD * TP].rearrange("p (k n) -> p k n", k=KD), ACT.Copy).then_inc(x2T_ok, 1)

            hid_std(0, HALF)
            hid_copy(0)
            hid_std(HALF, NT)
            for i in range(NT + 3):
                if i + 1 < NT:
                    hid_copy(i + 1)
                if i < NT:
                    relu(i)
                if i >= 3:
                    x2_copy(i - 3)
            act.wait_ge(var2_ok, NT)
            act.activation(std[:, :], mv[:, :, 1], ACT.Sqrt, bias=const("eps")[0:TP, :]).then_inc(std2_ok, 1)
            act.wait_ge(log_ok, 1)
            act.activation(logit[:, :, :], logit[:, :, :], ACT.Exp).then_inc(lexp_ok, 1)

            def xs_norm(c):
                act.wait_ge(ld_rec[c % RING], 16 * (c // RING + 1))
                if c >= 2:
                    act.wait_ge(xsT_ps, c - 1)
                act.activation(xs[:, c % 2, :], rec_c[:, c % RING, 0:D], ACT.Identity, bias=rec_c[:, c % RING, R_NM:R_NM + 1],
                               scale=rec_c[:, c % RING, R_RS:R_RS + 1]).then_inc(xs_ok, 1)

            def xs_copy(c):
                act.wait_ge(xsT_ps, c + 1)
                if c >= 2:
                    act.wait_ge(h_ps, c - 1)
                act.activation(xsT[:, c % 2, :, :], bank[7 * (c % 2)][:, :].rearrange("p (k n) -> p k n", k=KD),
                               ACT.Copy).then_inc(xsT_ok, 1)

            def gelu(c):
                e = act.value_load(own_i[0:1, c:c + 1], min_val=0, max_val=E - 1)
                act.wait_ge(hc_ps, c + 1)
                if c >= 2:
                    act.wait_ge(y_ps, c - 1)
                for f in range(KF):
                    b1 = little("b1").rearrange("p (f e) -> p f e", f=KF)
                    act.activation(hT[:, c % 2, f, :], bank[2][:, f * CH:(f + 1) * CH], ACT.Gelu,
                                   bias=b1[:, f, bass.ds(e, 1)]).then_inc(gelu_ok, 1)

            act.wait_ge(own_ok, 1)
            xs_norm(0)
            xs_norm(1)
            xs_copy(0)
            xs_norm(2)
            xs_copy(1)
            for c in range(NC):
                gelu(c)
                if c + 2 < NC:
                    xs_copy(c + 2)
                if c + 3 < NC:
                    xs_norm(c + 3)


def constants():
    c = np.zeros((128, CW), np.float32)
    p = np.arange(128)

    def put(name, v):
        a, w = CONSTS[name]
        c[:, a:a + w] = v

    put("ident", np.eye(128))
    put("ones", 1.0)
    put("before", p[:, None] < np.arange(TP)[None, :])
    place = np.arange(GC)[None, :] * TP + np.minimum(p, TP - 1)[:, None]
    rank = np.where(p[:, None] < TP, 2.0 ** (126.0 - place), 0.0)
    put("rank", rank)
    put("limit", 2.5 * rank)
    put("spare", SPARE + place)
    put("tag", PADID - (np.arange(NT)[None, :] * TP + p[:, None]))
    put("prefer", np.tile(E - np.arange(E), NT)[None, :])
    put("chunk", np.repeat(np.arange(NC), E)[None, :])
    put("cols", np.arange(CH)[None, :])
    put("eps", LN_EPS)
    return c


def kernel(x, src, dst, edge_weight, L0_gnn_Wm, L0_gnn_bm, L0_gnn_W1, L0_gnn_b1, L0_gnn_gamma, L0_gnn_beta,
           L0_gnn_W2, L0_gnn_b2, L0_mix_Wq, L0_mix_bq, L0_mix_Wk, L0_mix_bk, L0_mix_Wv, L0_mix_bv, L0_mix_Wp,
           L0_mix_bp, L0_ffn_Ws, L0_ffn_bs, L0_ffn_W1, L0_ffn_b1, L0_ffn_W2, L0_ffn_b2):
    import concourse.bacc as bacc
    from concourse.bass_utils import run_bass_kernel_spmd

    def arr(a):
        return np.asarray(a)

    def rows_first(w):
        return arr(w).reshape(-1, 128, w.shape[-1]).transpose(1, 0, 2)

    wqkvm = np.concatenate([rows_first(arr(w).T) for w in (L0_mix_Wq, L0_mix_Wk, L0_mix_Wv)]
                           + [rows_first(L0_gnn_Wm)], axis=2)
    biases = np.concatenate([arr(b) for b in (L0_mix_bq, L0_mix_bk, L0_mix_bv, L0_gnn_bm, L0_mix_bp, L0_gnn_b1,
                                              L0_gnn_b2, L0_ffn_bs)])
    small = np.concatenate([
        arr(L0_gnn_gamma)[:, None], arr(L0_gnn_beta)[:, None],
        arr(L0_ffn_b1).reshape(E, KF, 128).transpose(2, 1, 0).reshape(128, -1),
        rows_first(L0_ffn_Ws).reshape(128, -1), rows_first(L0_gnn_W1).reshape(128, -1), arr(L0_gnn_W2)], axis=1)
    arrays = {
        "x": arr(x), "edge_src": arr(src), "edge_dst": arr(dst), "edge_w": arr(edge_weight),
        "consts": constants(), "biases": biases, "small": small, "wqkvm": wqkvm,
        "wp": rows_first(arr(L0_mix_Wp).T),
        "w1f": arr(L0_ffn_W1).reshape(E, KD, 128, F).transpose(2, 1, 0, 3).reshape(128, KD, E * F),
        "w2f": arr(L0_ffn_W2).reshape(E, KF, 128, D).transpose(2, 1, 0, 3).reshape(128, KF, E * D),
        "b2f": arr(L0_ffn_b2).reshape(-1),
    }
    arrays = {k: np.ascontiguousarray(v) for k, v in arrays.items()}
    nc = bacc.Bacc("TRN2", target_bir_lowering=False, num_devices=1)
    args = {k: nc.dram_tensor(f"in_{k}", v.shape, mybir.dt.from_np(v.dtype), kind="ExternalInput").ap()
            for k, v in arrays.items()}
    out = nc.dram_tensor("out", (N, D), F32, kind="ExternalOutput").ap()
    build(nc, out=out, **args)
    r = run_bass_kernel_spmd(nc, [{f"in_{k}": v for k, v in arrays.items()}], core_ids=[0])
    return r.results[0]["out"]
```

```python
from contextlib import ExitStack

import numpy as np
import concourse.bass as bass
import concourse.mybir as mybir

F32 = mybir.dt.float32
I32 = mybir.dt.int32
BF16 = mybir.dt.bfloat16
F16 = mybir.dt.float16
F32R = mybir.dt.float32r
ALU = mybir.AluOpType
ACT = mybir.ActivationFunctionType
X = mybir.AxisListType.X

N, D, NE = 1250, 512, 21250
TP, NT = 125, 10
KD = D // 128
H, DH = 8, 64
MD, GH = D // 2, D // 4
E, F = 8, 256
KF = F // 128
EC = NE // TP
GC = 2
NG = EC // GC
TG = 6
G0 = NG - TG * NT
STATS_FROM = 14
NTAB = 2
PIECES = 6
TABW = 12288
SPARE = N * N
CH = 128
NC = (N + E * (CH - 1)) // CH
RING = 8
PADID = 2000
W_ROW = D + 4
R_P, R_RS, R_NM = D, D + 1, D + 2
SRCMUL = 2048
LN_EPS = 1e-5
SPANS = [(0, 500), (500, 1000), (1000, 1250)]

CONSTS, CW = {}, 0
for _n, _w in (("ident", 128), ("ones", 128), ("before", TP), ("rank", 2), ("limit", 2), ("spare", 2),
               ("tag", NT), ("prefer", NT * E), ("chunk", NC * E), ("cols", CH), ("eps", 1)):
    CONSTS[_n] = (CW, _w)
    CW += _w
BIAS, BW = {}, 0
for _n, _w in (("q", D), ("k", D), ("m", MD), ("p", D), ("g1", GH), ("g2", D), ("s", E)):
    BIAS[_n] = (BW, _w)
    BW += _w
BIAS1 = BIAS["p"][0]
SMALL, SW = {}, 0
for _n, _w in (("gamma", 1), ("beta", 1), ("b1", KF * E), ("ws", KD * E), ("w1g", KD * GH), ("w2g", D)):
    SMALL[_n] = (SW, _w)
    SW += _w

REGION = 40328
ZW = 1024
WN = 3 * D + MD

LOTS = [(0, 2), (2, 12), (12, G0)]
LOTS0 = len(LOTS)
LOTS += [(G0 + TG * t, G0 + TG * (t + 1)) for t in range(NT)]
HIDBANK = (0, 1, 2, 5, 6)
HALF = 4
KEYBANK = (0, 1, 6, 7)
ALONE = 7


def table_turns():
    return [0 if g < ALONE else (g - ALONE + 1) % NTAB for g in range(NG)]


def build(nc, x, edge_src, edge_dst, edge_w, consts, biases, small, wqkvm, wp, bvt, w1f, w2f, b2f, out):
    turns = table_turns()
    with ExitStack() as ctx:
        def sb(name, shape, dt=F32):
            return ctx.enter_context(nc.sbuf_tensor(name, shape, dt))

        def sem(name):
            return ctx.enter_context(nc.semaphore(name))

        tables = [nc.dram_tensor(f"edge_table{k}", [128 * TABW, 1], F32).ap() for k in range(NTAB)]
        x1_rows = nc.dram_tensor("x1_rows", [N, W_ROW], F32).ap()

        cst = sb("cst", [128, CW])
        bia = sb("bia", [128, BW])
        sml = sb("sml", [128, SW])
        rec_all = sb("rec", [128, NT * D])
        rec = rec_all[0:TP, :].rearrange("p (t n) -> p t n", t=NT)
        bv_col = sb("bv_col", [128, KD])
        xn = sb("xn", [TP, 2, D])

        def const(name):
            a, w = CONSTS[name]
            return cst[:, a:a + w]

        def bias(name):
            a, w = BIAS[name]
            return bia[0:TP, a:a + w]

        def little(name):
            a, w = SMALL[name]
            return sml[:, a:a + w]

        ident, ones = const("ident"), const("ones")
        base = (nc.sbuf_usable_end - 4 * REGION) // 32 * 32

        def place(name, col, shape, dt=F32):
            return nc.alloc_sbuf_tensor_at(name, shape, dt, offset=base + 4 * col)

        E0 = 35288
        src_i = place("src_i", E0, [TP, EC], I32)
        dst_i = place("dst_i", E0 + 176, [TP, EC], I32)
        wraw = place("wraw", E0 + 352, [TP, EC])
        cell = place("cell", E0 + 528, [TP, EC])
        away = place("away", E0 + 704, [TP, EC])
        again = place("again", E0 + 880, [TP, EC])
        cell_i = place("cell_i", E0 + 1056, [TP, EC], I32)
        wsum = place("wsum", E0 + 1232, [TP, EC])
        wexp = place("wexp", E0 + 1408, [TP, EC])
        key = place("key", E0 + 1584, [TP, EC])
        same = place("same", E0 + 1760, [TP, 2, GC, GC * TP], BF16)
        wu = place("wu", E0 + 2264, [TP, EC, 4], BF16)
        endsT = place("endsT", E0 + 2608, [NG, 2, GC * TP], F16)
        eye16 = place("eye16", E0 + 2864, [TP, 2, TP], F16)
        zeros = place("zeros", E0 + 2992, [128, ZW])
        w_raw = place("w_raw", 0, [128, KD, WN])
        w_hi = place("w_hi", 7168, [128, KD, WN], F32R)
        w_lo = place("w_lo", 14336, [128, KD, WN], F32R)
        q_sb = place("q_sb", 21504, [TP, NT, D])
        wp_raw = place("wp_raw", 26624, [128, KD, D])
        k_sb = place("k_sb", 28672, [TP, 2, D])
        v_sb = place("v_sb", 29696, [TP, 2, KD, 129])
        xT_hi = place("xT_hi", 30728, [128, 2, KD, TP], F32R)
        xT_lo = place("xT_lo", 31728, [128, 2, KD, TP], F32R)
        msg = place("msg", 32728, [TP, NT, MD])
        qT = place("qT", 0, [128, KD, N])
        wp_hi = place("wp_hi", 38280, [128, KD, D], F32R)
        wp_lo = place("wp_lo", 5120, [128, KD, D], F32R)
        ao = k_sb
        msg_hi = place("msg_hi", 14336, [TP, NT, MD], F32R)
        msg_lo = place("msg_lo", 16896, [TP, NT, MD], F32R)
        scaled_hi = place("scaled_hi", 19456, [TP, 2, MD], F32R)
        scaled_lo = place("scaled_lo", 19968, [TP, 2, MD], F32R)
        rows = [place(f"rows{r}", col, [TP, NTAB, N]) for r, col in enumerate((11264, 35288, 21504))]
        adj_hi = place("adj_hi", 5008, [TP, 2, N], F32R)
        adj_lo = place("adj_lo", 7512, [TP, 2, N], F32R)
        adjT_hi = place("adjT_hi", 0, [TP, 2, NT, TP], F32R)
        adjT_lo = place("adjT_lo", 2504, [TP, 2, NT, TP], F32R)
        msgT = place("msgT", 24008, [128, KD, N])
        out0 = place("out0", 20480, [TP, MD])
        hid = place("hid", 29008, [TP, NT, GH])
        hidT = place("hidT", 30288, [128, 2, TP])
        upd = place("upd", 30544, [TP, 2, D])
        w1_sb = place("w1_sb", 0, [128, KD, E * F])
        b2_sb = place("b2_sb", 8192, [128, E * D])
        w2_hi = place("w2_hi", 14336, [128, KF, E * D], F32R)
        w2_raw = place("w2_raw", 32136, [128, KF, E * D])
        w2_lo = place("w2_lo", 32136, [128, KF, E * D], F32R)
        x2T = msgT
        row_hot = place("row_hot", 13544, [TP, NT, CH], F16)
        chunk_tag = place("chunk_tag", 14184, [TP, NT, NC], F16)
        rec_c = rec_all[:, 0:RING * W_ROW].rearrange("p (r n) -> p r n", r=RING)
        logT = place("logT", 12288, [E, N])
        xs = place("xs", 24008, [128, 2, D])
        xsT = place("xsT", 25032, [128, 2, KD, CH])
        h_sb = place("h_sb", 26056, [128, 2, F])
        hT = place("hT", 26568, [128, 2, KF, CH])
        hT_hi = place("hT_hi", 27080, [128, 2, KF, CH], F32R)
        hT_lo = place("hT_lo", 27592, [128, 2, KF, CH], F32R)
        y_sb = place("y_sb", 28104, [128, 2, D])
        o_sb = place("o_sb", 29128, [128, 2, D])

        top = sb("top", [TP, 4])
        stat = sb("stat", [TP, NT, 6])
        mv = sb("mv", [TP, NT, 2])
        std = sb("std", [TP, NT])
        rstd = sb("rstd", [TP, NT])
        factors = sb("factors", [TP, NT, 4])
        hmax = sb("hmax", [TP, 2, H])
        hsum = sb("hsum", [TP, 2, H])
        hrec = sb("hrec", [TP, 2, H])
        ctxd = sb("ctxd", [128, 4, 130])
        rden = sb("rden", [TP, 2, 2, 2])
        rs = sb("rs", [TP, NT])
        rse = sb("rse", [TP, NT])
        rinv = sb("rinv", [TP, NT])
        valid = sb("valid", [TP, NT])
        logit = sb("logit", [TP, NT, E])
        eq = sb("eq", [TP, NT, E])
        oh = sb("oh", [TP, NT, E])
        oh16 = sb("oh16", [TP, NT, E], BF16)
        count16 = sb("count16", [TP, 2, TP], BF16)
        best = sb("best", [TP, NT])
        lmax = sb("lmax", [TP, NT])
        psm = sb("psm", [TP, NT])
        cnt_i = sb("cnt_i", [TP, 2, E], I32)
        cnt = sb("cnt", [TP, 4, E])
        pos_i = sb("pos_i", [TP, NT], I32)
        own = sb("own", [1, NC, E])
        ownf = sb("ownf", [1, NC])
        own_i = sb("own_i", [1, NC], I32)
        posf = sb("posf", [TP, 2, NT])
        rc_i = sb("rc_i", [TP, 2, NT], I32)
        chunk_hot = sb("chunk_hot", [TP, NT, NC])
        idf = sb("idf", [128, NC])
        out_i = sb("out_i", [128, NC], I32)
        get_i = sb("get_i", [128, NC], I32)

        bank = [ctx.enter_context(nc.psum_tensor(f"bank{i}", [128, 512], F32)) for i in range(8)]

        def hid_at(t):
            return bank[HIDBANK[t // 2]][0:TP, (t % 2) * GH:(t % 2 + 1) * GH]

        def key_at(g):
            if g < G0:
                return bank[KEYBANK[g % 4]][0:TP, 0:GC * TP]
            a = 256 * ((g - G0) % 2)
            return bank[1][0:TP, a:a + GC * TP]

        def tot_at(g0, g1):
            if g0 < G0:
                return bank[2][0:TP, 4 * GC * g0:4 * GC * g1]
            a = (g0 - G0) % TG
            return bank[6][0:TP, 256 + 4 * GC * a:256 + 4 * GC * (a + g1 - g0)]

        def logT_at(t):
            return bank[(6, 4)[t % 2]][0:E, 0:TP]

        def upd_at(t):
            return bank[(7, 5)[t % 2]][0:TP, :]

        def piece(a, i):
            half = E * D // 2
            return a[:, i // 2, i % 2 * half:(i % 2 + 1) * half]

        def ctx_at(k):
            return bank[7][:, k * 129:(k + 1) * 129] if k < 3 else bank[2][:, 0:129]

        def num_at(t, half):
            return bank[((3, 2), (4, 7))[t % 2][half]][0:TP, 0:260].rearrange("p (k n) -> p k n", k=2)

        def adjT_at(n):
            return bank[(3, 5)[n] if n < 2 else n % 2]

        ld_const, ld_edge, ld_bias, ld_small = sem("ld_const"), sem("ld_edge"), sem("ld_bias"), sem("ld_small")
        ld_x = [sem("ld_x0"), sem("ld_x1")]
        ld_wp, ld_w1, ld_b2 = sem("ld_wp"), sem("ld_w1"), sem("ld_b2")
        tab_zero = sem("tab_zero")
        ld_rows = [sem(f"ld_rows{r}") for r in range(3)]
        ld_wk = [sem(f"ld_wk{k}") for k in range(KD)]
        zero1 = [sem(f"zero1_{i}") for i in range(PIECES)]
        ld_w2k = [sem(f"ld_w2k{i}") for i in range(4)]
        w2_hi_ok, w2_lo_ok, w2_lo_ok0, hT_hi_ok, hT_lo_ok = (
            sem("w2_hi_ok"), sem("w2_lo_ok"), sem("w2_lo_ok0"), sem("hT_hi_ok"), sem("hT_lo_ok"))
        w_hi_ok, w_lo_ok, xT_lo_ok, wp_hi_ok, wp_lo_ok, aoT_lo_ok, msg_hi_ok, msg_lo_ok = (
            sem("w_hi_ok"), sem("w_lo_ok"), sem("xT_lo_ok"), sem("wp_hi_ok"), sem("wp_lo_ok"), sem("aoT_lo_ok"),
            sem("msg_hi_ok"), sem("msg_lo_ok"))
        adj_lo_ok, adjT_lo_ok, scaled_hi_ok, scaled_lo_ok, out0_sb, out0T_ps = (
            sem("adj_lo_ok"), sem("adjT_lo_ok"), sem("scaled_hi_ok"), sem("scaled_lo_ok"), sem("out0_sb"),
            sem("out0T_ps"))
        ld_rec = [sem(f"ld_rec{r}") for r in range(RING)]
        tab_add = [sem(f"tab_add{k}") for k in range(NTAB)]
        x1_st = sem("x1_st")
        out_st = [sem("out_st0"), sem("out_st1")]
        zeros_set, top_col, top_row, top_val, top_bc, top_sb, w_exp = (
            sem("zeros_set"), sem("top_col"), sem("top_row"), sem("top_val"), sem("top_bc"), sem("top_sb"), sem("w_exp"))
        w_split = sem("w_split")
        logT_ps, logT_ok = sem("logT_ps"), sem("logT_ok")
        ld_bias2 = sem("ld_bias2")
        ctxd_zero, ctx_ok1 = sem("ctxd_zero"), sem("ctx_ok1")
        row_ps, row_ok = sem("row_ps"), sem("row_ok")
        bp_ok, hid_got = sem("bp_ok"), sem("hid_got")
        ends_ok, ends_ps = sem("ends_ok"), sem("ends_ps")
        cell_ok, cell_ps, same_ok, tot_ps, lot_ok = (
            sem("cell_ok"), sem("cell_ps"), sem("same_ok"), sem("tot_ps"), sem("lot_ok"))
        stat_ok, var_ok, std_ok, xn_ok, xT_ps, xT_ok = sem("stat_ok"), sem("var_ok"), sem("std_ok"), sem("xn_ok"), sem("xT_ps"), sem("xT_ok")
        q_ps, k_ps, v_ps, m_ps = sem("q_ps"), sem("k_ps"), sem("v_ps"), sem("m_ps")
        q_got, k_got, v_ok, m_ok = sem("q_got"), sem("k_got"), sem("v_ok"), sem("m_ok")
        shifted, exp_ok, soft_ok, qT_ps, qT_ok, ctx_ps, ctx_ok = (
            sem("shifted"), sem("exp_ok"), sem("soft_ok"), sem("qT_ps"), sem("qT_ok"), sem("ctx_ps"), sem("ctx_ok"))
        num_ps, num_used, ao_ok, aoT_ps, aoT_ok, mix_ps, mix_ok = (
            sem("num_ps"), sem("num_used"), sem("ao_ok"), sem("aoT_ps"), sem("aoT_ok"),
            sem("mix_ps"), sem("mix_ok"))
        adj_sum, rinv_ok, adj_ok, adjT_ps, adjT_ok = (
            sem("adj_sum"), sem("rinv_ok"), sem("adj_ok"), sem("adjT_ps"), sem("adjT_ok"))
        out0_ps, out0_ok, out1_ps, out1_ok = (
            sem("out0_ps"), sem("out0_ok"), sem("out1_ps"), sem("out1_ok"))
        hid_ps, hvar_ok, hstd_ok, hn_ok, hT_ps, hidT_ok, upd_ps, upd_ok, relu_ok, x1_ok = (
            sem("hid_ps"), sem("hvar_ok"), sem("hstd_ok"), sem("hn_ok"), sem("hT_ps"), sem("hidT_ok"),
            sem("upd_ps"), sem("upd_ok"), sem("relu_ok"), sem("x1_ok"))
        var2_ok, std2_ok, x2_ok, x2T_ps, x2T_ok, log_ps, log_ok, lexp_ok, oh_ok, rank_ps = (
            sem("var2_ok"), sem("std2_ok"), sem("x2_ok"), sem("x2T_ps"), sem("x2T_ok"), sem("log_ps"),
            sem("log_ok"), sem("lexp_ok"), sem("oh_ok"), sem("rank_ps"))
        fac_ok, fac_st = sem("fac_ok"), sem("fac_st")
        hot_ok, ctab_ps, id_ok, own_ok = sem("hot_ok"), sem("ctab_ps"), sem("id_ok"), sem("own_ok")
        xs_ok, xsT_ps, xsT_ok, h_ps, h_ok, hc_ps, gelu_ok, y_ps, y_ok, o_ok = (
            sem("xs_ok"), sem("xsT_ps"), sem("xsT_ok"), sem("h_ps"), sem("h_ok"), sem("hc_ps"), sem("gelu_ok"),
            sem("y_ps"), sem("y_ok"), sem("o_ok"))
        v_step = sem("v_step")

        lot_of = [next(i for i, (a, b) in enumerate(LOTS) if a <= g < b) for g in range(NG)]

        def split(eng, dst, srcs, s):
            for a, b in ((0, 112), (112, TP)):
                eng.dma_start(dst(a, b), srcs(a, b)).then_inc(s, 16)

        def ctx_copies(copy, h):
            s = slice(64 * h, 64 * h + 64)
            got = bank[7][s, 0:387].rearrange("p (k n) -> p k n", k=3)
            copy(ctxd[s, 0:3, s], got[:, :, s])
            copy(ctxd[s, 0:3, 128 + h], got[:, :, 128])
            copy(ctxd[s, 3, s], bank[2][s, s])
            return copy(ctxd[s, 3, 128 + h:129 + h], bank[2][s, 128:129])

        block = ctx.enter_context(nc.Block())

        @block.sync
        def _(sp):
            def edges(v):
                return v.rearrange("(p c) -> p c", p=TP)

            split(sp, lambda a, b: src_i[a:b], lambda a, b: edges(edge_src)[a:b], ld_edge)
            split(sp, lambda a, b: dst_i[a:b], lambda a, b: edges(edge_dst)[a:b], ld_edge)
            split(sp, lambda a, b: wraw[a:b], lambda a, b: edges(edge_w)[a:b], ld_edge)
            sp.dma_start(cst[:, :], consts).then_inc(ld_const, 16)
            sp.wait_ge(zeros_set, 1)
            tab_v = [tb.rearrange("(p a n) b -> p a (n b)", p=128, n=ZW) for tb in tables]

            def zero(k, a, b, s):
                sp.dma_start(tab_v[k][:, a:b, :], zeros[:, :].unsqueeze(1).to_broadcast([128, b - a, ZW])).then_inc(s, 16)

            zero(0, 0, TABW // ZW, tab_zero)
            xv = x.rearrange("(t p) d -> p t d", p=TP)
            for h in range(2):
                t0 = 5 * h
                split(sp, lambda a, b: rec[a:b, t0:t0 + 5, :], lambda a, b: xv[a:b, t0:t0 + 5, :], ld_x[h])
            for k in range(KD):
                if k < 2:
                    sp.wait_ge(ld_x[k], 32)
                else:
                    sp.wait_ge(ld_wk[k - 2], 16)
                sp.dma_start(w_raw[:, k, :], wqkvm[:, k, :]).then_inc(ld_wk[k], 16)
            step = TABW // ZW // PIECES
            for i in range(PIECES):
                sp.wait_ge(ld_wk[2 + i] if i < 2 else zero1[i - 2], 16)
                zero(1, i * step, (i + 1) * step, zero1[i])
                if i == 0:
                    sp.dma_start(bia[:, 0:BIAS1], biases[0:BIAS1].partition_broadcast(128)).then_inc(ld_bias, 16)
            sp.wait_ge(zero1[PIECES - 2], 16)
            sp.dma_start(bia[:, BIAS1:BW], biases[BIAS1:BW].partition_broadcast(128)).then_inc(ld_bias2, 16)
            sp.wait_ge(zero1[PIECES - 1], 16)
            sp.dma_start(wp_raw[:, :, :], wp).then_inc(ld_wp, 16)
            sp.dma_start(bv_col[:, :], bvt).then_inc(ld_wp, 16)
            views = [tb[0:N * N, :].rearrange("(t p n) b -> p t (n b)", p=TP, t=NT) for tb in tables]
            for t in range(NT):
                r = t % 3
                if t == 0:
                    sp.wait_ge(m_ps, NT)
                if t == 2:
                    sp.wait_ge(ao_ok, NT)
                if t >= 3:
                    sp.wait_ge(adj_lo_ok, t - 2)
                    sp.wait_ge(adjT_ps, 3 * (t - 2))
                for k in (1 - turns[-1], turns[-1]):
                    if t == 0:
                        sp.wait_ge(tab_add[k], 16 * GC * turns.count(k))
                    split(sp, lambda a, b: rows[r][a:b, k, :], lambda a, b: views[k][a:b, t, :], ld_rows[r])
                if t == 2:
                    sp.dma_start(sml[:, :], small).then_inc(ld_small, 16)
            sp.wait_ge(out1_ps, NT)
            sp.wait_ge(out0_ps, NT)
            for i in range(4):
                sp.dma_start(piece(w2_raw, i), piece(w2f, i)).then_inc(ld_w2k[i], 16)
            sp.dma_start(w1_sb[:, :, :], w1f).then_inc(ld_w1, 16)
            sp.dma_start(b2_sb[:, :], b2f.partition_broadcast(128)).then_inc(ld_b2, 16)
            for t in range(NT):
                sp.wait_ge(x1_ok, t + 1)
                split(sp, lambda a, b: x1_rows[t * TP + a:t * TP + b, 0:D], lambda a, b: rec[a:b, t, :], x1_st)
            sp.wait_ge(fac_ok, 1)
            sp.dma_start(x1_rows.rearrange("(t p) n -> p t n", p=TP)[:, :, D:W_ROW],
                         factors[:, :, :]).then_inc(fac_st, 16)

        @block.gpsimd
        def _(pool):
            pool.memset(zeros[:, :], 0.0).then_inc(zeros_set, 1)
            used = [0] * NTAB
            for g, k in enumerate(turns):
                if g == 0 or lot_of[g] != lot_of[g - 1]:
                    pool.wait_ge(lot_ok, lot_of[g] + 1)
                if used[k]:
                    pool.wait_ge(tab_add[k], 16 * GC * used[k])
                elif k == 0:
                    pool.wait_ge(tab_zero, 16)
                else:
                    for z in zero1:
                        pool.wait_ge(z, 16)
                for c in range(g * GC, (g + 1) * GC):
                    pool.indirect_dma_start(tables[k], bass.IndirectOffsetOnAxis(ap=cell_i[:, c:c + 1], axis=0),
                                            wsum[:, c:c + 1], None, compute_op=ALU.add).then_inc(tab_add[k], 16)
                used[k] += 1
            for t in range(NT):
                if t == 0:
                    pool.wait_ge(m_ps, NT)
                if t >= 2:
                    pool.wait_ge(out1_ps, t - 1)
                pool.wait_ge(adj_ok, t + 1)
                pool.tensor_tensor(adj_lo[:, t % 2, :], rows[t % 3][:, 0, :], adj_hi[:, t % 2, :],
                                   ALU.subtract).then_inc(adj_lo_ok, 1)
                pool.wait_ge(mix_ok, NT)
                pool.tensor_tensor(rec[:, t, :], rec[:, t, :], bias("p"), ALU.add).then_inc(bp_ok, 1)
            pool.wait_ge(bp_ok, NT)
            for t in range(NT):
                pool.wait_ge(relu_ok, t + 1)
                pool.tensor_tensor(rec[:, t, :], rec[:, t, :], upd[:, t % 2, :], ALU.add).then_inc(x1_ok, 1)
            pool.wait_ge(w2_hi_ok, 1)
            pool.tensor_tensor(piece(w2_lo, 0), piece(w2_raw, 0), piece(w2_hi, 0), ALU.subtract).then_inc(w2_lo_ok0, 1)
            pool.wait_ge(x1_st, 32 * NT)
            pool.wait_ge(fac_st, 16)
            pool.wait_ge(id_ok, 1)

            def gather(c):
                if c >= RING:
                    pool.wait_ge(o_ok, c - RING + 1)
                pool.indirect_dma_start(rec_c[:, c % RING, :], None, x1_rows,
                                        bass.IndirectOffsetOnAxis(ap=get_i[:, c:c + 1], axis=0)
                                        ).then_inc(ld_rec[c % RING], 16)

            for c in range(RING):
                gather(c)
            for c in range(NC):
                pool.wait_ge(o_ok, c + 1)
                pool.indirect_dma_start(out, bass.IndirectOffsetOnAxis(ap=out_i[:, c:c + 1], axis=0),
                                        o_sb[:, c % 2, :], None, bounds_check=N - 1,
                                        oob_is_err=False).then_inc(out_st[c % 2], 16)
                if c + RING < NC:
                    gather(c + RING)
            pool.wait_ge(out_st[0], 16 * ((NC + 1) // 2))
            pool.wait_ge(out_st[1], 16 * (NC // 2))

        @block.tensor
        def _(pe):
            pe.wait_ge(ld_const, 16)
            pe.wait_ge(ends_ok, 1)
            for a, ends in enumerate((cell, away)):
                for i in range(GC):
                    o = (a * GC + i) * TP
                    mm = pe.transpose(bank[5][0:NG, o:o + TP], ends[:, :].rearrange("p (g i) -> p g i", i=GC)[:, :, i],
                                      ident[0:TP, 0:TP])
            mm.then_inc(ends_ps, 1)
            pe.wait_ge(ld_const, 16)
            pe.wait_ge(top_col, 1)
            pe.transpose(bank[3][0:1, 0:TP], top[:, 0:1], ident[0:TP, 0:TP]).then_inc(top_row, 1)
            pe.wait_ge(top_val, 1)
            pe.matmul(bank[4][0:TP, 0:1], ones[0:1, 0:TP], top[0:1, 2:3], start=True, stop=True).then_inc(top_bc, 1)
            pe.wait_ge(cell_ok, 1)

            def spread(g):
                if g >= G0:
                    pe.wait_ge(same_ok, G0 + (g - G0) // 2 * 2)
                elif g >= 4:
                    pe.wait_ge(same_ok, g - 3)
                for a in range(2):
                    mm = pe.matmul(key_at(g), eye16[0:NG, a, g:g + 1].to_broadcast([NG, TP]), endsT[:, a, :],
                                   start=(a == 0), stop=(a == 1))
                mm.then_inc(cell_ps, 1)

            def totals(g):
                if g == 0:
                    pe.wait_ge(w_split, 1)
                    pe.wait_ge(top_sb, 1)
                pe.wait_ge(same_ok, g + 1)
                for j in range(GC):
                    for i in range(GC):
                        mm = pe.matmul(tot_at(g, g + 1)[:, 4 * j:4 * j + 4],
                                       same[:, g % 2, i, j * TP:(j + 1) * TP], wu[:, g * GC + i, :],
                                       start=(i == 0), stop=(i == GC - 1))
                mm.then_inc(tot_ps, 1)

            spread(0)
            spread(1)
            for g in range(G0):
                if g + 2 < G0:
                    spread(g + 2)
                totals(g)

            def x_turn(t):
                pe.wait_ge(xn_ok, t + 1)
                if t == 0:
                    pe.wait_ge(same_ok, G0)
                else:
                    pe.wait_ge(xT_lo_ok, t)
                    if t >= 3:
                        pe.wait_ge(qT_ok, t - 2)
                for k in range(KD):
                    mm = pe.transpose(bank[0][:, k * TP:(k + 1) * TP], xn[:, t % 2, k * 128:(k + 1) * 128],
                                      ident[0:TP, 0:TP])
                mm.then_inc(xT_ps, 1)

            def split_product(dst, parts):
                n = 3 * len(parts)
                for i, (ab, cd) in enumerate([(u, v) for (ah, al), (bh, bl) in parts
                                              for u, v in ((ah, bh), (ah, bl), (al, bh))]):
                    mm = pe.matmul(dst, ab, cd, start=(i == 0), stop=(i == n - 1))
                return mm

            def project(t):
                pe.wait_ge(xT_ok, t + 1)
                pe.wait_ge(xT_lo_ok, t + 1)
                if t == 0:
                    pe.wait_ge(w_hi_ok, KD)
                    pe.wait_ge(w_lo_ok, KD)
                    pe.wait_ge(lot_ok, LOTS0)
                g = G0 + TG * t
                spread(g)
                spread(g + 1)
                for b, a, n, free, done in ((3, 0, D, q_got, q_ps), (4, D, D, k_got, k_ps),
                                            (5, 2 * D, D, v_ok, v_ps), (6, 3 * D, MD, m_ok, m_ps)):
                    if t >= 1:
                        pe.wait_ge(free, t)
                    split_product(bank[b][0:TP, 0:n],
                                  [((xT_hi[:, t % 2, k, :], xT_lo[:, t % 2, k, :]),
                                    (w_hi[:, k, a:a + n], w_lo[:, k, a:a + n])) for k in range(KD)]).then_inc(done, 1)
                    if b == 3:
                        if t >= 1:
                            pe.wait_ge(m_ok, t)
                            pe.wait_ge(lot_ok, LOTS0 + t)
                        totals(g)
                        totals(g + 1)
                        spread(g + 2)
                        spread(g + 3)
                    if b == 4:
                        totals(g + 2)
                        totals(g + 3)
                        spread(g + 4)
                        spread(g + 5)
                    if b == 5:
                        totals(g + 4)
                        totals(g + 5)

            def context(t):
                r = t % 2
                pe.wait_ge(soft_ok, t + 1)
                pe.wait_ge(v_ok, t + 1)
                pe.wait_ge(xT_lo_ok, min(t + 3, NT))
                if t >= 1:
                    pe.wait_ge(qT_ok, t)
                for k in range(KD):
                    mm = pe.transpose(bank[0][:, k * TP:(k + 1) * TP], q_sb[:, t, k * 128:(k + 1) * 128],
                                      ident[0:TP, 0:TP])
                mm.then_inc(qT_ps, 1)
                for k in range(KD):
                    kk = k_sb[:, r, k * 128:(k + 1) * 128]
                    first, last = t == 0 and k == 0, t == NT - 1
                    mm = pe.matmul(ctx_at(k), kk, v_sb[:, r, k, :], start=first or (t == 0 and k == 3), stop=last,
                                   skip_group_check=True)
                mm.then_inc(ctx_ps, 1)

            x_turn(0)
            for t in range(NT):
                if t + 1 < NT:
                    x_turn(t + 1)
                project(t)
                if t >= 1:
                    context(t - 1)
            pe.wait_ge(ld_wp, 32)
            pe.wait_ge(m_ok, NT)
            pe.wait_ge(lot_ok, len(LOTS))
            def bias_row(k):
                return pe.matmul(bank[6][0:TP, :], bv_col[:, k:k + 1].to_broadcast([128, TP]), wp_raw[:, k, :],
                                 start=(k == 0), stop=(k == KD - 1))

            bias_row(0)
            bias_row(1)
            context(NT - 1)

            pe.wait_ge(ctx_ok, 1)
            pe.wait_ge(ctx_ok1, 1)
            pe.wait_ge(qT_ok, NT)

            def attend(t):
                if t >= 2:
                    pe.wait_ge(num_used, t - 1)
                for k in range(KD):
                    mm = pe.matmul(num_at(t, k // 2)[:, k % 2, :], qT[:, k, t * TP:(t + 1) * TP],
                                   ctxd[:, k, :], start=True, stop=True)
                mm.then_inc(num_ps, 1)

            def ao_turn(t):
                pe.wait_ge(ao_ok, t + 1)
                if t == 1:
                    pe.wait_ge(row_ok, 1)
                if t >= 2:
                    pe.wait_ge(aoT_lo_ok, t - 1)
                for k in range(KD):
                    mm = pe.transpose(bank[5 + t % 2][:, k * TP:(k + 1) * TP], ao[:, t % 2, k * 128:(k + 1) * 128],
                                      ident[0:TP, 0:TP])
                mm.then_inc(aoT_ps, 1)

            def mix_out(t):
                pe.wait_ge(aoT_ok, t + 1)
                if t >= 2:
                    pe.wait_ge(mix_ok, t - 1)
                pe.wait_ge(aoT_lo_ok, t + 1)
                if t == 0:
                    pe.wait_ge(wp_hi_ok, 1)
                    pe.wait_ge(wp_lo_ok, KD)
                split_product(bank[t % 2][0:TP, :],
                              [((xT_hi[:, t % 2, k, :], xT_lo[:, t % 2, k, :]),
                                (wp_hi[:, k, :], wp_lo[:, k, :])) for k in range(KD)]).then_inc(mix_ps, 1)

            def adj_turn(t, part):
                n = 3 * t + part
                if n == 0:
                    pe.wait_ge(num_used, NT - 1)
                elif n == 1:
                    pe.wait_ge(aoT_lo_ok, NT - 1)
                elif n <= 3:
                    pe.wait_ge(mix_ok, NT - 3 + n)
                else:
                    pe.wait_ge(adjT_lo_ok, n - 1)
                lo, hi = (0, 4, 8)[part], (4, 8, 10)[part]
                for j in range(lo, hi):
                    mm = pe.transpose(adjT_at(n)[0:TP, (j - lo) * TP:(j - lo + 1) * TP],
                                      rows[t % 3][:, 0, j * TP:(j + 1) * TP], ident[0:TP, 0:TP])
                mm.then_inc(adjT_ps, 1)

            pe.wait_ge(m_ok, NT)
            attend(0)
            attend(1)
            bias_row(2)
            bias_row(3).then_inc(row_ps, 1)
            ao_turn(0)
            for t in range(NT):
                if t + 2 < NT:
                    attend(t + 2)
                if t + 1 < NT:
                    ao_turn(t + 1)
                else:
                    pe.wait_ge(adj_sum, 1)
                    adj_turn(0, 0)
                    adj_turn(0, 1)
                mix_out(t)

            def into(t, m):
                r = t % 2
                ms = slice(m * 128, (m + 1) * 128)
                for i, (a, b) in enumerate(SPANS):
                    if i < 2:
                        dst = bank[3 + 2 * m + i][:, 0:500]
                    else:
                        dst = bank[7][:, 250 * m:250 * m + 250]
                    for j, (w, v) in enumerate(((scaled_hi, adj_hi), (scaled_hi, adj_lo), (scaled_lo, adj_hi))):
                        mm = pe.matmul(dst, w[:, r, ms], v[:, r, a:b],
                                       start=(t == 0 and j == 0 and not (i == 2 and m == 1)),
                                       stop=(t == NT - 1 and j == 2), skip_group_check=True)
                if m == 1:
                    mm.then_inc(out1_ps, 1)

            def out0_turn(t):
                pe.wait_ge(out0_sb, t + 1)
                for m in range(2):
                    mm = pe.transpose(bank[2][:, MD + m * TP:MD + (m + 1) * TP], out0[:, m * 128:(m + 1) * 128],
                                      ident[0:TP, 0:TP])
                mm.then_inc(out0T_ps, 1)

            def outward(t):
                pe.wait_ge(adjT_ok, 3 * t + 3)
                pe.wait_ge(adjT_lo_ok, 3 * t + 3)
                if t >= 1:
                    pe.wait_ge(out0_ok, t)
                split_product(bank[2][0:TP, 0:MD],
                              [((adjT_hi[:, t % 2, j, :], adjT_lo[:, t % 2, j, :]), (msg_hi[:, j, :], msg_lo[:, j, :]))
                               for j in range(NT)]).then_inc(out0_ps, 1)

            pe.wait_ge(msg_lo_ok, NT)
            for t in range(NT):
                if t >= 1:
                    pe.wait_ge(adj_sum, t + 1)
                    adj_turn(t, 0)
                    adj_turn(t, 1)
                if t == 0:
                    adj_turn(t, 2)
                    outward(t)
                pe.wait_ge(scaled_hi_ok, t + 1)
                pe.wait_ge(scaled_lo_ok, t + 1)
                pe.wait_ge(adj_ok, t + 1)
                pe.wait_ge(adj_lo_ok, t + 1)
                into(t, 0)
                if t >= 1:
                    adj_turn(t, 2)
                    out0_turn(t - 1)
                into(t, 1)
                if t >= 1:
                    outward(t)
            out0_turn(NT - 1)

            pe.wait_ge(ld_small, 16)
            pe.wait_ge(adjT_lo_ok, 3 * NT)
            pe.wait_ge(out0_ok, NT)
            w1g = little("w1g").rearrange("p (k n) -> p k n", k=KD)

            def hidden(t):
                for k in range(KD):
                    if t == 0 and k == 2:
                        pe.wait_ge(out1_ok, 6)
                    mm = pe.matmul(hid_at(t), msgT[:, k, t * TP:(t + 1) * TP], w1g[:, k, :],
                                   start=(k == 0), stop=(k == KD - 1))
                mm.then_inc(hid_ps, 1)

            ws = little("ws").rearrange("p (k e) -> p k e", k=KD)

            def hid_turn(t):
                pe.wait_ge(hn_ok, t + 1)
                if t >= 1:
                    pe.wait_ge(hidT_ok, t)
                pe.transpose(bank[3][:, 0:TP], hid[:, t, :], ident[0:TP, 0:TP]).then_inc(hT_ps, 1)

            def hid_out(t):
                pe.wait_ge(hidT_ok, t + 1)
                if t == 1:
                    pe.wait_ge(hid_got, 4)
                if t >= 2:
                    pe.wait_ge(upd_ok, t - 1)
                pe.matmul(upd_at(t), hidT[:, t % 2, :], little("w2g"),
                          start=True, stop=True).then_inc(upd_ps, 1)

            def x2_turn(t):
                pe.wait_ge(x2_ok, t + 1)
                if t == 0:
                    pe.wait_ge(hid_got, NT // 2)
                if t >= 2:
                    pe.wait_ge(x2T_ok, t - 1)
                for k in range(KD):
                    mm = pe.transpose(bank[t % 2][:, k * TP:(k + 1) * TP], xn[:, t % 2, k * 128:(k + 1) * 128],
                                      ident[0:TP, 0:TP])
                mm.then_inc(x2T_ps, 1)

            def route(t):
                pe.wait_ge(x2T_ok, t + 1)
                if t >= 2:
                    pe.wait_ge(logT_ok, t - 1)
                for k in range(KD):
                    mm = pe.matmul(logT_at(t), ws[:, k, :], x2T[:, k, t * TP:(t + 1) * TP],
                                   start=(k == 0), stop=(k == KD - 1))
                mm.then_inc(logT_ps, 1)

            def route_turn(t):
                pe.wait_ge(logT_ok, t + 1)
                pe.transpose(bank[2][0:TP, t * E:(t + 1) * E], logT[:, t * TP:(t + 1) * TP], ident[0:E, 0:E]
                             ).then_inc(log_ps, 1)

            for t in range(NT):
                hidden(t)
                if t == HALF + 2:
                    hid_turn(0)
                if t == NT - 2:
                    hid_turn(1)
                    hid_out(0)
            for i in range(1, NT + 5):
                if i + 1 < NT:
                    hid_turn(i + 1)
                if i < NT:
                    hid_out(i)
                if 3 <= i < NT + 3:
                    x2_turn(i - 3)
                if 4 <= i < NT + 4:
                    route(i - 4)
                if i >= 5:
                    route_turn(i - 5)
            pe.wait_ge(oh_ok, 1)
            for t in range(NT):
                n = NT - t
                mm = pe.matmul(bank[7][0:TP, (t + 1) * E:(NT + 1) * E].rearrange("p (a e) -> p a e", a=n),
                               count16[:, 0, :], oh16[:, t:t + 1, :].to_broadcast([TP, n, E]), start=(t == 0),
                               stop=False, skip_group_check=True)
            mm = pe.matmul(bank[7][0:TP, 0:NT * E], count16[:, 1, :], oh16[:, :, :].rearrange("p t e -> p (t e)"),
                           start=False, stop=True, skip_group_check=True)
            mm.then_inc(rank_ps, 1)
            pe.wait_ge(hot_ok, 1)
            for t in range(NT):
                mm = pe.matmul(bank[6][:, 0:NC], row_hot[:, t, :], chunk_tag[:, t, :], start=(t == 0), stop=(t == NT - 1))
            mm.then_inc(ctab_ps, 1)

            def xs_turn(c):
                pe.wait_ge(xs_ok, c + 1)
                if c >= 2:
                    pe.wait_ge(xsT_ok, c - 1)
                for k in range(KD):
                    mm = pe.transpose(bank[7 * (c % 2)][:, k * CH:(k + 1) * CH], xs[:, c % 2, k * 128:(k + 1) * 128], ident)
                mm.then_inc(xsT_ps, 1)

            def up(c):
                pe.wait_ge(xsT_ok, c + 1)
                if c >= 1:
                    pe.wait_ge(h_ok, c)
                e = pe.value_load(own_i[0:1, c:c + 1], min_val=0, max_val=E - 1)
                for k in range(KD):
                    mm = pe.matmul(bank[1][:, 0:F], xsT[:, c % 2, k, :], w1_sb[:, k, bass.ds(e * F, F)],
                                   start=(k == 0), stop=(k == KD - 1))
                mm.then_inc(h_ps, 1)
                return e

            def h_turn(c):
                pe.wait_ge(h_ok, c + 1)
                if c >= 1:
                    pe.wait_ge(gelu_ok, 2 * c)
                for f in range(KF):
                    mm = pe.transpose(bank[2][:, f * CH:(f + 1) * CH], h_sb[:, c % 2, f * 128:(f + 1) * 128], ident)
                mm.then_inc(hc_ps, 1)

            def down(c, e):
                pe.wait_ge(hT_lo_ok, c + 1)
                if c == 0:
                    pe.wait_ge(w2_hi_ok, 4)
                    pe.wait_ge(w2_lo_ok0, 1)
                    pe.wait_ge(w2_lo_ok, 3)
                if c >= 2:
                    pe.wait_ge(y_ok, c - 1)
                split_product(bank[3 + c % 2][:, :],
                              [((hT_hi[:, c % 2, f, :], hT_lo[:, c % 2, f, :]),
                                (w2_hi[:, f, bass.ds(e * D, D)], w2_lo[:, f, bass.ds(e * D, D)]))
                               for f in range(KF)]).then_inc(y_ps, 1)

            pe.wait_ge(own_ok, 1)
            pe.wait_ge(ld_w1, 16)
            xs_turn(0)
            xs_turn(1)
            e = up(0)
            for c in range(NC):
                h_turn(c)
                e_next = up(c + 1) if c + 1 < NC else None
                if c + 2 < NC:
                    xs_turn(c + 2)
                down(c, e)
                e = e_next

        @block.vector
        def _(dve):
            steps = [0]

            def own_step(ins):
                ins.then_inc(v_step, 1)
                steps[0] += 1
                dve.wait_ge(v_step, steps[0])

            def pairs(a):
                return a[:, :].rearrange("p (g i) -> p g i", i=GC)

            dve.wait_ge(ld_edge, 96)
            dve.tensor_reduce(top[:, 0:1], wraw[:, :], X, ALU.max).then_inc(top_col, 1)
            dve.tensor_copy(cell[:, :], src_i[:, :])
            own_step(dve.tensor_copy(away[:, :], dst_i[:, :]))
            dve.engine_nop().then_inc(ends_ok, 1)
            dve.scalar_tensor_tensor(key[:, :], cell[:, :], float(SRCMUL), away[:, :], ALU.mult, ALU.add)
            dve.wait_ge(ld_const, 16)
            dve.tensor_scalar(eye16[:, 0, :], ident[0:TP, 0:TP], float(SRCMUL), None, ALU.mult)
            dve.tensor_copy(eye16[:, 1, :], ident[0:TP, 0:TP])
            dve.wait_ge(ends_ps, 1)
            dve.tensor_copy(endsT[:, :, :], bank[5][0:NG, 0:2 * GC * TP].rearrange("p (a q) -> p a q", a=2)
                            ).then_inc(cell_ok, 1)
            own_step(dve.scalar_tensor_tensor(cell[:, :], cell[:, :], float(N), away[:, :], ALU.mult, ALU.add))
            dve.wait_ge(top_row, 1)
            own_step(dve.tensor_reduce(top[0:1, 1:2], bank[3][0:1, 0:TP], X, ALU.max))
            dve.tensor_scalar(top[0:1, 2:3], top[0:1, 1:2], 0.0, -1.0, ALU.max, ALU.mult).then_inc(top_val, 1)
            for i in range(GC):
                last = dve.tensor_scalar(pairs(away)[:, :, i], pairs(cell)[:, :, i], -1.0,
                                         const("spare")[0:TP, i:i + 1], ALU.mult, ALU.add)
            own_step(last)
            dve.wait_ge(top_bc, 1)
            dve.tensor_copy(top[:, 3:4], bank[4][0:TP, 0:1]).then_inc(top_sb, 1)

            def compare(g):
                dve.wait_ge(cell_ps, g + 1 if g < G0 else G0 + (g - G0) // 2 * 2 + 2)
                if g >= 2:
                    dve.wait_ge(tot_ps, g - 1)
                dve.tensor_tensor(same[:, g % 2, :, :],
                                  key_at(g).unsqueeze(1).to_broadcast([TP, GC, GC * TP]),
                                  key[:, g * GC:(g + 1) * GC].unsqueeze(2).to_broadcast([TP, GC, GC * TP]),
                                  ALU.is_equal).then_inc(same_ok, 1)

            def finish_lot(i):
                g0, g1 = LOTS[i]
                a, b = g0 * GC, g1 * GC
                dve.wait_ge(tot_ps, g1)
                tv = tot_at(g0, g1).rearrange("p (c a) -> p c a", a=4)
                own_step(dve.tensor_tensor(pairs(again)[:, g0:g1, :], tv[:, :, 3].rearrange("p (g i) -> p g i", i=GC),
                                           const("limit")[0:TP, :].unsqueeze(1).to_broadcast([TP, g1 - g0, GC]),
                                           ALU.is_ge))
                dve.tensor_reduce(wsum[:, a:b], tv[:, :, 0:3], X, ALU.add)
                own_step(dve.tensor_tensor(again[:, a:b], again[:, a:b], away[:, a:b], ALU.mult))
                dve.tensor_tensor(cell_i[:, a:b], again[:, a:b], cell[:, a:b], ALU.add).then_inc(lot_ok, 1)

            def norm_stats(t):
                if t % 5 == 0:
                    dve.wait_ge(ld_x[t // 5], 32)
                dve.bn_stats(stat[:, t, :], rec[:, t, 0:D]).then_inc(stat_ok, 1)

            def norm_var(t):
                dve.wait_ge(stat_ok, t + 1)
                dve.bn_aggr(mv[:, t, :], stat[:, t, :]).then_inc(var_ok, 1)

            def split_exp():
                dve.wait_ge(w_exp, 1)
                dve.tensor_copy(wu[:, :, 3].rearrange("p (g i) -> p g i", i=GC),
                                const("rank")[0:TP, :].unsqueeze(1).to_broadcast([TP, NG, GC]))
                for i in range(3):
                    own_step(dve.tensor_copy(wu[:, :, i], wexp[:, :]))
                    if i < 2:
                        own_step(dve.tensor_tensor(wexp[:, :], wexp[:, :], wu[:, :, i], ALU.subtract))
                dve.engine_nop().then_inc(w_split, 1)

            for i, (g0, g1) in enumerate(LOTS[:LOTS0]):
                for g in range(g0, g1):
                    compare(g)
                    if g == 1:
                        split_exp()
                    n = g - STATS_FROM
                    if 0 <= n < NT:
                        norm_stats(n)
                    if 1 <= n < NT + 1:
                        norm_var(n - 1)
                    n = g - (G0 - KD)
                    if n >= 0:
                        dve.wait_ge(w_hi_ok, n + 1)
                        dve.tensor_tensor(w_lo[:, n, :], w_raw[:, n, :], w_hi[:, n, :], ALU.subtract).then_inc(w_lo_ok, 1)
                finish_lot(i)

            dve.wait_ge(std_ok, 1)
            own_step(dve.reciprocal(rstd[:, :], std[:, :]))

            def norm(t):
                if t >= 2:
                    dve.wait_ge(xT_ps, t - 1)
                dve.tensor_scalar(xn[:, t % 2, :], rec[:, t, 0:D], mv[:, t, 0:1], rstd[:, t:t + 1],
                                  ALU.subtract, ALU.mult).then_inc(xn_ok, 1)

            def xT_split(t):
                dve.wait_ge(xT_ok, t + 1)
                dve.tensor_tensor(xT_lo[:, t % 2, :, :], bank[0][:, 0:KD * TP].rearrange("p (k n) -> p k n", k=KD),
                                  xT_hi[:, t % 2, :, :], ALU.subtract).then_inc(xT_lo_ok, 1)

            norm(0)
            norm(1)
            xT_split(0)
            dve.memset(v_sb[:, :, :, 128:129], 1.0)
            own_step(dve.memset(ctxd[:, :, :], 0.0))
            dve.engine_nop().then_inc(ctxd_zero, 1)
            dve.wait_ge(ld_bias, 16)
            for t in range(NT):
                r = t % 2
                if t >= 2:
                    dve.wait_ge(ctx_ps, t - 1)
                heads = [a.rearrange("p (h d) -> p h d", d=DH) for a in (q_sb[:, t, :], k_sb[:, r, :])]

                def shift(i, b, a, ps, got):
                    dve.wait_ge(ps, t + 1)
                    dve.tensor_tensor(a, bank[3 + i][0:TP, :], bias(b), ALU.add).then_inc(got, 1)
                    dve.wait_ge(got, t + 1)
                    own_step(dve.tensor_reduce(hmax[:, i, :], heads[i], X, ALU.max))
                    dve.tensor_tensor(heads[i], heads[i], hmax[:, i, :].unsqueeze(2).to_broadcast([TP, H, DH]),
                                      ALU.subtract).then_inc(shifted, 1)

                g = G0 + TG * t
                compare(g)
                compare(g + 1)
                shift(0, "q", q_sb[:, t, :], q_ps, q_got)
                compare(g + 2)
                compare(g + 3)
                shift(1, "k", k_sb[:, r, :], k_ps, k_got)
                compare(g + 4)
                compare(g + 5)
                if t + 1 < NT:
                    xT_split(t + 1)
                if t + 2 < NT:
                    norm(t + 2)
                if 2 <= t < 2 + KD:
                    if t == 2:
                        dve.wait_ge(wp_hi_ok, 1)
                        dve.wait_ge(w_lo_ok, KD)
                    dve.tensor_tensor(wp_lo[:, t - 2, :], wp_raw[:, t - 2, :], wp_hi[:, t - 2, :],
                                      ALU.subtract).then_inc(wp_lo_ok, 1)
                dve.wait_ge(m_ps, t + 1)
                dve.tensor_tensor(msg[:, t, :], bank[6][0:TP, 0:MD], bias("m"), ALU.add).then_inc(m_ok, 1)
                finish_lot(LOTS0 + t)
                dve.wait_ge(exp_ok, 2 * t + 2)
                own_step(dve.reciprocal(hrec[:, :, :], hsum[:, :, :]))
                for i in range(2):
                    last = dve.tensor_tensor(heads[i], heads[i], hrec[:, i, :].unsqueeze(2).to_broadcast([TP, H, DH]),
                                             ALU.mult)
                last.then_inc(soft_ok, 1)

            dve.wait_ge(ctx_ps, NT)
            ctx_copies(dve.tensor_copy, 0).then_inc(ctx_ok, 1)

            def aoT_split(t):
                dve.wait_ge(aoT_ok, t + 1)
                dve.tensor_tensor(xT_lo[:, t % 2, :, :], bank[5 + t % 2][:, 0:KD * TP].rearrange("p (k n) -> p k n", k=KD),
                                  xT_hi[:, t % 2, :, :], ALU.subtract).then_inc(aoT_lo_ok, 1)

            def msg_split(t):
                dve.wait_ge(msg_hi_ok, t + 1)
                dve.tensor_tensor(msg_lo[:, t, :], msg[:, t, :], msg_hi[:, t, :], ALU.subtract).then_inc(msg_lo_ok, 1)

            def attend(t):
                dve.wait_ge(num_ps, t + 1)
                if t >= 2:
                    dve.wait_ge(aoT_ps, t - 1)
                for half in range(2):
                    last = dve.reciprocal(rden[:, half, :, :], num_at(t, half)[:, :, 128:130])
                own_step(last)
                for half in range(2):
                    last = dve.tensor_tensor(
                        ao[:, t % 2, half * 256:(half + 1) * 256].rearrange("p (k h d) -> p k h d", k=2, h=2),
                        num_at(t, half)[:, :, 0:128].rearrange("p k (h d) -> p k h d", h=2),
                        rden[:, half, :, :].unsqueeze(3).to_broadcast([TP, 2, 2, DH]), ALU.mult)
                last.then_inc(num_used, 1)
                dve.wait_ge(num_used, t + 1)
                dve.tensor_tensor(ao[:, t % 2, :], ao[:, t % 2, :], q_sb[:, t, :], ALU.add).then_inc(ao_ok, 1)

            def mix_add(t):
                dve.wait_ge(mix_ps, t + 1)
                dve.tensor_tensor(rec[:, t, :], rec[:, t, :], bank[t % 2][0:TP, :], ALU.add).then_inc(mix_ok, 1)

            for t in range(NT):
                attend(t)
                if t == 0:
                    dve.wait_ge(row_ps, 1)
                    dve.wait_ge(ld_bias2, 16)
                    dve.tensor_tensor(bias("p"), bias("p"), bank[6][0:TP, :], ALU.add).then_inc(row_ok, 1)
                if t >= 1:
                    aoT_split(t - 1)
                if t >= 2:
                    mix_add(t - 2)
                msg_split(t)
            aoT_split(NT - 1)

            def adj_add(t):
                rw = rows[t % 3]
                dve.wait_ge(ld_rows[t % 3], 64 * (t // 3 + 1))
                dve.scalar_tensor_tensor(rw[:, 0, :], rw[:, 0, :], 1.0, rw[:, 1, :], ALU.mult, ALU.add,
                                         accum_out=rs[:, t:t + 1]).then_inc(adj_sum, 1)
                dve.wait_ge(adj_sum, t + 1)
                dve.tensor_scalar(valid[:, t:t + 1], rs[:, t:t + 1], 0.0, None, ALU.is_gt)
                own_step(dve.tensor_scalar(rse[:, t:t + 1], rs[:, t:t + 1], 1e-6, None, ALU.add))
                dve.reciprocal(rinv[:, t:t + 1], rse[:, t:t + 1]).then_inc(rinv_ok, 1)

            def scaled_split(t):
                dve.wait_ge(scaled_hi_ok, t + 1)
                dve.scalar_tensor_tensor(scaled_lo[:, t % 2, :], msg[:, t, :], rinv[:, t:t + 1], scaled_hi[:, t % 2, :],
                                         ALU.mult, ALU.subtract).then_inc(scaled_lo_ok, 1)

            def adjT_split(t, part):
                lo, hi = (0, 4, 8)[part], (4, 8, 10)[part]
                n = 3 * t + part
                dve.wait_ge(adjT_ok, n + 1)
                dve.tensor_tensor(adjT_lo[:, t % 2, lo:hi, :],
                                  adjT_at(n)[0:TP, 0:(hi - lo) * TP].rearrange("p (j n) -> p j n", j=hi - lo),
                                  adjT_hi[:, t % 2, lo:hi, :], ALU.subtract).then_inc(adjT_lo_ok, 1)

            adj_add(0)
            mix_add(NT - 2)
            for t in range(NT):
                if t >= 1:
                    scaled_split(t)
                    if t + 1 < NT:
                        adj_add(t + 1)
                adjT_split(t, 0)
                adjT_split(t, 1)
                if t == 0:
                    mix_add(NT - 1)
                    adjT_split(t, 2)
                    scaled_split(t)
                    adj_add(1)
                if t >= 1:
                    adjT_split(t, 2)
            dve.wait_ge(out1_ps, NT)
            for m, a, b, bk, lo in ((0, 0, 500, 3, 0), (0, 1000, 1250, 7, 0), (1, 1000, 1250, 7, 250)):
                dve.tensor_copy(msgT[:, 2 + m, a:b], bank[bk][:, lo:lo + b - a]).then_inc(out1_ok, 1)

            def hid_norm(t0, t1, part):
                dve.wait_ge(hstd_ok, part)
                own_step(dve.reciprocal(rstd[:, t0:t1], std[:, t0:t1]))
                for t in range(t0, t1):
                    dve.tensor_scalar(hid[:, t, :], hid[:, t, :], mv[:, t, 0:1],
                                      rstd[:, t:t + 1], ALU.subtract, ALU.mult).then_inc(hn_ok, 1)

            for j in range(NT // 2):
                if j == 2:
                    hid_norm(0, HALF, 1)
                dve.wait_ge(hid_ps, 2 * j + 2)
                both = bank[HIDBANK[j]][0:TP, 0:2 * GH].rearrange("p (a n) -> p a n", a=2)
                dve.tensor_tensor(hid[:, 2 * j:2 * j + 2, :], both, bias("g1").unsqueeze(1).to_broadcast([TP, 2, GH]),
                                  ALU.add).then_inc(hid_got, 1)
                dve.wait_ge(hid_got, j + 1)
                for t in (2 * j, 2 * j + 1):
                    last = dve.bn_stats(stat[:, t, :], hid[:, t, :])
                own_step(last)
                for t in (2 * j, 2 * j + 1):
                    dve.bn_aggr(mv[:, t, :], stat[:, t, :]).then_inc(hvar_ok, 1)
            def upd_bias(t):
                dve.wait_ge(upd_ps, t + 1)
                if t >= 2:
                    dve.wait_ge(x1_ok, t - 1)
                dve.tensor_tensor(upd[:, t % 2, :], upd_at(t), bias("g2"), ALU.add).then_inc(upd_ok, 1)

            def x1_norm(t):
                dve.wait_ge(x1_ok, t + 1)
                own_step(dve.bn_stats(stat[:, t, :], rec[:, t, :]))
                dve.wait_ge(hn_ok, NT)
                dve.bn_aggr(mv[:, t, :], stat[:, t, :]).then_inc(var2_ok, 1)
                dve.wait_ge(var2_ok, t + 1)
                if t >= 2:
                    dve.wait_ge(x2T_ps, t - 1)
                dve.tensor_scalar(xn[:, t % 2, :], rec[:, t, :], mv[:, t, 0:1], None, ALU.subtract).then_inc(x2_ok, 1)

            for t in range(NT):
                upd_bias(t)
                if t == 0:
                    hid_norm(HALF, NT, 2)
                if t >= 2:
                    x1_norm(t - 2)
            x1_norm(NT - 2)
            x1_norm(NT - 1)

            dve.tensor_copy(count16[:, 0, :], ones[0:TP, 0:TP])
            dve.tensor_copy(count16[:, 1, :], const("before")[0:TP, :])
            dve.wait_ge(std2_ok, 1)
            own_step(dve.reciprocal(rstd[:, :], std[:, :]))
            dve.memset(factors[:, :, 3], 0.0)
            dve.tensor_copy(factors[:, :, 1], rstd[:, :])
            own_step(dve.scalar_tensor_tensor(factors[:, :, 2], mv[:, :, 0], -1.0, rstd[:, :], ALU.mult, ALU.mult))

            def over_e(a):
                return a.unsqueeze(2).to_broadcast([TP, NT, E])

            dve.wait_ge(log_ps, NT)
            own_step(dve.tensor_tensor(logit[:, :, :], bank[2][0:TP, 0:NT * E].rearrange("p (t e) -> p t e", t=NT),
                                       over_e(rstd[:, :]), ALU.mult))
            own_step(dve.tensor_tensor(logit[:, :, :], logit[:, :, :],
                                       bias("s").unsqueeze(1).to_broadcast([TP, NT, E]), ALU.add))
            own_step(dve.tensor_reduce(lmax[:, :], logit[:, :, :], X, ALU.max))
            dve.tensor_tensor(eq[:, :, :], logit[:, :, :], over_e(lmax[:, :]), ALU.is_equal)
            own_step(dve.tensor_tensor(logit[:, :, :], logit[:, :, :], over_e(lmax[:, :]), ALU.subtract))
            prefer = const("prefer")[0:TP, :].rearrange("p (t e) -> p t e", t=NT)
            dve.memset(cnt[:, 2, :], 0.0).then_inc(log_ok, 1)
            own_step(dve.tensor_tensor(eq[:, :, :], eq[:, :, :], prefer, ALU.mult))
            own_step(dve.tensor_reduce(best[:, :], eq[:, :, :], X, ALU.max))
            dve.tensor_tensor(oh16[:, :, :], prefer, over_e(best[:, :]), ALU.is_equal).then_inc(oh_ok, 1)
            dve.tensor_tensor(oh[:, :, :], prefer, over_e(best[:, :]), ALU.is_equal)
            dve.wait_ge(lexp_ok, 1)
            own_step(dve.tensor_reduce(psm[:, :], logit[:, :, :], X, ALU.add))
            dve.reciprocal(factors[:, :, 0], psm[:, :]).then_inc(fac_ok, 1)
            dve.wait_ge(rank_ps, 1)
            own_step(dve.tensor_scalar(cnt_i[:, 0, :], bank[7][0:TP, NT * E:(NT + 1) * E], float(CH - 1), None, ALU.add))
            own_step(dve.tensor_scalar(cnt_i[:, 1, :], cnt_i[:, 0, :], CH.bit_length() - 1, None,
                                       ALU.logical_shift_right))
            own_step(dve.tensor_copy(cnt[:, 0, :], cnt_i[:, 1, :]))
            own_step(dve.tensor_tensor_scan(cnt[:, 1, :], cnt[:, 0, :], cnt[:, 2, :], 0.0, ALU.add, ALU.add))
            own_step(dve.tensor_tensor(cnt[:, 3, :], cnt[:, 1, :], cnt[:, 0, :], ALU.subtract))
            own_step(dve.tensor_scalar(cnt[:, 3, :], cnt[:, 3, :], float(CH), None, ALU.mult))
            own_step(dve.tensor_tensor(eq[:, :, :], bank[7][0:TP, 0:NT * E].rearrange("p (t e) -> p t e", t=NT),
                                       cnt[:, 3:4, :].to_broadcast([TP, NT, E]), ALU.add))
            own_step(dve.tensor_tensor(eq[:, :, :], eq[:, :, :], oh[:, :, :], ALU.mult))
            own_step(dve.tensor_reduce(best[:, :], eq[:, :, :], X, ALU.add))
            own_step(dve.tensor_copy(pos_i[:, :], best[:, :]))
            dve.tensor_scalar(rc_i[:, 0, :], pos_i[:, :], CH - 1, None, ALU.bitwise_and)
            own_step(dve.tensor_scalar(rc_i[:, 1, :], pos_i[:, :], CH.bit_length() - 1, None, ALU.logical_shift_right))
            own_step(dve.tensor_copy(posf[:, :, :], rc_i[:, :, :]))
            dve.tensor_tensor(row_hot[:, :, :], const("cols")[0:TP, :].unsqueeze(1).to_broadcast([TP, NT, CH]),
                              posf[:, 0, :].unsqueeze(2).to_broadcast([TP, NT, CH]), ALU.is_equal)
            own_step(dve.tensor_tensor(chunk_hot[:, :, :], const("cols")[0:TP, 0:NC].unsqueeze(1).to_broadcast([TP, NT, NC]),
                                       posf[:, 1, :].unsqueeze(2).to_broadcast([TP, NT, NC]), ALU.is_equal))
            dve.tensor_tensor(chunk_tag[:, :, :], chunk_hot[:, :, :],
                              const("tag")[0:TP, :].unsqueeze(2).to_broadcast([TP, NT, NC]), ALU.mult).then_inc(hot_ok, 1)
            own_step(dve.tensor_tensor(own[:, :, :], cnt[0:1, 1:2, :].to_broadcast([1, NC, E]),
                                       const("chunk")[0:1, :].rearrange("p (c e) -> p c e", c=NC), ALU.is_le))
            own_step(dve.tensor_reduce(ownf[:, :], own[:, :, :], X, ALU.add))
            dve.tensor_scalar(own_i[:, :], ownf[:, :], float(E - 1), None, ALU.min).then_inc(own_ok, 1)
            dve.wait_ge(ctab_ps, 1)
            own_step(dve.tensor_scalar(idf[:, :], bank[6][:, 0:NC], -1.0, float(PADID), ALU.mult, ALU.add))
            dve.tensor_copy(out_i[:, :], idf[:, :])
            dve.tensor_scalar(get_i[:, :], idf[:, :], float(N - 1), None, ALU.min).then_inc(id_ok, 1)

            def h_copy(c):
                dve.wait_ge(h_ps, c + 1)
                if c >= 2:
                    dve.wait_ge(hc_ps, c - 1)
                dve.tensor_copy(h_sb[:, c % 2, :], bank[1][:, 0:F]).then_inc(h_ok, 1)

            def finish(c):
                e = dve.value_load(own_i[0:1, c:c + 1], min_val=0, max_val=E - 1)
                dve.wait_ge(y_ps, c + 1)
                dve.tensor_tensor(y_sb[:, c % 2, :], bank[3 + c % 2][:, :], b2_sb[:, bass.ds(e * D, D)],
                                  ALU.add).then_inc(y_ok, 1)
                dve.wait_ge(y_ok, c + 1)
                if c >= 2:
                    dve.wait_ge(out_st[c % 2], 16 * (c // 2))
                dve.scalar_tensor_tensor(o_sb[:, c % 2, :], y_sb[:, c % 2, :],
                                         rec_c[:, c % RING, R_P:R_P + 1], rec_c[:, c % RING, 0:D], ALU.mult, ALU.add).then_inc(o_ok, 1)

            def hT_split(c):
                dve.wait_ge(hT_hi_ok, c + 1)
                dve.tensor_tensor(hT_lo[:, c % 2, :, :], hT[:, c % 2, :, :], hT_hi[:, c % 2, :, :],
                                  ALU.subtract).then_inc(hT_lo_ok, 1)

            for i in range(1, 4):
                dve.wait_ge(w2_hi_ok, i + 1)
                dve.tensor_tensor(piece(w2_lo, i), piece(w2_raw, i), piece(w2_hi, i),
                                  ALU.subtract).then_inc(w2_lo_ok, 1)
            dve.wait_ge(own_ok, 1)
            dve.wait_ge(ld_b2, 16)
            h_copy(0)
            for c in range(NC):
                hT_split(c)
                if c + 1 < NC:
                    h_copy(c + 1)
                dve.wait_ge(ld_rec[c % RING], 16 * (c // RING + 1))
                finish(c)

        @block.scalar
        def _(act):
            act.wait_ge(ld_edge, 96)
            act.wait_ge(top_sb, 1)
            act.activation(wexp[:, :], wraw[:, :], ACT.Exp, bias=top[:, 3:4]).then_inc(w_exp, 1)
            for k in range(KD):
                act.wait_ge(ld_wk[k], 16)
                act.activation(w_hi[:, k, :], w_raw[:, k, :], ACT.Copy).then_inc(w_hi_ok, 1)
            act.wait_ge(var_ok, NT)
            act.activation(std[:, :], mv[:, :, 1], ACT.Sqrt, bias=const("eps")[0:TP, :]).then_inc(std_ok, 1)

            def x_copy(t):
                act.wait_ge(xT_ps, t + 1)
                if t >= 2:
                    act.wait_ge(m_ps, t - 1)
                act.activation(xT_hi[:, t % 2, :, :],
                               bank[0][:, 0:KD * TP].rearrange("p (k n) -> p k n", k=KD), ACT.Copy).then_inc(xT_ok, 1)

            def q_copy(t):
                act.wait_ge(qT_ps, t + 1)
                if t == 0:
                    act.wait_ge(w_lo_ok, KD)
                act.activation(qT[:, :, t * TP:(t + 1) * TP],
                               bank[0][:, 0:KD * TP].rearrange("p (k n) -> p k n", k=KD), ACT.Copy).then_inc(qT_ok, 1)

            x_copy(0)
            for t in range(NT):
                if t + 1 < NT:
                    x_copy(t + 1)
                for i, a in enumerate((q_sb[:, t, :], k_sb[:, t % 2, :])):
                    act.wait_ge(shifted, 2 * t + i + 1)
                    for h in range(H):
                        ah = a[:, h * DH:(h + 1) * DH]
                        last = act.activation(ah, ah, ACT.Exp, accum_out=hsum[:, i, h:h + 1])
                    last.then_inc(exp_ok, 1)
                if t == 1:
                    act.wait_ge(ld_wp, 32)
                    for z in zero1:
                        act.wait_ge(z, 16)
                    act.activation(wp_hi[:, :, :], wp_raw[:, :, :], ACT.Copy).then_inc(wp_hi_ok, 1)
                act.wait_ge(v_ps, t + 1)
                if t >= 2:
                    act.wait_ge(ctx_ps, t - 1)
                act.activation(v_sb[:, t % 2, :, 0:128], bank[5][0:TP, :].rearrange("p (k n) -> p k n", k=KD),
                               ACT.Copy).then_inc(v_ok, 1)
                if t >= 1:
                    q_copy(t - 1)
            q_copy(NT - 1)
            act.wait_ge(ctx_ps, NT)
            act.wait_ge(ctxd_zero, 1)
            ctx_copies(lambda dst, src: act.activation(dst, src, ACT.Copy), 1).then_inc(ctx_ok1, 1)
            act.wait_ge(m_ps, NT)
            act.wait_ge(m_ok, NT)
            for t in range(NT):
                act.activation(msg_hi[:, t, :], msg[:, t, :], ACT.Copy).then_inc(msg_hi_ok, 1)
                act.wait_ge(aoT_ps, t + 1)
                if t >= 2:
                    act.wait_ge(mix_ps, t - 1)
                act.activation(xT_hi[:, t % 2, :, :],
                               bank[5 + t % 2][:, 0:KD * TP].rearrange("p (k n) -> p k n", k=KD),
                               ACT.Copy).then_inc(aoT_ok, 1)

            def adj_high(t):
                act.wait_ge(adj_sum, t + 1)
                if t == 0:
                    act.wait_ge(mix_ps, NT)
                if t >= 2:
                    act.wait_ge(out1_ps, t - 1)
                act.activation(adj_hi[:, t % 2, :], rows[t % 3][:, 0, :], ACT.Copy).then_inc(adj_ok, 1)
                act.wait_ge(rinv_ok, t + 1)
                act.activation(scaled_hi[:, t % 2, :], msg[:, t, :], ACT.Copy,
                               scale=rinv[:, t:t + 1]).then_inc(scaled_hi_ok, 1)

            def adjT_high(t, part):
                lo, hi = (0, 4, 8)[part], (4, 8, 10)[part]
                n = 3 * t + part
                act.wait_ge(adjT_ps, n + 1)
                if t == 0 and part == 0:
                    act.wait_ge(num_ps, NT)
                if t >= 2 and part == 0:
                    act.wait_ge(out0_ps, t - 1)
                act.activation(adjT_hi[:, t % 2, lo:hi, :],
                               adjT_at(n)[0:TP, 0:(hi - lo) * TP].rearrange("p (j n) -> p j n", j=hi - lo),
                               ACT.Copy).then_inc(adjT_ok, 1)

            def out0_scale(t):
                act.wait_ge(out0_ps, t + 1)
                if t >= 1:
                    act.wait_ge(out0T_ps, t)
                act.activation(out0[:, :], bank[2][0:TP, 0:MD], ACT.Copy, scale=rinv[:, t:t + 1]).then_inc(out0_sb, 1)

            def out0_copy(t):
                act.wait_ge(out0T_ps, t + 1)
                act.activation(msgT[:, 0:2, t * TP:(t + 1) * TP],
                               bank[2][:, MD:MD + 2 * TP].rearrange("p (m n) -> p m n", m=2),
                               ACT.Copy).then_inc(out0_ok, 1)

            for t in range(NT):
                if 1 <= t < NT - 1:
                    adj_high(t + 1)
                adjT_high(t, 0)
                if t >= 1:
                    out0_scale(t - 1)
                adjT_high(t, 1)
                adjT_high(t, 2)
                if t == 0:
                    adj_high(0)
                if t >= 1:
                    out0_copy(t - 1)
                if t == 0:
                    adj_high(1)
            act.wait_ge(out1_ps, NT)
            for m, a, b, bk in ((1, 0, 500, 5), (1, 500, 1000, 6), (0, 500, 1000, 4)):
                act.activation(msgT[:, 2 + m, a:b], bank[bk][:, 0:500], ACT.Copy).then_inc(out1_ok, 1)
            out0_scale(NT - 1)
            out0_copy(NT - 1)

            def hid_std(t0, t1):
                act.wait_ge(hvar_ok, t1)
                act.activation(std[:, t0:t1], mv[:, t0:t1, 1], ACT.Sqrt, bias=const("eps")[0:TP, :]).then_inc(hstd_ok, 1)

            def hid_copy(t):
                act.wait_ge(hT_ps, t + 1)
                if t >= 2:
                    act.wait_ge(upd_ps, t - 1)
                act.activation(hidT[:, t % 2, :], bank[3][:, 0:TP], ACT.Relu, bias=little("beta"),
                               scale=little("gamma")).then_inc(hidT_ok, 1)

            def relu(t):
                act.wait_ge(upd_ok, t + 1)
                act.activation(upd[:, t % 2, :], upd[:, t % 2, :], ACT.Relu, scale=valid[:, t:t + 1]).then_inc(relu_ok, 1)

            def x2_copy(t):
                act.wait_ge(x2T_ps, t + 1)
                act.activation(x2T[:, :, t * TP:(t + 1) * TP],
                               bank[t % 2][:, 0:KD * TP].rearrange("p (k n) -> p k n", k=KD), ACT.Copy).then_inc(x2T_ok, 1)

            def w2_high(i):
                act.wait_ge(ld_w2k[i], 16)
                act.activation(piece(w2_hi, i), piece(w2_raw, i), ACT.Copy).then_inc(w2_hi_ok, 1)

            hid_std(0, HALF)
            hid_copy(0)
            def log_copy(t):
                act.wait_ge(logT_ps, t + 1)
                act.activation(logT[:, t * TP:(t + 1) * TP], logT_at(t), ACT.Copy).then_inc(logT_ok, 1)

            for i in range(NT + 4):
                if i + 1 < NT:
                    hid_copy(i + 1)
                if i == 0:
                    hid_std(HALF, NT)
                if i < NT:
                    relu(i)
                if 3 <= i < NT + 3:
                    x2_copy(i - 3)
                if i >= 4:
                    log_copy(i - 4)
            act.wait_ge(var2_ok, NT)
            act.activation(std[:, :], mv[:, :, 1], ACT.Sqrt, bias=const("eps")[0:TP, :]).then_inc(std2_ok, 1)
            w2_high(0)
            act.wait_ge(log_ok, 1)
            act.activation(logit[:, :, :], logit[:, :, :], ACT.Exp).then_inc(lexp_ok, 1)

            def xs_norm(c):
                act.wait_ge(ld_rec[c % RING], 16 * (c // RING + 1))
                if c >= 2:
                    act.wait_ge(xsT_ps, c - 1)
                act.activation(xs[:, c % 2, :], rec_c[:, c % RING, 0:D], ACT.Identity, bias=rec_c[:, c % RING, R_NM:R_NM + 1],
                               scale=rec_c[:, c % RING, R_RS:R_RS + 1]).then_inc(xs_ok, 1)

            def xs_copy(c):
                act.wait_ge(xsT_ps, c + 1)
                if c >= 2:
                    act.wait_ge(h_ps, c - 1)
                act.activation(xsT[:, c % 2, :, :], bank[7 * (c % 2)][:, :].rearrange("p (k n) -> p k n", k=KD),
                               ACT.Copy).then_inc(xsT_ok, 1)

            def gelu(c):
                e = act.value_load(own_i[0:1, c:c + 1], min_val=0, max_val=E - 1)
                act.wait_ge(hc_ps, c + 1)
                if c >= 2:
                    act.wait_ge(y_ps, c - 1)
                for f in range(KF):
                    b1 = little("b1").rearrange("p (f e) -> p f e", f=KF)
                    act.activation(hT[:, c % 2, f, :], bank[2][:, f * CH:(f + 1) * CH], ACT.Gelu,
                                   bias=b1[:, f, bass.ds(e, 1)]).then_inc(gelu_ok, 1)
                act.wait_ge(gelu_ok, 2 * c + 2)
                act.activation(hT_hi[:, c % 2, :, :], hT[:, c % 2, :, :], ACT.Copy).then_inc(hT_hi_ok, 1)

            for i in range(1, 4):
                w2_high(i)
            act.activation(std[:, 0:1], const("eps")[0:TP, :], ACT.Gelu)
            act.wait_ge(own_ok, 1)
            xs_norm(0)
            xs_norm(1)
            xs_copy(0)
            xs_norm(2)
            xs_copy(1)
            for c in range(NC):
                gelu(c)
                if c + 2 < NC:
                    xs_copy(c + 2)
                if c + 3 < NC:
                    xs_norm(c + 3)


def constants():
    c = np.zeros((128, CW), np.float32)
    p = np.arange(128)

    def put(name, v):
        a, w = CONSTS[name]
        c[:, a:a + w] = v

    put("ident", np.eye(128))
    put("ones", 1.0)
    put("before", p[:, None] < np.arange(TP)[None, :])
    place = np.arange(GC)[None, :] * TP + np.minimum(p, TP - 1)[:, None]
    rank = np.where(p[:, None] < TP, 2.0 ** (126.0 - place), 0.0)
    put("rank", rank)
    put("limit", 2.5 * rank)
    put("spare", SPARE + place)
    put("tag", PADID - (np.arange(NT)[None, :] * TP + p[:, None]))
    put("prefer", np.tile(E - np.arange(E), NT)[None, :])
    put("chunk", np.repeat(np.arange(NC), E)[None, :])
    put("cols", np.arange(CH)[None, :])
    put("eps", LN_EPS)
    return c


def kernel(x, src, dst, edge_weight, L0_gnn_Wm, L0_gnn_bm, L0_gnn_W1, L0_gnn_b1, L0_gnn_gamma, L0_gnn_beta,
           L0_gnn_W2, L0_gnn_b2, L0_mix_Wq, L0_mix_bq, L0_mix_Wk, L0_mix_bk, L0_mix_Wv, L0_mix_bv, L0_mix_Wp,
           L0_mix_bp, L0_ffn_Ws, L0_ffn_bs, L0_ffn_W1, L0_ffn_b1, L0_ffn_W2, L0_ffn_b2):
    import concourse.bacc as bacc
    from concourse.bass_utils import run_bass_kernel_spmd

    def arr(a):
        return np.asarray(a)

    def rows_first(w):
        return arr(w).reshape(-1, 128, w.shape[-1]).transpose(1, 0, 2)

    wqkvm = np.concatenate([rows_first(arr(w).T) for w in (L0_mix_Wq, L0_mix_Wk, L0_mix_Wv)]
                           + [rows_first(L0_gnn_Wm)], axis=2)
    biases = np.concatenate([arr(b) for b in (L0_mix_bq, L0_mix_bk, L0_gnn_bm, L0_mix_bp, L0_gnn_b1,
                                              L0_gnn_b2, L0_ffn_bs)])
    small = np.concatenate([
        arr(L0_gnn_gamma)[:, None], arr(L0_gnn_beta)[:, None],
        arr(L0_ffn_b1).reshape(E, KF, 128).transpose(2, 1, 0).reshape(128, -1),
        rows_first(L0_ffn_Ws).reshape(128, -1), rows_first(L0_gnn_W1).reshape(128, -1), arr(L0_gnn_W2)], axis=1)
    arrays = {
        "x": arr(x), "edge_src": arr(src), "edge_dst": arr(dst), "edge_w": arr(edge_weight),
        "consts": constants(), "biases": biases, "small": small, "wqkvm": wqkvm,
        "wp": rows_first(arr(L0_mix_Wp).T), "bvt": arr(L0_mix_bv).reshape(KD, 128).T,
        "w1f": arr(L0_ffn_W1).reshape(E, KD, 128, F).transpose(2, 1, 0, 3).reshape(128, KD, E * F),
        "w2f": arr(L0_ffn_W2).reshape(E, KF, 128, D).transpose(2, 1, 0, 3).reshape(128, KF, E * D),
        "b2f": arr(L0_ffn_b2).reshape(-1),
    }
    arrays = {k: np.ascontiguousarray(v) for k, v in arrays.items()}
    nc = bacc.Bacc("TRN2", target_bir_lowering=False, num_devices=1)
    args = {k: nc.dram_tensor(f"in_{k}", v.shape, mybir.dt.from_np(v.dtype), kind="ExternalInput").ap()
            for k, v in arrays.items()}
    out = nc.dram_tensor("out", (N, D), F32, kind="ExternalOutput").ap()
    build(nc, out=out, **args)
    r = run_bass_kernel_spmd(nc, [{f"in_{k}": v for k, v in arrays.items()}], core_ids=[0])
    return r.results[0]["out"]
```
